# Optimizing a Trainium2 kernel written in Bass

```python
import numpy as np
import jax
import jax.numpy as jnp

def _softmax(x, axis=-1):
    return jax.nn.softmax(x, axis=axis)

def _gelu(x):
    return jax.nn.gelu(x, approximate=True)

def _silu(x):
    return jax.nn.silu(x)

def _sigmoid(x):
    return jax.nn.sigmoid(x)

def _layernorm(x, axis=-1, eps=1e-05):
    m = jnp.mean(x, axis=axis, keepdims=True)
    v = jnp.var(x, axis=axis, keepdims=True)
    return (x - m) / jnp.sqrt(v + eps)

def _scatter_add(tgt, idx, src, axis=0):
    return tgt.at[idx].add(src)

def _segment_sum(src, seg, n):
    return jax.ops.segment_sum(src, seg, n)
kernel_name = 'mk_vit_tower_d1_tok_img768_r4_6ebbcb'

def setup_inputs(seed: int=0):
    np.random.seed(seed)
    _w = jnp.asarray

    def _rec_inputs():
        import jax
        import jax.numpy as jnp
        _rk = jax.random.key(seed)
        x = -0.00016672 + 0.999947 * jax.random.normal(jax.random.fold_in(_rk, 1), (32, 3, 96, 96), jnp.float32)
        return x
    x = _rec_inputs()

    def _L0_tok_setup():
        import jax, jax.numpy as jnp
        import numpy as np
        PATCH = 16

        def _patchify(x, p):
            B, C, H, W = x.shape
            Hp, Wp = (H // p, W // p)
            xu = x.reshape(B, C, Hp, p, Wp, p).transpose(0, 1, 2, 4, 3, 5)
            num_patches = Hp * Wp
            return xu.reshape(B, num_patches, -1)
        key = jax.random.key(seed)
        k1, k2, k3 = jax.random.split(key, 3)
        B, C, H = (64, 3, 96)
        hidden = 192
        d = C * PATCH * PATCH
        x = jax.random.normal(k1, (B, C, H, H), dtype=jnp.float32)
        W = jax.random.normal(k2, (hidden, d), dtype=jnp.float32) * 0.02
        b = jax.random.normal(k3, (hidden,), dtype=jnp.float32) * 0.02
        return {'x': x, 'W': W, 'b': b}
    _L0_tok_all = _L0_tok_setup()
    _L0_tok_in = {k: v for k, v in _L0_tok_all.items() if k in ('W', 'b')}
    del _L0_tok_all

    def _L0_attn_setup():
        import jax, jax.numpy as jnp
        import numpy as np
        D_MODEL = 192
        D_INNER = 384
        D_STATE = 16
        DT_RANK = 96
        H_FFN = 512
        B, L = (1, 512)
        EPS = 1e-06

        def rmsnorm(x, w):
            return x * jax.lax.rsqrt(jnp.mean(x * x, axis=-1, keepdims=True) + EPS) * w

        def selective_scan(z, W_xproj, W_dt, b_dt, A_log, D_skip):
            xdbl = jnp.einsum('bld,kd->blk', z, W_xproj)
            dt_in, Bm, Cm = jnp.split(xdbl, [DT_RANK, DT_RANK + D_STATE], axis=-1)
            dt = jax.nn.softplus(jnp.einsum('blr,dr->bld', dt_in, W_dt) + b_dt)
            A = -jnp.exp(A_log)
            A_bar = jnp.exp(dt[..., None] * A)
            Bx = (dt * z)[..., None] * Bm[:, :, None, :]

            def comb(e1, e2):
                a1, b1 = e1
                a2, b2 = e2
                return (a1 * a2, a2 * b1 + b2)
            _, h = jax.lax.associative_scan(comb, (A_bar, Bx), axis=1)
            y = jnp.einsum('blds,bls->bld', h, Cm) + D_skip * z
            return y
        key = jax.random.key(seed)
        ks = jax.random.split(key, 10)
        s = lambda k, shape, scale=0.02: jax.random.normal(k, shape, dtype=jnp.float32) * scale
        return {'x': jax.random.normal(ks[0], (B, L, D_MODEL), dtype=jnp.float32), 'w_norm1': jnp.ones((D_MODEL,), jnp.float32), 'W_in': s(ks[1], (D_INNER, D_MODEL)), 'W_gate': s(ks[2], (D_INNER, D_MODEL)), 'W_xproj': s(ks[3], (DT_RANK + 2 * D_STATE, D_INNER)), 'W_dt': s(ks[4], (D_INNER, DT_RANK)), 'b_dt': jnp.full((D_INNER,), -4.6, jnp.float32), 'A_log': jnp.log(jnp.tile(jnp.arange(1, D_STATE + 1, dtype=jnp.float32), (D_INNER, 1))), 'D_skip': jnp.ones((D_INNER,), jnp.float32), 'W_out': s(ks[5], (D_MODEL, D_INNER)), 'w_ffn_norm': jnp.ones((D_MODEL,), jnp.float32), 'W_up': s(ks[6], (H_FFN, D_MODEL)), 'W_gate_ffn': s(ks[7], (H_FFN, D_MODEL)), 'W_down': s(ks[8], (D_MODEL, H_FFN))}
    _L0_attn_all = _L0_attn_setup()
    _L0_attn_in = {k: v for k, v in _L0_attn_all.items() if k in ('w_norm1', 'W_in', 'W_gate', 'W_xproj', 'W_dt', 'b_dt', 'A_log', 'D_skip', 'W_out', 'w_ffn_norm', 'W_up', 'W_gate_ffn', 'W_down')}
    del _L0_attn_all

    def _L0_ffn_setup():
        import jax, jax.numpy as jnp
        import numpy as np
        B, S, H = (2, 256, 192)
        E, K, I = (16, 4, 192)
        ALPHA, LIMIT, EPS = (1.702, 7.0, 1e-05)

        def _swiglu(h):
            x_glu, x_lin = jnp.split(h, 2, axis=-1)
            x_glu = jnp.minimum(x_glu, LIMIT)
            x_lin = jnp.clip(x_lin, -LIMIT, LIMIT)
            return x_glu * jax.nn.sigmoid(ALPHA * x_glu) * (x_lin + 1.0)
        key = jax.random.key(seed)
        ks = jax.random.split(key, 7)
        x = jax.random.normal(ks[0], (B, S, H), dtype=jnp.float32)
        scale = jnp.ones((H,), jnp.float32)
        gate_w = jax.random.normal(ks[1], (E, H), jnp.float32) * 0.02
        gate_b = jnp.zeros((E,), jnp.float32)
        w1 = jax.random.normal(ks[2], (E, H, 2 * I), jnp.float32) * 0.02
        b1 = jax.random.normal(ks[3], (E, 2 * I), jnp.float32) * 0.02
        w2 = jax.random.normal(ks[4], (E, I, H), jnp.float32) * 0.02
        b2 = jax.random.normal(ks[5], (E, H), jnp.float32) * 0.02
        return {'x': x, 'scale': scale, 'gate_w': gate_w, 'gate_b': gate_b, 'w1': w1, 'b1': b1, 'w2': w2, 'b2': b2}
    _L0_ffn_all = _L0_ffn_setup()
    _L0_ffn_in = {k: v for k, v in _L0_ffn_all.items() if k in ('scale', 'gate_w', 'gate_b', 'w1', 'b1', 'w2', 'b2')}
    del _L0_ffn_all
    return {'x': x, 'L0_tok_W': _L0_tok_in['W'], 'L0_tok_b': _L0_tok_in['b'], 'L0_attn_w_norm1': _L0_attn_in['w_norm1'], 'L0_attn_W_in': _L0_attn_in['W_in'], 'L0_attn_W_gate': _L0_attn_in['W_gate'], 'L0_attn_W_xproj': _L0_attn_in['W_xproj'], 'L0_attn_W_dt': _L0_attn_in['W_dt'], 'L0_attn_b_dt': _L0_attn_in['b_dt'], 'L0_attn_A_log': _L0_attn_in['A_log'], 'L0_attn_D_skip': _L0_attn_in['D_skip'], 'L0_attn_W_out': _L0_attn_in['W_out'], 'L0_attn_w_ffn_norm': _L0_attn_in['w_ffn_norm'], 'L0_attn_W_up': _L0_attn_in['W_up'], 'L0_attn_W_gate_ffn': _L0_attn_in['W_gate_ffn'], 'L0_attn_W_down': _L0_attn_in['W_down'], 'L0_ffn_scale': _L0_ffn_in['scale'], 'L0_ffn_gate_w': _L0_ffn_in['gate_w'], 'L0_ffn_gate_b': _L0_ffn_in['gate_b'], 'L0_ffn_w1': _L0_ffn_in['w1'], 'L0_ffn_b1': _L0_ffn_in['b1'], 'L0_ffn_w2': _L0_ffn_in['w2'], 'L0_ffn_b2': _L0_ffn_in['b2']}

def reference(x, L0_tok_W, L0_tok_b, L0_attn_w_norm1, L0_attn_W_in, L0_attn_W_gate, L0_attn_W_xproj, L0_attn_W_dt, L0_attn_b_dt, L0_attn_A_log, L0_attn_D_skip, L0_attn_W_out, L0_attn_w_ffn_norm, L0_attn_W_up, L0_attn_W_gate_ffn, L0_attn_W_down, L0_ffn_scale, L0_ffn_gate_w, L0_ffn_gate_b, L0_ffn_w1, L0_ffn_b1, L0_ffn_w2, L0_ffn_b2):
    import jax
    import jax.numpy as jnp

    def _L0_tok_ref(x, W, b):
        import jax, jax.numpy as jnp
        import numpy as np
        PATCH = 16

        def _patchify(x, p):
            B, C, H, W = x.shape
            Hp, Wp = (H // p, W // p)
            xu = x.reshape(B, C, Hp, p, Wp, p).transpose(0, 1, 2, 4, 3, 5)
            num_patches = Hp * Wp
            return xu.reshape(B, num_patches, -1)
        patches = _patchify(x, PATCH)
        return jnp.einsum('bnd,hd->bnh', patches, W) + b

    def _L0_attn_ref(x, w_norm1, W_in, W_gate, W_xproj, W_dt, b_dt, A_log, D_skip, W_out, w_ffn_norm, W_up, W_gate_ffn, W_down):
        import jax, jax.numpy as jnp
        import numpy as np
        D_MODEL = 192
        D_INNER = 384
        D_STATE = 16
        DT_RANK = 96
        H_FFN = 512
        B, L = (1, 512)
        EPS = 1e-06

        def rmsnorm(x, w):
            return x * jax.lax.rsqrt(jnp.mean(x * x, axis=-1, keepdims=True) + EPS) * w

        def selective_scan(z, W_xproj, W_dt, b_dt, A_log, D_skip):
            xdbl = jnp.einsum('bld,kd->blk', z, W_xproj)
            dt_in, Bm, Cm = jnp.split(xdbl, [DT_RANK, DT_RANK + D_STATE], axis=-1)
            dt = jax.nn.softplus(jnp.einsum('blr,dr->bld', dt_in, W_dt) + b_dt)
            A = -jnp.exp(A_log)
            A_bar = jnp.exp(dt[..., None] * A)
            Bx = (dt * z)[..., None] * Bm[:, :, None, :]

            def comb(e1, e2):
                a1, b1 = e1
                a2, b2 = e2
                return (a1 * a2, a2 * b1 + b2)
            _, h = jax.lax.associative_scan(comb, (A_bar, Bx), axis=1)
            y = jnp.einsum('blds,bls->bld', h, Cm) + D_skip * z
            return y
        residual = x
        h = rmsnorm(x, w_norm1)
        z = h @ W_in.T
        z = z * jax.nn.sigmoid(h @ W_gate.T)
        y = selective_scan(z, W_xproj, W_dt, b_dt, A_log, D_skip)
        x = residual + y @ W_out.T
        hf = rmsnorm(x, w_ffn_norm)
        ffn = jax.nn.silu(hf @ W_gate_ffn.T) * (hf @ W_up.T) @ W_down.T
        return x + ffn

    def _L0_ffn_ref(x, scale, gate_w, gate_b, w1, b1, w2, b2):
        import jax, jax.numpy as jnp
        import numpy as np
        B, S, H = (2, 256, 192)
        E, K, I = (16, 4, 192)
        ALPHA, LIMIT, EPS = (1.702, 7.0, 1e-05)

        def _swiglu(h):
            x_glu, x_lin = jnp.split(h, 2, axis=-1)
            x_glu = jnp.minimum(x_glu, LIMIT)
            x_lin = jnp.clip(x_lin, -LIMIT, LIMIT)
            return x_glu * jax.nn.sigmoid(ALPHA * x_glu) * (x_lin + 1.0)
        Bx, Sx, Hx = x.shape
        xf = x.astype(jnp.float32)
        t = xf * jax.lax.rsqrt(jnp.mean(xf * xf, axis=-1, keepdims=True) + EPS) * scale
        t = t.reshape(-1, Hx)
        T = t.shape[0]
        g = t @ gate_w.T + gate_b
        vals, idx = jax.lax.top_k(g, K)
        w = jax.nn.softmax(vals, axis=-1) / K
        full_w = jnp.zeros((T, E), jnp.float32).at[jnp.arange(T)[:, None], idx].set(w)
        h = jnp.einsum('th,ehf->tef', t, w1) + b1
        h = _swiglu(h)
        y = jnp.einsum('tei,eih->teh', h, w2) + b2
        out = jnp.einsum('teh,te->th', y, full_w) * K
        return x + out.astype(x.dtype).reshape(Bx, Sx, Hx)
    h = _L0_tok_ref(x, L0_tok_W, L0_tok_b)
    h = h + _L0_attn_ref(_layernorm(h, axis=-1), L0_attn_w_norm1, L0_attn_W_in, L0_attn_W_gate, L0_attn_W_xproj, L0_attn_W_dt, L0_attn_b_dt, L0_attn_A_log, L0_attn_D_skip, L0_attn_W_out, L0_attn_w_ffn_norm, L0_attn_W_up, L0_attn_W_gate_ffn, L0_attn_W_down)
    h = h + _L0_ffn_ref(_layernorm(h, axis=-1), L0_ffn_scale, L0_ffn_gate_w, L0_ffn_gate_b, L0_ffn_w1, L0_ffn_b1, L0_ffn_w2, L0_ffn_b2)
    return h

_drawn_inputs = setup_inputs


def setup_inputs(seed=0):
    import zlib

    import numpy as np

    out = dict(_drawn_inputs(seed))
    spreads = {'L0_attn_w_norm1': (1.0, 0.6),
     'L0_attn_b_dt': (-4.599999904632568, 0.6),
     'L0_attn_D_skip': (1.0, 0.6),
     'L0_attn_w_ffn_norm': (1.0, 0.6),
     'L0_ffn_scale': (1.0, 0.6),
     'L0_ffn_gate_b': (0.0, 0.8)}
    factors = {'L0_attn_W_gate': 8.0,
     'L0_attn_W_xproj': 8.0,
     'L0_attn_W_dt': 8.0,
     'L0_attn_A_log': 8.0,
     'L0_attn_W_up': 4.562,
     'L0_attn_W_gate_ffn': 4.59,
     'L0_attn_W_down': 4.552,
     'L0_ffn_gate_w': 7.039,
     'L0_ffn_w1': 6.586,
     'L0_ffn_b1': 8.0,
     'L0_ffn_w2': 6.434,
     'L0_ffn_b2': 35.705}
    for name, (base, spread) in spreads.items():
        noise = np.random.default_rng([zlib.crc32(name.encode()), seed]).standard_normal(out[name].shape)
        drawn = base * np.exp(spread * noise) if base else spread * noise
        out[name] = jnp.asarray(drawn.astype(out[name].dtype))
    for name, factor in factors.items():
        out[name] = (out[name] * factor).astype(out[name].dtype)
    return out
```

```python
from contextlib import ExitStack

import numpy as np

import concourse.bass as bass
import concourse.mybir as mybir

F32 = mybir.dt.float32
F32R = mybir.dt.float32r
I32 = mybir.dt.int32
BF16 = mybir.dt.bfloat16
ALU = mybir.AluOpType
ACT = mybir.ActivationFunctionType
AX = mybir.AxisListType

P = 128
IMAGES, TOKENS_PER_IMAGE = 32, 36
CHUNK_IMAGES = 8
CHUNKS = IMAGES // CHUNK_IMAGES
T = CHUNK_IMAGES * TOKENS_PER_IMAGE
PATCH_DIM, HIDDEN, INNER, STATES, DT_RANK, FFN_DIM = 768, 192, 384, 16, 96, 512
REST = HIDDEN - P
EXPERTS, TOP_K, EXPERT_DIM = 16, 4, 192
KP = PATCH_DIM // P
NJ = INNER // P
NF = FFN_DIM // P
D8 = P // STATES
GROUPS_PER_BLOCK = P // D8
PAIRS = EXPERTS // 2
UNITS = 3 * PAIRS
PAIR_COLS = 6 * P
SCAN_STEPS = NJ * GROUPS_PER_BLOCK // 2
RT = T // 3
LIMIT, ALPHA = 7.0, 1.702
PAD_LOGIT = -3.0e38

LOG1P = (0.999999971, -0.499995015, 0.333192713, -0.248443699, 0.191114311, -0.136747697,
         0.078361668, -0.0295885074, 0.0052534578)
ROOT_GUESS = float(0x5F3759DF)
ROOT_STEPS = 13


class Signal:

    def __init__(self, semaphore, per_chunk, unit=1):
        self.sem, self.per_chunk, self.unit = semaphore, per_chunk, unit

    def at(self, chunk, k):
        return (chunk * self.per_chunk + k) * self.unit


def after_first(chunk):
    return not isinstance(chunk, int)


def schedule():
    pre = [("embed", 0), ("center", 0), ("variance", 0), ("scale", 0)]
    pre += [("inproj", j) for j in range(NJ)]
    pre += [("xproj", 0), ("delta", 0), ("broadcast", 0), ("log1p", 0), ("stack", 0)]
    post = [("outproj", 0), ("variance2", 0), ("scale2", 0)] + [("ffn", k) for k in range(NF)]
    post += [("down", 0), ("center3", 0), ("variance3", 0), ("scale3", 0), ("topk", 0), ("weights", 0)]

    pieces = [[("start", 0)]]
    for u in range(UNITS):
        pieces.append([("gate", u)] + ([("scale", u - 1)] if u else []))
        pieces.append([("linear", u), ("mix", u)] + ([("down", u - 2)] if u % 2 and u > 2 else []))
    pieces.append([("scale", UNITS - 1)])
    pieces.append([("down", UNITS - 1), ("finish", 0)])
    steps = []
    for n, s in enumerate(pre):
        steps.append((s, PIECES_BEFORE_PRE.get(n, 0)))
    for i in range(SCAN_STEPS):
        steps.append((("scan", i), 0))
        steps.append((("scan_second", i), 1))
        steps.append((("advance", i), 1 if i in PIECES_BEFORE_ADVANCE else 0))
        if i:
            steps.append((("collect", i - 1), 0))
    steps.append((("collect", SCAN_STEPS - 1), 1))
    for n, s in enumerate(post):
        steps.append((s, PIECES_BEFORE_POST.get(n, 0)))
    out = []
    for n, (s, count) in enumerate(steps):
        if s == ("scale3", 0):
            count = len(pieces)
        for _ in range(min(count, len(pieces))):
            out += [("B",) + p for p in pieces.pop(0)]
        out.append(("A",) + s)
    return out


PIECES_BEFORE_PRE = {1: 2, 2: 1, 3: 1, 4: 1, 7: 1, 8: 1, 9: 2, 10: 2, 11: 2}
PIECES_BEFORE_ADVANCE = ()
PIECES_BEFORE_POST = {0: 1, 1: 1, 2: 2, 3: 1, 7: 1, 8: 2, 9: 2, 10: 2}


def vit_tower(nc, patches, embed_w, in_w, in_w_rest, xproj_w, dt_w, out_w, ffn_w, ffn_w_rest,
              ffn_down, router_w, router_w_rest, router_b, expert_w1, expert_w2, expert_b2,
              vectors, decay_log, unit_pick, group_pick, state_pick, channel_sum, ones_mean,
              identity, out_main, out_rest):
    ORDER = schedule()
    with ExitStack() as ctx:
        def sb(name, shape, dt=F32):
            return ctx.enter_context(nc.sbuf_tensor(name, shape, dt))

        def signal(name, per_chunk, unit=1):
            return Signal(ctx.enter_context(nc.semaphore(name)), per_chunk, unit)

        w_embed = sb("w_embed", [P, KP, 2 * P])
        w_in = sb("w_in", [P, 2, INNER])
        w_in_rest = sb("w_in_rest", [REST, 2, INNER])
        w_xproj = sb("w_xproj", [P, NJ, P])
        w_dt = sb("w_dt", [DT_RANK, INNER])
        w_out = sb("w_out", [P, NJ, 2 * P])
        w_ffn = sb("w_ffn", [P, 2, FFN_DIM])
        w_ffn_rest = sb("w_ffn_rest", [REST, 2, FFN_DIM])
        w_down = sb("w_down", [P, NF, 2 * P])
        w_router = sb("w_router", [P, EXPERTS])
        w_router_rest = sb("w_router_rest", [REST, EXPERTS])
        b_router = sb("b_router", [1, EXPERTS])
        w2 = sb("w2", [P, UNITS, HIDDEN])
        b2 = sb("b2", [EXPERTS, HIDDEN])
        vec = sb("vec", [P, vectors.shape[1]])
        decay = sb("decay", [P, NJ * GROUPS_PER_BLOCK])
        pick_unit = sb("pick_unit", [96, UNITS, P], BF16)
        pick_group = sb("pick_group", [96, 4, P], BF16)
        pick_state = sb("pick_state", [96, 2, P], BF16)
        sum_channel = sb("sum_channel", [P, 4, 32])
        mean_ones = sb("mean_ones", [P, P])
        ident = sb("ident", [P, P])
        ones = sb("ones", [RT, P])
        zero = sb("zero", [P, 1])
        after_wait = sb("after_wait", [RT, 1])
        at, first = {}, 0
        for name, n in (("embed_b", 2), ("norm1", 2), ("norm2", 2), ("norm3", 2), ("dt_b", NJ),
                        ("skip", NJ), ("b1_gate", UNITS), ("b1_linear", UNITS)):
            at[name] = first
            first += n

        def col(name, k):
            return vec[:, at[name] + k:at[name] + k + 1]

        x_patch = sb("x_patch", [P, KP, T])
        h0 = sb("h0", [P, 2, T])
        centered = sb("centered", [P, 2, T])
        squares = sb("squares", [P, 2, T])
        normed = squares
        root = sb("root", [RT, 4, 6])
        diag = sb("diag", [RT, 6, RT])
        y1 = sb("y1", [P, 2, T])
        gate_tanh = sb("gate_tanh", [P, 2, T])
        z = sb("z", [P, NJ, T])
        dt_in = sb("dt_in", [DT_RANK, T])
        bc = sb("bc", [32, 2, T])
        bc_mid = sb("bc_mid", [32, T], BF16)
        bc_parts = sb("bc_parts", [96, T], BF16)
        b_all = sb("b_all", [P, T])
        c_all = sb("c_all", [P, T])
        sp_exp = sb("sp_exp", [P, NJ, T])
        u_left = sb("u_left", [P, NJ, T])
        dt = sb("dt", [P, NJ, T])
        u = sb("u", [P, NJ, T])
        y = sb("y", [P, NJ, T])
        shared = sb("shared", [P, 3 * NJ * T // 2])
        dt_parts = shared[:, :].bitcast(BF16).rearrange("p (a j t) -> p a j t", a=3, j=NJ)
        ffn = shared[:, 0:NF * T].rearrange("p (k t) -> p k t", k=NF)
        u_parts = sb("u_parts", [P, 3, NJ, T], BF16)
        dt_rows = sb("dt_rows", [96, NJ, 4, T], BF16)
        u_rows = sb("u_rows", [96, NJ, 4, T], BF16)
        a_bar = sb("a_bar", [P, 2, 2 * T])
        b_x = sb("b_x", [P, 2, 2 * T])
        state = sb("state", [P, 2, 2 * T])
        read = sb("read", [P, 2, 2 * T])
        ffn_gate = sb("ffn_gate", [P, T])
        t_in = sb("t_in", [P, 2, T])
        t_high = sb("t_high", [P, 2, T], F32R)
        t_low = sb("t_low", [P, 2, T], F32R)
        base = sb("base", [P, 2, T])
        logits = sb("logits", [RT, 3, EXPERTS + 4])
        replaced = sb("replaced", [RT, 3, EXPERTS + 4])
        top8 = sb("top8", [RT, 3, 8])
        top4 = sb("top4", [RT, 3, 8])
        route = sb("route", [RT, 3, EXPERTS])
        chosen = sb("chosen", [RT, 3, EXPERTS])
        route_sum = sb("route_sum", [RT, 2, 3])
        mix_w = sb("mix_w", [EXPERTS, T])
        mix_r = sb("mix_r", [EXPERTS, T])
        mix_mid = sb("mix_mid", [EXPERTS, T], BF16)
        mix_parts = sb("mix_parts", [96, T], BF16)

        HALF = PAIR_COLS // 2
        w1 = sb("w1", [P, 2, 3, PAIR_COLS], F32R)
        scratch = sb("scratch", [P, 9 * T])
        w1_raw = scratch[:, 0:2 * HALF].rearrange("p (a n) -> p a n", a=2)

        def piece(n):
            return scratch[:, n * T:(n + 1) * T]

        g_raw, l_raw, g_tanh, g_act, glu = piece(0), piece(1), piece(2), piece(3), piece(4)
        g_min, l_clip = (piece(5), piece(6)), (piece(7), piece(8))
        hid = sb("hid", [P, 4, T])
        result = sb("result", [P, 2, T])

        pa = ctx.enter_context(nc.psum_tensor("pa", [P, 3, 512], F32))
        pb = ctx.enter_context(nc.psum_tensor("pb", [P, 5, 512], F32))
        GATE, LINEAR, WEIGHT, SUM, SUM_REST = range(5)

        w1_store = nc.dram_tensor("w1_store", [PAIRS, P, 3, PAIR_COLS], F32).ap()

        load_embed = signal("load_embed", 0)
        load_ssm = signal("load_ssm", 0)
        load_late = signal("load_late", 0)
        constants = signal("constants", 0)
        in_halved = signal("in_halved", 0)
        late_prepared = signal("late_prepared", 0)
        decay_exp = signal("decay_exp", 0)
        decay_ready = signal("decay_ready", 0)
        w1_raw_in = signal("w1_raw_in", 0)
        w1_high_done = signal("w1_high_done", 0)
        w1_low_done = signal("w1_low_done", 0)
        w1_stored = signal("w1_stored", 0)

        patches_in = signal("patches_in", 1, 16)
        pe_embed = signal("pe_embed", 2)
        embedded = signal("embedded", 2)
        pe_mean = signal("pe_mean", 2)
        is_centered = signal("is_centered", 2)
        squared = signal("squared", 3)
        pe_var = signal("pe_var", 3)
        root_steps = signal("root_steps", 3 * ROOT_STEPS)
        pe_root = signal("pe_root", 3)
        y1_ready = signal("y1_ready", 3)
        norm_ready = signal("norm_ready", 4)
        pe_in = signal("pe_in", 2 * NJ)
        tanh_ready = signal("tanh_ready", NJ)
        z_ready = signal("z_ready", NJ)
        pe_xproj = signal("pe_xproj", 1)
        dt_in_ready = signal("dt_in_ready", 1)
        bc_copied = signal("bc_copied", 1)
        bc_split = signal("bc_split", 4)
        bc_placed = signal("bc_placed", 2)
        pe_bc = signal("pe_bc", 2)
        bc_ready = signal("bc_ready", 2)
        pe_dt = signal("pe_dt", NJ)
        v_abs = signal("v_abs", NJ)
        v_max = signal("v_max", NJ)
        exp_ready = signal("exp_ready", 1)
        poly = signal("poly", len(LOG1P) + 1)
        u_ready = signal("u_ready", 1)
        part_high = signal("part_high", 2)
        part_mid = signal("part_mid", 2)
        dt_res = signal("dt_res", 2)
        u_res = signal("u_res", 2)
        dt_stacked = signal("dt_stacked", 12, 16)
        u_stacked = signal("u_stacked", 12, 16)
        pe_dt_all = signal("pe_dt_all", 2 * SCAN_STEPS)
        pe_u_all = signal("pe_u_all", 2 * SCAN_STEPS)
        decayed = signal("decayed", 2 * SCAN_STEPS)
        bx_ready = signal("bx_ready", 2 * SCAN_STEPS)
        scanned = signal("scanned", SCAN_STEPS)
        read_out = signal("read_out", SCAN_STEPS)
        pe_y = signal("pe_y", SCAN_STEPS)
        y_ready = signal("y_ready", NJ)
        pe_out = signal("pe_out", 1)
        pe_ffn = signal("pe_ffn", 2 * NF)
        ffn_tanh = signal("ffn_tanh", NF)
        ffn_gated = signal("ffn_gated", NF)
        ffn_ready = signal("ffn_ready", NF)
        pe_down = signal("pe_down", 1)
        h1_ready = signal("h1_ready", 1)
        base_ready = signal("base_ready", 2)
        t_ready = signal("t_ready", 2)
        t_high_ready = signal("t_high_ready", 1)
        t_low_ready = signal("t_low_ready", 1)
        pe_logits = signal("pe_logits", 1)
        route_steps = signal("route_steps", 10)
        route_exp = signal("route_exp", 1)
        pe_mix = signal("pe_mix", 1)
        mix_copied = signal("mix_copied", 1)
        mix_split = signal("mix_split", 4)
        mix_placed = signal("mix_placed", 2)

        w1_in = [signal(f"w1_in{k}", PAIRS // 2, 16) for k in range(2)]
        pe_gate = signal("pe_gate", UNITS)
        pe_linear = signal("pe_linear", UNITS)
        pe_weight = signal("pe_weight", UNITS)
        gate_copied = signal("gate_copied", UNITS)
        linear_copied = signal("linear_copied", UNITS)
        gate_min = signal("gate_min", UNITS)
        linear_clip = signal("linear_clip", UNITS)
        g_tanh_ready = signal("g_tanh_ready", UNITS)
        gate_act = signal("gate_act", UNITS)
        glu_ready = signal("glu_ready", UNITS)
        hid_ready = signal("hid_ready", UNITS)
        pe_hid = signal("pe_hid", UNITS // 2)
        result_part = signal("result_part", 3)
        stored = signal("stored", 2, 16)

        block = ctx.enter_context(nc.Block())

        def run(engine, steps):
            for phase, step, i in ORDER:
                if phase == "A":
                    if step in steps:
                        steps[step](0, i)
                    if step == "scan" and i < 2 * PAIRS:
                        steps.get("split_w1", lambda i: None)(i)
            with engine.Fori(1, CHUNKS) as c:
                for phase, step, i in ORDER:
                    name = step if phase == "A" else "experts_" + step
                    if name in steps:
                        steps[name](c if phase == "A" else c - 1, i)
            for phase, step, i in ORDER:
                if phase == "B" and "experts_" + step in steps:
                    steps["experts_" + step](CHUNKS - 1, i)

        def scan_slot(i, k):
            j, r = divmod(i, GROUPS_PER_BLOCK // 2)
            q, pair = divmod(r, 2)
            return j, q, 2 * pair + k

        def over_images(ap):
            return ap.rearrange("p (n l) -> p n l", n=CHUNK_IMAGES)[:, :, 1:TOKENS_PER_IMAGE]

        def twice(ap):
            return ap.unsqueeze(1).to_broadcast([P, 2, T])

        EMBED_LOADS = ((w_embed[:, :, :], embed_w), (vec[:, :], vectors), (mean_ones[:, :], ones_mean),
                       (ident[:, :], identity))
        SSM_LOADS = ((w_in[:, :, :], in_w), (w_in_rest[:, :, :], in_w_rest),
                     (w_xproj[:, :, :], xproj_w), (pick_state[:, :, :], state_pick),
                     (w_dt[:, :], dt_w), (decay[:, :], decay_log), (pick_group[:, :, :], group_pick),
                     (sum_channel[:, :, :], channel_sum))
        LATE_LOADS = ((w_out[:, :, :], out_w), (w_ffn[:, :, :], ffn_w), (w_ffn_rest[:, :, :], ffn_w_rest),
                      (w_down[:, :, :], ffn_down), (w_router[:, :], router_w),
                      (w_router_rest[:, :], router_w_rest), (b_router[:, :], router_b),
                      (w2[:, :, :], expert_w2), (b2[:, :], expert_b2),
                      (pick_unit[:, :, :], unit_pick))

        @block.sync
        def _(sp):
            def stack(c, _):
                if after_first(c):
                    sp.wait_ge(pe_dt_all.sem, pe_dt_all.at(c - 1, 2 * SCAN_STEPS))
                    sp.wait_ge(pe_u_all.sem, pe_u_all.at(c - 1, 2 * SCAN_STEPS))
                sp.wait_ge(dt_res.sem, dt_res.at(c, 2))
                for part in range(3):
                    for b in range(4):
                        sp.dma_start(dt_rows[32 * part:32 * part + 32, :, b, :],
                                     dt_parts[32 * b:32 * b + 32, part, :, :]).then_inc(dt_stacked.sem, 16)
                sp.wait_ge(u_res.sem, u_res.at(c, 2))
                for part in range(3):
                    for b in range(4):
                        sp.dma_start(u_rows[32 * part:32 * part + 32, :, b, :],
                                     u_parts[32 * b:32 * b + 32, part, :, :]).then_inc(u_stacked.sem, 16)

            def split_w1(n):
                e, half = divmod(n, 2)
                if n:
                    sp.wait_ge(w1_high_done.sem, n)
                    sp.wait_ge(w1_low_done.sem, n)
                if n and half == 0:
                    sp.dma_start(w1_store[e - 1], w1[:, (e - 1) % 2, :, :].bitcast(F32)).then_inc(w1_stored.sem, 16)
                sp.dma_start(w1_raw, expert_w1[e][:, :, half * HALF:(half + 1) * HALF]).then_inc(w1_raw_in.sem, 16)
                if n == 2 * PAIRS - 1:
                    sp.wait_ge(w1_high_done.sem, n + 1)
                    sp.wait_ge(w1_low_done.sem, n + 1)
                    sp.dma_start(w1_store[e], w1[:, e % 2, :, :].bitcast(F32)).then_inc(w1_stored.sem, 16)
                    sp.wait_ge(w1_stored.sem, 16 * PAIRS)
                    for k in range(2):
                        sp.dma_start(w1[:, k, :, :].bitcast(F32), w1_store[k]).then_inc(w1_in[k].sem, 16)

            def embed(c, _):
                if after_first(c):
                    sp.wait_ge(pe_embed.sem, pe_embed.at(c - 1, 2))
                    sp.dma_start(x_patch[:, :, :], patches[c]).then_inc(patches_in.sem, 16)

            def experts_linear(c, un):
                e = un // 3
                if un % 3 == 2 and (e + 2 < PAIRS or after_first(c)):
                    sp.wait_ge(pe_linear.sem, pe_linear.at(c, un + 1))
                    sp.dma_start(w1[:, e % 2, :, :].bitcast(F32), w1_store[(e + 2) % PAIRS]).then_inc(w1_in[e % 2].sem, 16)

            def experts_finish(c, _):
                sp.wait_ge(result_part.sem, result_part.at(c, 1))
                sp.dma_start(out_main[c], result[:, 0, :]).then_inc(stored.sem, 16)
                sp.wait_ge(result_part.sem, result_part.at(c, 3))
                sp.dma_start(out_rest[c], result[0:REST, 1, :]).then_inc(stored.sem, 16)

            for dst, src in EMBED_LOADS[0:1]:
                sp.dma_start(dst, src).then_inc(load_embed.sem, 16)
            sp.dma_start(x_patch[:, :, :], patches[0]).then_inc(patches_in.sem, 16)
            for dst, src in EMBED_LOADS[1:]:
                sp.dma_start(dst, src).then_inc(load_embed.sem, 16)
            for dst, src in SSM_LOADS:
                sp.dma_start(dst, src).then_inc(load_ssm.sem, 16)
            for dst, src in LATE_LOADS:
                sp.dma_start(dst, src).then_inc(load_late.sem, 16)
            run(sp, {"stack": stack, "split_w1": split_w1, "embed": embed,
                     "experts_linear": experts_linear, "experts_finish": experts_finish})
            sp.wait_ge(stored.sem, 2 * 16 * CHUNKS)

        @block.tensor
        def _(pe):
            def mm(out, lhsT, rhs, start, stop):
                return nc.tensor.matmul(out, lhsT, rhs, start=start, stop=stop)

            def embed(c, _):
                if not after_first(c):
                    pe.wait_ge(load_embed.sem, 16 * len(EMBED_LOADS))
                pe.wait_ge(patches_in.sem, patches_in.at(c, 1))
                if after_first(c):
                    pe.wait_ge(mix_copied.sem, mix_copied.at(c - 1, 1))
                    pe.wait_ge(root_steps.sem, root_steps.at(c - 1, 2 * ROOT_STEPS + 1))
                for m in range(2):
                    for k in range(KP):
                        last = mm(pa[:, m, 0:T], w_embed[:, k, m * P:(m + 1) * P], x_patch[:, k, :],
                                  k == 0, k == KP - 1)
                    last.then_inc(pe_embed.sem, 1)

            def feature_mean(bank, x, done):
                mm(pa[:, bank, 0:T], mean_ones[:, :], x[:, 0, :], True, False)
                mm(pa[:, bank, 0:T], mean_ones[0:REST, :], x[0:REST, 1, :], False, True).then_inc(done.sem, 1)

            def center(c, _):
                if after_first(c):
                    pe.wait_ge(route_steps.sem, route_steps.at(c - 1, 1))
                pe.wait_ge(embedded.sem, embedded.at(c, 2))
                feature_mean(2, h0, pe_mean)

            def token_means(bank):
                for i in range(3):
                    o = pa[0:RT, bank, i:i + 1]
                    mm(o, squares[:, 0, RT * i:RT * (i + 1)], mean_ones[:, 0:1], True, False)
                    last = mm(o, squares[0:REST, 1, RT * i:RT * (i + 1)], mean_ones[0:REST, 0:1], False, True)
                last.then_inc(pe_var.sem, 1)

            def spread_roots(c, n, banks):
                pe.wait_ge(root_steps.sem, root_steps.at(c, ROOT_STEPS * n))
                for k, bank in enumerate(banks):
                    last = mm(pa[:, bank, 0:T], ones[0:RT, :],
                              diag[:, 3 * k:3 * k + 3, :].rearrange("p i t -> p (i t)"), True, True)
                last.then_inc(pe_root.sem, 1)

            def variance(c, _):
                pe.wait_ge(squared.sem, squared.at(c, 1))
                token_means(2)

            def scale(c, _):
                spread_roots(c, 1, (0, 1))

            def two_tiles(bank, w, w_rest, which, m, done):
                mm(pa[:, bank, 0:T], w[:, which, m * P:(m + 1) * P], normed[:, 0, :], True, False)
                mm(pa[:, bank, 0:T], w_rest[:, which, m * P:(m + 1) * P], normed[0:REST, 1, :],
                   False, True).then_inc(done.sem, 1)

            def inproj(c, j):
                if j == 0:
                    if not after_first(c):
                        pe.wait_ge(load_ssm.sem, 16 * len(SSM_LOADS))
                        pe.wait_ge(in_halved.sem, 1)
                    pe.wait_ge(norm_ready.sem, norm_ready.at(c, 2))
                if j == 2:
                    pe.wait_ge(tanh_ready.sem, tanh_ready.at(c, 1))
                two_tiles((2 * j) % 3, w_in, w_in_rest, 0, j, pe_in)
                if j:
                    pe.wait_ge(z_ready.sem, z_ready.at(c, j))
                two_tiles((2 * j + 1) % 3, w_in, w_in_rest, 1, j, pe_in)

            def xproj(c, _):
                pe.wait_ge(z_ready.sem, z_ready.at(c, NJ))
                for j in range(NJ):
                    last = mm(pa[:, 0, 0:T], w_xproj[:, j, :], z[:, j, :], j == 0, j == NJ - 1)
                last.then_inc(pe_xproj.sem, 1)

            def delta(c, _):
                pe.wait_ge(dt_in_ready.sem, dt_in_ready.at(c, 1))
                for j in range(NJ):
                    if j == 2:
                        pe.wait_ge(bc_copied.sem, bc_copied.at(c, 1))
                    mm(pa[:, (j + 1) % 3, 0:T], w_dt[:, j * P:(j + 1) * P], dt_in[:, :],
                       True, True).then_inc(pe_dt.sem, 1)

            def broadcast(c, _):
                pe.wait_ge(bc_split.sem, bc_split.at(c, 4))
                pe.wait_ge(bc_placed.sem, bc_placed.at(c, 2))
                for k in range(2):
                    pe.wait_ge(v_max.sem, v_max.at(c, k + 1))
                    mm(pa[:, 1 + k, 0:T], pick_state[:, k, :], bc_parts[:, :], True, True).then_inc(pe_bc.sem, 1)

            def expand(c, i, k):
                j, q, b = scan_slot(i, k)
                n = 2 * i + k
                if n == 0:
                    pe.wait_ge(dt_stacked.sem, dt_stacked.at(c, 12))
                    pe.wait_ge(v_max.sem, v_max.at(c, NJ))
                else:
                    pe.wait_ge(decayed.sem, decayed.at(c, n))
                mm(pa[:, 0, 0:T], pick_group[:, q, :], dt_rows[:, j, b, :], True, True).then_inc(pe_dt_all.sem, 1)
                if n == 0:
                    pe.wait_ge(u_stacked.sem, u_stacked.at(c, 12))
                    pe.wait_ge(bc_ready.sem, bc_ready.at(c, 1))
                else:
                    pe.wait_ge(bx_ready.sem, bx_ready.at(c, n))
                mm(pa[:, 1, 0:T], pick_group[:, q, :], u_rows[:, j, b, :], True, True).then_inc(pe_u_all.sem, 1)

            def collect(c, i):
                if i == 0:
                    pe.wait_ge(bc_ready.sem, bc_ready.at(c, 2))
                elif i % (GROUPS_PER_BLOCK // 2) == 0:
                    pe.wait_ge(y_ready.sem, y_ready.at(c, i // (GROUPS_PER_BLOCK // 2)))
                pe.wait_ge(read_out.sem, read_out.at(c, i + 1))
                for k in range(2):
                    _, q, b = scan_slot(i, k)
                    last = mm(pa[32 * b:32 * b + 32, 2, 0:T], sum_channel[:, q, :],
                              read[:, i % 2, k * T:(k + 1) * T], q == 0, q == 3)
                last.then_inc(pe_y.sem, 1)

            def outproj(c, _):
                if not after_first(c):
                    pe.wait_ge(load_late.sem, 16 * len(LATE_LOADS))
                    pe.wait_ge(late_prepared.sem, 3)
                pe.wait_ge(y_ready.sem, y_ready.at(c, NJ))
                for m in range(2):
                    for j in range(NJ):
                        last = mm(pa[:, m, 0:T], w_out[:, j, m * P:(m + 1) * P], y[:, j, :], j == 0, j == NJ - 1)
                last.then_inc(pe_out.sem, 1)

            def variance2(c, _):
                pe.wait_ge(squared.sem, squared.at(c, 2))
                token_means(2)

            def scale2(c, _):
                spread_roots(c, 2, (0,))

            def ffn_up(c, k):
                if k == 0:
                    pe.wait_ge(norm_ready.sem, norm_ready.at(c, 4))
                for which in range(2):
                    n = 2 * k + which
                    if n >= 3:
                        before = n - 3
                        if before % 2:
                            pe.wait_ge(ffn_ready.sem, ffn_ready.at(c, before // 2 + 1))
                        else:
                            pe.wait_ge(ffn_gated.sem, ffn_gated.at(c, before // 2 + 1))
                    two_tiles(n % 3, w_ffn, w_ffn_rest, which, k, pe_ffn)

            def down(c, _):
                pe.wait_ge(ffn_ready.sem, ffn_ready.at(c, NF))
                for m in range(2):
                    for k in range(NF):
                        last = mm(pa[:, 1 + m, 0:T], w_down[:, k, m * P:(m + 1) * P], ffn[:, k, :],
                                  k == 0, k == NF - 1)
                last.then_inc(pe_down.sem, 1)

            def center3(c, _):
                pe.wait_ge(h1_ready.sem, h1_ready.at(c, 1))
                feature_mean(0, h0, pe_mean)

            def variance3(c, _):
                pe.wait_ge(squared.sem, squared.at(c, 3))
                token_means(1)

            def scale3(c, _):
                spread_roots(c, 3, (0, 2))

            def topk(c, _):
                pe.wait_ge(t_ready.sem, t_ready.at(c, 2))
                for i in range(3):
                    o = pa[0:RT, 2, EXPERTS * i:EXPERTS * (i + 1)]
                    mm(o, t_in[:, 0, RT * i:RT * (i + 1)], w_router[:, :], True, False)
                    mm(o, t_in[0:REST, 1, RT * i:RT * (i + 1)], w_router_rest[:, :], False, False)
                    last = mm(o, ones[0:1, 0:RT], b_router[:, :], False, True)
                last.then_inc(pe_logits.sem, 1)

            def weights(c, _):
                pe.wait_ge(route_steps.sem, route_steps.at(c, 10))
                for i in range(3):
                    last = nc.tensor.transpose(pa[0:EXPERTS, 0, RT * i:RT * (i + 1)], route[:, i, :],
                                               ident[0:RT, 0:RT])
                last.then_inc(pe_mix.sem, 1)

            def experts_start(c, _):
                pe.wait_ge(mix_copied.sem, mix_copied.at(c, 1))
                pe.wait_ge(mix_split.sem, mix_split.at(c, 4))
                pe.wait_ge(mix_placed.sem, mix_placed.at(c, 2))
                pe.wait_ge(t_high_ready.sem, t_high_ready.at(c, 1))
                pe.wait_ge(t_low_ready.sem, t_low_ready.at(c, 1))
                mm(pb[:, SUM, 0:T], b2[:, 0:P], mix_w[:, :], True, False)
                mm(pb[0:REST, SUM_REST, 0:T], b2[:, P:HIDDEN], mix_w[:, :], True, False)

            def experts_up(bank, e, first):
                cols = slice(first, first + P)
                o = pb[:, bank, 0:T]
                w = w1[:, e % 2, :, cols]
                mm(o, w[:, 0, :], t_high[:, 0, :], True, False)
                mm(o, w[:, 1, :], t_high[:, 0, :], False, False)
                mm(o, w[:, 0, :], t_low[:, 0, :], False, False)
                mm(o, w[:, 2, :], t_high[:, 1, :], False, False)
                return mm(o, w[0:REST, 2, :], t_low[0:REST, 1, :], False, True)

            def experts_gate(c, un):
                e, k = divmod(un, 3)
                if k == 0:
                    pe.wait_ge(w1_in[e % 2].sem, w1_in[e % 2].at(c, e // 2 + 1))
                if un:
                    pe.wait_ge(gate_copied.sem, gate_copied.at(c, un))
                experts_up(GATE, e, 2 * k * P).then_inc(pe_gate.sem, 1)

            def experts_linear(c, un):
                e, k = divmod(un, 3)
                if un:
                    pe.wait_ge(linear_copied.sem, linear_copied.at(c, un))
                experts_up(LINEAR, e, (2 * k + 1) * P).then_inc(pe_linear.sem, 1)

            def experts_mix(c, un):
                if un:
                    pe.wait_ge(hid_ready.sem, hid_ready.at(c, un))
                mm(pb[:, WEIGHT, 0:T], pick_unit[:, un, :], mix_parts[:, :], True, True).then_inc(pe_weight.sem, 1)

            def experts_down(c, v):
                pe.wait_ge(hid_ready.sem, hid_ready.at(c, v + 1))
                for un in (v - 1, v):
                    mm(pb[:, SUM, 0:T], w2[:, un, 0:P], hid[:, un % 4, :], False, un == UNITS - 1)
                for k, un in enumerate((v - 1, v)):
                    last = mm(pb[k * REST:(k + 1) * REST, SUM_REST, 0:T], w2[:, un, P:HIDDEN],
                              hid[:, un % 4, :], un == 1, un >= UNITS - 2)
                last.then_inc(pe_hid.sem, 1)

            run(pe, {
                "embed": embed, "center": center, "variance": variance, "scale": scale, "inproj": inproj,
                "xproj": xproj, "delta": delta, "broadcast": broadcast,
                "scan": lambda c, i: expand(c, i, 0), "scan_second": lambda c, i: expand(c, i, 1),
                "collect": collect, "outproj": outproj, "variance2": variance2, "scale2": scale2,
                "ffn": ffn_up, "down": down, "center3": center3, "variance3": variance3, "scale3": scale3, "topk": topk,
                "weights": weights, "experts_start": experts_start, "experts_gate": experts_gate,
                "experts_linear": experts_linear, "experts_mix": experts_mix,
                "experts_down": experts_down})

        @block.scalar
        def _(act):
            def activate(out, in_, func, **kw):
                return nc.scalar.activation(out, in_, func, **kw)

            def embed(c, _):
                if after_first(c):
                    act.wait_ge(base_ready.sem, base_ready.at(c - 1, 2))
                for m in range(2):
                    act.wait_ge(pe_embed.sem, pe_embed.at(c, m + 1))
                    activate(h0[:, m, :], pa[:, m, 0:T], ACT.Identity, bias=col("embed_b", m)).then_inc(embedded.sem, 1)

            def center(c, _):
                act.wait_ge(is_centered.sem, is_centered.at(c, 1))
                activate(squares[:, :, :], centered[:, :, :], ACT.Square).then_inc(squared.sem, 1)

            def inproj(c, j):
                act.wait_ge(pe_in.sem, pe_in.at(c, 2 * j + 2))
                if j >= 2:
                    act.wait_ge(z_ready.sem, z_ready.at(c, j - 1))
                activate(gate_tanh[:, j % 2, :], pa[:, (2 * j + 1) % 3, 0:T], ACT.Tanh, scale=0.5)\
                    .then_inc(tanh_ready.sem, 1)

            def xproj(c, _):
                act.wait_ge(pe_xproj.sem, pe_xproj.at(c, 1))
                activate(dt_in[:, :], pa[0:DT_RANK, 0, 0:T], ACT.Copy).then_inc(dt_in_ready.sem, 1)

            def delta(c, _):
                for j in range(NJ):
                    act.wait_ge(pe_dt.sem, pe_dt.at(c, j + 1))
                    activate(sp_exp[:, j, :], pa[:, (j + 1) % 3, 0:T], ACT.Abs, bias=col("dt_b", j))\
                        .then_inc(v_abs.sem, 1)
                act.wait_ge(v_abs.sem, v_abs.at(c, NJ))
                activate(sp_exp[:, :, :], sp_exp[:, :, :], ACT.Exp, scale=-1.0).then_inc(exp_ready.sem, 1)

            def broadcast(c, _):
                act.wait_ge(bc_split.sem, bc_split.at(c, 3))
                activate(bc_parts[32:64, :], bc_mid[:, :], ACT.Copy).then_inc(bc_placed.sem, 1)
                act.wait_ge(bc_split.sem, bc_split.at(c, 4))
                activate(bc_parts[64:96, :], bc[:, 0, :], ACT.Copy).then_inc(bc_placed.sem, 1)
                for k, tile in enumerate((b_all, c_all)):
                    act.wait_ge(pe_bc.sem, pe_bc.at(c, k + 1))
                    activate(tile[:, :], pa[:, 1 + k, 0:T], ACT.Copy).then_inc(bc_ready.sem, 1)

            def stack(c, _):
                if after_first(c):
                    act.wait_ge(dt_stacked.sem, dt_stacked.at(c - 1, 12))
                    act.wait_ge(u_stacked.sem, u_stacked.at(c - 1, 12))
                act.wait_ge(poly.sem, poly.at(c, len(LOG1P) + 1))
                activate(dt_parts[:, 0, :, :], dt[:, :, :], ACT.Copy).then_inc(part_high.sem, 1)
                act.wait_ge(u_ready.sem, u_ready.at(c, 1))
                activate(u_parts[:, 0, :, :], u[:, :, :], ACT.Copy).then_inc(part_high.sem, 1)
                act.wait_ge(dt_res.sem, dt_res.at(c, 1))
                activate(dt_parts[:, 1, :, :], sp_exp[:, :, :], ACT.Copy).then_inc(part_mid.sem, 1)
                act.wait_ge(u_res.sem, u_res.at(c, 1))
                activate(u_parts[:, 1, :, :], u_left[:, :, :], ACT.Copy).then_inc(part_mid.sem, 1)

            def decay_group(c, i, k):
                j, q, b = scan_slot(i, k)
                group = GROUPS_PER_BLOCK * j + 4 * b + q
                if not after_first(c) and i == 0 and k == 0:
                    act.wait_ge(constants.sem, 1)
                    act.wait_ge(decay_ready.sem, 1)
                if i >= 2:
                    act.wait_ge(scanned.sem, scanned.at(c, i - 1))
                act.wait_ge(pe_dt_all.sem, pe_dt_all.at(c, 2 * i + k + 1))
                activate(over_images(a_bar[:, i % 2, k * T:(k + 1) * T]), over_images(pa[:, 0, 0:T]), ACT.Exp,
                         scale=decay[:, group:group + 1]).then_inc(decayed.sem, 1)

            def split_w1(n):
                e, half = divmod(n, 2)
                cols = slice(half * HALF, (half + 1) * HALF)
                act.wait_ge(w1_raw_in.sem, 16 * (n + 1))
                if e >= 2:
                    act.wait_ge(w1_stored.sem, 16 * (e - 1))
                activate(w1[:, e % 2, 0, cols], w1_raw[:, 0, :], ACT.Copy)
                activate(w1[:, e % 2, 2, cols], w1_raw[:, 1, :], ACT.Copy).then_inc(w1_high_done.sem, 1)

            def variance2(c, _):
                act.wait_ge(y1_ready.sem, y1_ready.at(c, 2))
                activate(squares[:, :, :], y1[:, :, :], ACT.Square).then_inc(squared.sem, 1)

            def ffn_gate_tanh(c, k):
                act.wait_ge(pe_ffn.sem, pe_ffn.at(c, 2 * k + 1))
                if k >= 2:
                    act.wait_ge(ffn_gated.sem, ffn_gated.at(c, k - 1))
                activate(gate_tanh[:, k % 2, :], pa[:, (2 * k) % 3, 0:T], ACT.Tanh, scale=0.5).then_inc(ffn_tanh.sem, 1)

            def center3(c, _):
                act.wait_ge(is_centered.sem, is_centered.at(c, 2))
                activate(squares[:, :, :], centered[:, :, :], ACT.Square).then_inc(squared.sem, 1)

            def scale3(c, _):
                if after_first(c):
                    act.wait_ge(pe_linear.sem, pe_linear.at(c - 1, UNITS))
                act.wait_ge(t_ready.sem, t_ready.at(c, 2))
                activate(t_high[:, :, :], t_in[:, :, :], ACT.Copy).then_inc(t_high_ready.sem, 1)

            def topk(c, _):
                act.wait_ge(route_steps.sem, route_steps.at(c, 6))
                activate(route[:, :, :], route[:, :, :], ACT.Exp).then_inc(route_exp.sem, 1)

            def weights(c, _):
                act.wait_ge(pe_mix.sem, pe_mix.at(c, 1))
                activate(mix_w[:, :], pa[0:EXPERTS, 0, 0:T], ACT.Copy).then_inc(mix_copied.sem, 1)
                if after_first(c):
                    act.wait_ge(pe_weight.sem, pe_weight.at(c - 1, UNITS))
                act.wait_ge(mix_split.sem, mix_split.at(c, 3))
                activate(mix_parts[32:32 + EXPERTS, :], mix_mid[:, :], ACT.Copy).then_inc(mix_placed.sem, 1)
                act.wait_ge(mix_split.sem, mix_split.at(c, 4))
                activate(mix_parts[64:64 + EXPERTS, :], mix_r[:, :], ACT.Copy).then_inc(mix_placed.sem, 1)

            def experts_gate(c, un):
                act.wait_ge(pe_gate.sem, pe_gate.at(c, un + 1))
                if un:
                    act.wait_ge(gate_min.sem, gate_min.at(c, un))
                activate(g_raw, pb[:, GATE, 0:T], ACT.Identity, bias=col("b1_gate", un)).then_inc(gate_copied.sem, 1)

            def experts_linear(c, un):
                act.wait_ge(pe_linear.sem, pe_linear.at(c, un + 1))
                if un:
                    act.wait_ge(linear_clip.sem, linear_clip.at(c, un))
                activate(l_raw, pb[:, LINEAR, 0:T], ACT.Identity, bias=col("b1_linear", un))\
                    .then_inc(linear_copied.sem, 1)

            def experts_mix(c, un):
                act.wait_ge(gate_min.sem, gate_min.at(c, un + 1))
                if un:
                    act.wait_ge(gate_act.sem, gate_act.at(c, un))
                activate(g_tanh, g_min[un % 2], ACT.Tanh, scale=ALPHA / 2).then_inc(g_tanh_ready.sem, 1)

            act.wait_ge(load_ssm.sem, 16 * len(SSM_LOADS))
            activate(decay[:, :], decay[:, :], ACT.Exp).then_inc(decay_exp.sem, 1)
            act.wait_ge(load_embed.sem, 16 * len(EMBED_LOADS))
            run(act, {
                "embed": embed, "center": center, "inproj": inproj, "xproj": xproj, "delta": delta,
                "broadcast": broadcast, "stack": stack, "split_w1": split_w1,
                "scan": lambda c, i: decay_group(c, i, 0), "scan_second": lambda c, i: decay_group(c, i, 1),
                "variance2": variance2, "ffn": ffn_gate_tanh, "center3": center3, "scale3": scale3,
                "topk": topk, "weights": weights, "experts_gate": experts_gate,
                "experts_linear": experts_linear, "experts_mix": experts_mix})

        @block.vector
        def _(dve):
            def center(c, _):
                dve.wait_ge(embedded.sem, embedded.at(c, 2))
                dve.wait_ge(pe_mean.sem, pe_mean.at(c, 1))
                dve.tensor_tensor(centered[:, :, :], h0[:, :, :], twice(pa[:, 2, 0:T]), ALU.subtract)\
                    .then_inc(is_centered.sem, 1)

            def roots(c, n, bank, ln_eps, rms_eps):
                step = ROOT_STEPS * (n - 1)
                x, r, s, bits = root[:, 0, :], root[:, 1, :], root[:, 2, :], root[:, 3, :].bitcast(I32)
                v = pa[0:RT, bank, 0:3]
                dve.wait_ge(pe_var.sem, pe_var.at(c, n))
                dve.tensor_scalar(x[:, 0:3], v, ln_eps, None, ALU.add)
                dve.tensor_scalar(x[:, 3:6], v, 1.0 + rms_eps, ln_eps * rms_eps, ALU.mult, ALU.add)\
                    .then_inc(root_steps.sem, 1)
                dve.wait_ge(root_steps.sem, root_steps.at(c, step + 1))
                dve.tensor_scalar(bits, x.bitcast(I32), 1, None, ALU.arith_shift_right).then_inc(root_steps.sem, 1)
                dve.wait_ge(root_steps.sem, root_steps.at(c, step + 2))
                dve.tensor_scalar(r.bitcast(I32), bits, -1.0, ROOT_GUESS, ALU.mult, ALU.add)\
                    .then_inc(root_steps.sem, 1)
                for k in range(3):
                    dve.wait_ge(root_steps.sem, root_steps.at(c, step + 3 * k + 3))
                    dve.scalar_tensor_tensor(s, r, -0.5, r, ALU.mult, ALU.mult).then_inc(root_steps.sem, 1)
                    dve.wait_ge(root_steps.sem, root_steps.at(c, step + 3 * k + 4))
                    dve.tensor_tensor(s, s, x, ALU.mult).then_inc(root_steps.sem, 1)
                    dve.wait_ge(root_steps.sem, root_steps.at(c, step + 3 * k + 5))
                    dve.scalar_tensor_tensor(r, s, 1.5, r, ALU.add, ALU.mult).then_inc(root_steps.sem, 1)
                dve.wait_ge(root_steps.sem, root_steps.at(c, step + 12))
                dve.tensor_tensor(diag[:, :, :], ident[0:RT, 0:RT].unsqueeze(1).to_broadcast([RT, 6, RT]),
                                  r.unsqueeze(2).to_broadcast([RT, 6, RT]), ALU.mult).then_inc(root_steps.sem, 1)

            def variance(c, _):
                roots(c, 1, 2, 1e-5, 1e-6)

            def scale(c, _):
                dve.wait_ge(pe_root.sem, pe_root.at(c, 1))
                dve.tensor_tensor(y1[:, :, :], centered[:, :, :], twice(pa[:, 0, 0:T]), ALU.mult)\
                    .then_inc(y1_ready.sem, 1)
                for m in range(2):
                    dve.scalar_tensor_tensor(normed[:, m, :], centered[:, m, :], col("norm1", m),
                                             pa[:, 1, 0:T], ALU.mult, ALU.mult).then_inc(norm_ready.sem, 1)

            def inproj(c, j):
                dve.wait_ge(tanh_ready.sem, tanh_ready.at(c, j + 1))
                dve.scalar_tensor_tensor(z[:, j, :], gate_tanh[:, j % 2, :], 1.0, pa[:, (2 * j) % 3, 0:T],
                                         ALU.add, ALU.mult).then_inc(z_ready.sem, 1)

            def xproj(c, _):
                dve.wait_ge(dt_in_ready.sem, dt_in_ready.at(c, 1))
                dve.tensor_copy(bc[:, 0, :], pa[DT_RANK:P, 0, 0:T]).then_inc(bc_copied.sem, 1)

            def delta(c, _):
                for j in range(NJ):
                    dve.wait_ge(v_abs.sem, v_abs.at(c, j + 1))
                    dve.tensor_scalar(u[:, j, :], pa[:, (j + 1) % 3, 0:T], col("dt_b", j), 0.0,
                                      ALU.add, ALU.max).then_inc(v_max.sem, 1)

            def log1p(c, _):
                dve.wait_ge(exp_ready.sem, exp_ready.at(c, 1))
                dve.wait_ge(v_max.sem, v_max.at(c, NJ))
                dve.tensor_scalar(dt[:, :, :], sp_exp[:, :, :], LOG1P[-1], None, ALU.mult).then_inc(poly.sem, 1)
                for n, coefficient in enumerate(LOG1P[-2::-1]):
                    dve.wait_ge(poly.sem, poly.at(c, n + 1))
                    dve.scalar_tensor_tensor(dt[:, :, :], dt[:, :, :], coefficient, sp_exp[:, :, :],
                                             ALU.add, ALU.mult).then_inc(poly.sem, 1)
                dve.wait_ge(poly.sem, poly.at(c, len(LOG1P)))
                dve.tensor_tensor(dt[:, :, :], dt[:, :, :], u[:, :, :], ALU.add).then_inc(poly.sem, 1)

            def stack(c, _):
                dve.wait_ge(part_high.sem, part_high.at(c, 1))
                dve.tensor_tensor(sp_exp[:, :, :], dt[:, :, :], dt_parts[:, 0, :, :], ALU.subtract)\
                    .then_inc(dt_res.sem, 1)
                dve.wait_ge(part_mid.sem, part_mid.at(c, 1))
                dve.tensor_tensor(dt_parts[:, 2, :, :], sp_exp[:, :, :], dt_parts[:, 1, :, :], ALU.subtract)\
                    .then_inc(dt_res.sem, 1)

            def split_w1(n):
                e, half = divmod(n, 2)
                cols = slice(half * HALF, (half + 1) * HALF)
                dve.wait_ge(w1_high_done.sem, n + 1)
                dve.tensor_tensor(w1[:, e % 2, 1, cols], w1_raw[:, 0, :],
                                   w1[:, e % 2, 0, cols].bitcast(F32), ALU.subtract)
                low = w1[REST:P, e % 2, 2, cols]
                dve.tensor_tensor(low, w1_raw[REST:P, 1, :], low.bitcast(F32), ALU.subtract)\
                    .then_inc(w1_low_done.sem, 1)

            def drive(c, i, k):
                if i == 0:
                    dve.wait_ge(bc_ready.sem, bc_ready.at(c, 1))
                dve.wait_ge(pe_u_all.sem, pe_u_all.at(c, 2 * i + k + 1))
                dve.tensor_tensor(b_x[:, i % 2, k * T:(k + 1) * T], b_all[:, :], pa[:, 1, 0:T], ALU.mult)\
                    .then_inc(bx_ready.sem, 1)

            def advance(c, i):
                dve.wait_ge(decayed.sem, decayed.at(c, 2 * i + 2))
                dve.wait_ge(bx_ready.sem, bx_ready.at(c, 2 * i + 2))
                if i >= 2:
                    dve.wait_ge(read_out.sem, read_out.at(c, i - 1))
                dve.tensor_tensor_scan(state[:, i % 2, :], a_bar[:, i % 2, :], b_x[:, i % 2, :], 0.0,
                                       ALU.mult, ALU.add).then_inc(scanned.sem, 1)

            def collect(c, i):
                per_block = GROUPS_PER_BLOCK // 2
                if i % per_block == per_block - 1:
                    j = i // per_block
                    dve.wait_ge(pe_y.sem, pe_y.at(c, i + 1))
                    dve.scalar_tensor_tensor(y[:, j, :], z[:, j, :], col("skip", j), pa[:, 2, 0:T],
                                             ALU.mult, ALU.add).then_inc(y_ready.sem, 1)

            def outproj(c, _):
                dve.wait_ge(pe_out.sem, pe_out.at(c, 1))
                dve.tensor_tensor(y1[:, :, :], y1[:, :, :], pa[:, 0:2, 0:T], ALU.add).then_inc(y1_ready.sem, 1)

            def variance2(c, _):
                roots(c, 2, 2, 1e-6, 0.0)

            def scale2(c, _):
                dve.wait_ge(pe_root.sem, pe_root.at(c, 2))
                for m in range(2):
                    dve.scalar_tensor_tensor(normed[:, m, :], y1[:, m, :], col("norm2", m), pa[:, 0, 0:T],
                                             ALU.mult, ALU.mult).then_inc(norm_ready.sem, 1)

            def ffn_product(c, k):
                dve.wait_ge(ffn_tanh.sem, ffn_tanh.at(c, k + 1))
                if k:
                    dve.wait_ge(ffn_ready.sem, ffn_ready.at(c, k))
                dve.scalar_tensor_tensor(ffn_gate[:, :], gate_tanh[:, k % 2, :], 1.0, pa[:, (2 * k) % 3, 0:T],
                                         ALU.add, ALU.mult).then_inc(ffn_gated.sem, 1)
                dve.wait_ge(ffn_gated.sem, ffn_gated.at(c, k + 1))
                dve.wait_ge(pe_ffn.sem, pe_ffn.at(c, 2 * k + 2))
                if k == 0:
                    dve.wait_ge(dt_stacked.sem, dt_stacked.at(c, 12))
                dve.tensor_tensor(ffn[:, k, :], ffn_gate[:, :], pa[:, (2 * k + 1) % 3, 0:T], ALU.mult)\
                    .then_inc(ffn_ready.sem, 1)

            def down(c, _):
                dve.wait_ge(pe_down.sem, pe_down.at(c, 1))
                dve.tensor_tensor(y1[:, :, :], y1[:, :, :], pa[:, 1:3, 0:T], ALU.add).then_inc(y1_ready.sem, 1)
                dve.wait_ge(y1_ready.sem, y1_ready.at(c, 3))
                dve.tensor_tensor(h0[:, :, :], h0[:, :, :], y1[:, :, :], ALU.add).then_inc(h1_ready.sem, 1)

            def center3(c, _):
                dve.wait_ge(h1_ready.sem, h1_ready.at(c, 1))
                dve.wait_ge(pe_mean.sem, pe_mean.at(c, 2))
                dve.tensor_tensor(centered[:, :, :], h0[:, :, :], twice(pa[:, 0, 0:T]), ALU.subtract)\
                    .then_inc(is_centered.sem, 1)

            def variance3(c, _):
                roots(c, 3, 1, 1e-5, 1e-5)

            def scale3(c, _):
                dve.wait_ge(pe_root.sem, pe_root.at(c, 3))
                for m in range(2):
                    dve.scalar_tensor_tensor(t_in[:, m, :], centered[:, m, :], col("norm3", m),
                                             pa[:, 2, 0:T], ALU.mult, ALU.mult).then_inc(t_ready.sem, 1)
                dve.tensor_tensor(base[:, :, :], centered[:, :, :], twice(pa[:, 0, 0:T]), ALU.mult)\
                    .then_inc(base_ready.sem, 1)
                dve.wait_ge(t_high_ready.sem, t_high_ready.at(c, 1))
                dve.wait_ge(t_ready.sem, t_ready.at(c, 2))
                dve.tensor_tensor(t_low[:, :, :], t_in[:, :, :], t_high[:, :, :].bitcast(F32), ALU.subtract)\
                    .then_inc(t_low_ready.sem, 1)

            def topk(c, _):
                E = EXPERTS
                dve.wait_ge(pe_logits.sem, pe_logits.at(c, 1))
                dve.tensor_copy(logits[:, :, 0:E], pa[0:RT, 2, 0:3 * E].rearrange("p (i e) -> p i e", i=3))\
                    .then_inc(route_steps.sem, 1)
                dve.wait_ge(route_steps.sem, route_steps.at(c, 1))
                dve.memset(after_wait[:, :], 0.0)
                for i in range(3):
                    last = dve.max(top8[:, i, :], logits[:, i, 0:E])
                last.then_inc(route_steps.sem, 1)
                dve.wait_ge(route_steps.sem, route_steps.at(c, 2))
                dve.tensor_copy(top4[:, :, 0:TOP_K], top8[:, :, 0:TOP_K]).then_inc(route_steps.sem, 1)
                dve.wait_ge(route_steps.sem, route_steps.at(c, 3))
                dve.memset(after_wait[:, :], 0.0)
                for i in range(3):
                    last = dve.match_replace(replaced[:, i, :], top4[:, i, :], logits[:, i, :], -PAD_LOGIT)
                last.then_inc(route_steps.sem, 1)
                dve.wait_ge(route_steps.sem, route_steps.at(c, 4))
                dve.tensor_tensor(chosen[:, :, :], replaced[:, :, 0:E], logits[:, :, 0:E], ALU.not_equal)\
                    .then_inc(route_steps.sem, 1)
                dve.tensor_tensor(route[:, :, :], logits[:, :, 0:E],
                                  top8[:, :, 0:1].to_broadcast([RT, 3, E]), ALU.subtract)\
                    .then_inc(route_steps.sem, 1)
                dve.wait_ge(route_steps.sem, route_steps.at(c, 5))
                dve.wait_ge(route_exp.sem, route_exp.at(c, 1))
                dve.tensor_tensor(route[:, :, :], route[:, :, :], chosen[:, :, :], ALU.mult)\
                    .then_inc(route_steps.sem, 1)
                dve.wait_ge(route_steps.sem, route_steps.at(c, 7))
                dve.reduce_sum(route_sum[:, 0, :], route[:, :, :], AX.X).then_inc(route_steps.sem, 1)
                dve.wait_ge(route_steps.sem, route_steps.at(c, 8))
                dve.reciprocal(route_sum[:, 1, :], route_sum[:, 0, :]).then_inc(route_steps.sem, 1)
                dve.wait_ge(route_steps.sem, route_steps.at(c, 9))
                dve.tensor_tensor(route[:, :, :], route[:, :, :],
                                  route_sum[:, 1, :].unsqueeze(2).to_broadcast([RT, 3, E]), ALU.mult)\
                    .then_inc(route_steps.sem, 1)
                if after_first(c):
                    dve.wait_ge(stored.sem, stored.at(c - 1, 2))

            def experts_gate(c, un):
                dve.wait_ge(gate_copied.sem, gate_copied.at(c, un + 1))
                if un >= 2:
                    dve.wait_ge(gate_act.sem, gate_act.at(c, un - 1))
                dve.tensor_scalar(g_min[un % 2], g_raw, LIMIT, None, ALU.min).then_inc(gate_min.sem, 1)

            def experts_linear(c, un):
                dve.wait_ge(linear_copied.sem, linear_copied.at(c, un + 1))
                if un >= 2:
                    dve.wait_ge(glu_ready.sem, glu_ready.at(c, un - 1))
                dve.tensor_scalar(l_clip[un % 2], l_raw, 1.0 + LIMIT, 1.0 - LIMIT, ALU.min, ALU.max)\
                    .then_inc(linear_clip.sem, 1)

            def experts_mix(c, un):
                dve.wait_ge(g_tanh_ready.sem, g_tanh_ready.at(c, un + 1))
                if un:
                    dve.wait_ge(glu_ready.sem, glu_ready.at(c, un))
                dve.scalar_tensor_tensor(g_act, g_tanh, 1.0, g_min[un % 2], ALU.add, ALU.mult)\
                    .then_inc(gate_act.sem, 1)

            def experts_scale(c, un):
                dve.wait_ge(glu_ready.sem, glu_ready.at(c, un + 1))
                dve.wait_ge(pe_weight.sem, pe_weight.at(c, un + 1))
                if un >= 4:
                    dve.wait_ge(pe_hid.sem, pe_hid.at(c, (un - 4) // 2 + 1))
                dve.tensor_tensor(hid[:, un % 4, :], glu, pb[:, WEIGHT, 0:T], ALU.mult).then_inc(hid_ready.sem, 1)

            def experts_finish(c, _):
                dve.wait_ge(base_ready.sem, base_ready.at(c, 2))
                dve.wait_ge(pe_hid.sem, pe_hid.at(c, UNITS // 2))
                dve.tensor_tensor(result[:, 0, :], base[:, 0, :], pb[:, SUM, 0:T], ALU.add)\
                    .then_inc(result_part.sem, 1)
                dve.tensor_tensor(result[0:REST, 1, :], base[0:REST, 1, :], pb[0:REST, SUM_REST, 0:T], ALU.add)\
                    .then_inc(result_part.sem, 1)
                dve.wait_ge(result_part.sem, result_part.at(c, 2))
                dve.tensor_tensor(result[0:REST, 1, :], result[0:REST, 1, :], pb[REST:P, SUM_REST, 0:T], ALU.add)\
                    .then_inc(result_part.sem, 1)

            dve.wait_ge(load_embed.sem, 16 * len(EMBED_LOADS))
            dve.wait_ge(constants.sem, 1)
            run(dve, {
                "center": center, "variance": variance, "scale": scale, "inproj": inproj, "xproj": xproj,
                "delta": delta, "log1p": log1p, "stack": stack, "split_w1": split_w1,
                "scan": lambda c, i: drive(c, i, 0), "scan_second": lambda c, i: drive(c, i, 1),
                "advance": advance, "collect": collect, "outproj": outproj, "variance2": variance2,
                "scale2": scale2, "ffn": ffn_product, "down": down, "center3": center3,
                "variance3": variance3, "scale3": scale3, "topk": topk, "experts_gate": experts_gate,
                "experts_linear": experts_linear, "experts_mix": experts_mix,
                "experts_scale": experts_scale, "experts_finish": experts_finish})

        @block.gpsimd
        def _(pool):
            def zeros(partitions):
                return zero[0:partitions, :].to_broadcast([partitions, T])

            def xproj(c, _):
                pool.wait_ge(bc_copied.sem, bc_copied.at(c, 1))
                pool.tensor_tensor(bc_parts[0:32, :], bc[:, 0, :], zeros(32), ALU.add).then_inc(bc_split.sem, 1)
                pool.wait_ge(bc_split.sem, bc_split.at(c, 1))
                pool.tensor_tensor(bc[:, 1, :], bc[:, 0, :], bc_parts[0:32, :], ALU.subtract).then_inc(bc_split.sem, 1)
                pool.wait_ge(bc_split.sem, bc_split.at(c, 2))
                pool.tensor_tensor(bc_mid[:, :], bc[:, 1, :], zeros(32), ALU.add).then_inc(bc_split.sem, 1)
                pool.wait_ge(bc_split.sem, bc_split.at(c, 3))
                pool.tensor_tensor(bc[:, 0, :], bc[:, 1, :], bc_mid[:, :], ALU.subtract).then_inc(bc_split.sem, 1)

            def stack(c, _):
                pool.wait_ge(poly.sem, poly.at(c, len(LOG1P) + 1))
                pool.tensor_tensor(u[:, :, :], dt[:, :, :], z[:, :, :], ALU.mult).then_inc(u_ready.sem, 1)
                pool.wait_ge(u_ready.sem, u_ready.at(c, 1))
                pool.wait_ge(part_high.sem, part_high.at(c, 2))
                pool.tensor_tensor(u_left[:, :, :], u[:, :, :], u_parts[:, 0, :, :], ALU.subtract).then_inc(u_res.sem, 1)
                pool.wait_ge(u_res.sem, u_res.at(c, 1))
                pool.wait_ge(part_mid.sem, part_mid.at(c, 2))
                pool.tensor_tensor(u_parts[:, 2, :, :], u_left[:, :, :], u_parts[:, 1, :, :], ALU.subtract)\
                    .then_inc(u_res.sem, 1)

            def advance(c, i):
                if i == 0:
                    pool.wait_ge(bc_ready.sem, bc_ready.at(c, 2))
                pool.wait_ge(scanned.sem, scanned.at(c, i + 1))
                if i >= 2:
                    pool.wait_ge(pe_y.sem, pe_y.at(c, i - 1))
                pool.tensor_tensor(read[:, i % 2, :].rearrange("p (k t) -> p k t", k=2),
                                   state[:, i % 2, :].rearrange("p (k t) -> p k t", k=2),
                                   twice(c_all[:, :]), ALU.mult).then_inc(read_out.sem, 1)

            def scale3(c, _):
                pool.wait_ge(base_ready.sem, base_ready.at(c, 1))
                pool.tensor_tensor(base[:, :, :], base[:, :, :], h0[:, :, :], ALU.add).then_inc(base_ready.sem, 1)

            def weights(c, _):
                if after_first(c):
                    pool.wait_ge(pe_weight.sem, pe_weight.at(c - 1, UNITS))
                pool.wait_ge(mix_copied.sem, mix_copied.at(c, 1))
                pool.tensor_tensor(mix_parts[0:EXPERTS, :], mix_w[:, :], zeros(EXPERTS), ALU.add).then_inc(mix_split.sem, 1)
                pool.wait_ge(mix_split.sem, mix_split.at(c, 1))
                pool.tensor_tensor(mix_r[:, :], mix_w[:, :], mix_parts[0:EXPERTS, :], ALU.subtract)\
                    .then_inc(mix_split.sem, 1)
                pool.wait_ge(mix_split.sem, mix_split.at(c, 2))
                pool.tensor_tensor(mix_mid[:, :], mix_r[:, :], zeros(EXPERTS), ALU.add).then_inc(mix_split.sem, 1)
                pool.wait_ge(mix_split.sem, mix_split.at(c, 3))
                pool.tensor_tensor(mix_r[:, :], mix_r[:, :], mix_mid[:, :], ALU.subtract).then_inc(mix_split.sem, 1)

            def experts_mix(c, un):
                pool.wait_ge(gate_act.sem, gate_act.at(c, un + 1))
                pool.wait_ge(linear_clip.sem, linear_clip.at(c, un + 1))
                if un:
                    pool.wait_ge(hid_ready.sem, hid_ready.at(c, un))
                pool.tensor_tensor(glu, g_act, l_clip[un % 2], ALU.mult).then_inc(glu_ready.sem, 1)

            pool.memset(zero[:, :], 0.0)
            pool.memset(ones[:, :], 1.0)
            pool.memset(a_bar[:, :, :], 0.0)
            pool.memset(mix_parts[:, :], 0.0)
            pool.memset(logits[:, :, EXPERTS:EXPERTS + 4], PAD_LOGIT)
            pool.memset(top4[:, :, TOP_K:8], PAD_LOGIT).then_inc(constants.sem, 1)
            pool.wait_ge(constants.sem, 1)
            pool.wait_ge(load_ssm.sem, 16 * len(SSM_LOADS))
            pool.tensor_scalar(w_in[:, 0, :], w_in[:, 0, :], 0.5, None, ALU.mult)
            pool.tensor_scalar(w_in_rest[:, 0, :], w_in_rest[:, 0, :], 0.5, None, ALU.mult)\
                .then_inc(in_halved.sem, 1)
            pool.wait_ge(decay_exp.sem, 1)
            pool.tensor_scalar(decay[:, :], decay[:, :], -1.0, None, ALU.mult).then_inc(decay_ready.sem, 1)

            def late(c, _):
                if not after_first(c):
                    pool.wait_ge(load_late.sem, 16 * len(LATE_LOADS))
                    pool.tensor_scalar(w_ffn[:, 1, :], w_ffn[:, 1, :], 0.5, None, ALU.mult)
                    pool.tensor_scalar(w_ffn_rest[:, 1, :], w_ffn_rest[:, 1, :], 0.5, None, ALU.mult)\
                        .then_inc(late_prepared.sem, 1)
                    pool.tensor_scalar(w2[:, :, :], w2[:, :, :], 0.5, None, ALU.mult).then_inc(late_prepared.sem, 1)
                    linear = vec[:, at["b1_linear"]:at["b1_linear"] + UNITS]
                    pool.tensor_scalar(linear, linear, 1.0, None, ALU.add).then_inc(late_prepared.sem, 1)

            run(pool, {
                "xproj": xproj, "delta": late, "stack": stack, "advance": advance,
                "scale3": scale3, "weights": weights,
                "experts_mix": experts_mix})


def _twice(w):
    return np.concatenate([w, w[..., P:HIDDEN]], axis=-1)


def _tiles(w, n):
    return w.reshape(n, P, -1).transpose(1, 0, 2)


def _picks():
    bfloat16 = mybir.dt.np(BF16)
    unit = np.zeros((96, UNITS, P), np.float32)
    group = np.zeros((96, 4, P), np.float32)
    state = np.zeros((96, 2, P), np.float32)
    total = np.zeros((P, 4, 32), np.float32)
    col = np.arange(P)
    for part in range(3):
        for un in range(UNITS):
            pair, k = divmod(un, 3)
            expert = 2 * pair + (k if k < 2 else col // REST)
            unit[32 * part + expert, un, col] = 1
        for q in range(4):
            group[32 * part + D8 * q + col // STATES, q, col] = 1
        for k in range(2):
            state[32 * part + STATES * k + col % STATES, k, col] = 1
    for q in range(4):
        total[col, q, D8 * q + col // STATES] = 1
    return unit.astype(bfloat16), group.astype(bfloat16), state.astype(bfloat16), total


def _layout(i):
    x = i["x"].reshape(IMAGES, 3, 6, 16, 6, 16).transpose(0, 1, 2, 4, 3, 5).reshape(IMAGES * TOKENS_PER_IMAGE, PATCH_DIM)
    a = {"patches": x.T.reshape(KP, P, CHUNKS, T).transpose(2, 1, 0, 3)}
    a["embed_w"] = _tiles(_twice(i["L0_tok_W"].T), KP)
    w_in = np.stack([i["L0_attn_W_in"].T, i["L0_attn_W_gate"].T], axis=1)
    a["in_w"], a["in_w_rest"] = w_in[:P], w_in[P:]
    a["xproj_w"] = _tiles(i["L0_attn_W_xproj"].T, NJ)
    a["dt_w"] = i["L0_attn_W_dt"].T
    a["out_w"] = _tiles(_twice(i["L0_attn_W_out"].T), NJ)
    w_ffn = np.stack([i["L0_attn_W_gate_ffn"].T, i["L0_attn_W_up"].T], axis=1)
    a["ffn_w"], a["ffn_w_rest"] = w_ffn[:P], w_ffn[P:]
    a["ffn_down"] = _tiles(_twice(i["L0_attn_W_down"].T), NF)
    gate = i["L0_ffn_gate_w"].T
    a["router_w"], a["router_w_rest"] = gate[:P], gate[P:]
    a["router_b"] = i["L0_ffn_gate_b"][None]
    w1, b1, w2 = i["L0_ffn_w1"], i["L0_ffn_b1"][:, None], i["L0_ffn_w2"]
    I = EXPERT_DIM

    def units(w):
        w = w.reshape(PAIRS, 2, w.shape[1], 2, I).transpose(0, 2, 3, 1, 4)
        rest = w[..., P:].reshape(*w.shape[:3], 1, P)
        return np.concatenate([w[..., :P], rest], axis=3).transpose(0, 1, 3, 2, 4)

    w1 = units(w1).reshape(PAIRS, HIDDEN, PAIR_COLS)
    a["expert_w1"] = np.stack([w1[:, :P], np.concatenate([w1[:, P:], w1[:, P:]], axis=1)], axis=2)
    b1 = units(b1).reshape(UNITS, 2, P)
    w2 = w2.reshape(PAIRS, 2, I, HIDDEN)
    w2 = np.concatenate([w2[:, :, :P], w2[:, :, P:].reshape(PAIRS, 1, P, HIDDEN)], axis=1)
    a["expert_w2"] = w2.transpose(2, 0, 1, 3).reshape(P, UNITS, HIDDEN)
    a["expert_b2"] = i["L0_ffn_b2"]
    a["vectors"] = np.concatenate(
        [_twice(i[n]).reshape(2, P) for n in ("L0_tok_b", "L0_attn_w_norm1", "L0_attn_w_ffn_norm", "L0_ffn_scale")]
        + [i["L0_attn_b_dt"].reshape(NJ, P), i["L0_attn_D_skip"].reshape(NJ, P), b1[:, 0], b1[:, 1]]).T
    a["decay_log"] = i["L0_attn_A_log"].reshape(NJ * GROUPS_PER_BLOCK, P).T
    a["unit_pick"], a["group_pick"], a["state_pick"], a["channel_sum"] = _picks()
    a["ones_mean"] = np.full((P, P), 1 / HIDDEN, np.float32)
    a["identity"] = np.eye(P, dtype=np.float32)
    return a


def kernel(**inputs):
    import concourse.bacc as _bacc
    from concourse.bass_utils import run_bass_kernel_spmd as _run

    nc = _bacc.Bacc("TRN2", target_bir_lowering=False, num_devices=1)
    arrays, args = {}, {}
    for name, a in _layout({k: np.asarray(v) for k, v in inputs.items()}).items():
        a = np.ascontiguousarray(a)
        arrays[name] = a
        args[name] = nc.dram_tensor(name, a.shape, mybir.dt.from_np(a.dtype), kind="ExternalInput").ap()
    args["out_main"] = nc.dram_tensor("out_main", (CHUNKS, P, T), F32, kind="ExternalOutput").ap()
    args["out_rest"] = nc.dram_tensor("out_rest", (CHUNKS, REST, T), F32, kind="ExternalOutput").ap()
    vit_tower(nc, **args)
    r = _run(nc, [arrays], core_ids=[0]).results[0]
    features = np.concatenate([r["out_main"], r["out_rest"]], axis=1)
    return features.transpose(0, 2, 1).reshape(IMAGES, TOKENS_PER_IMAGE, HIDDEN)
```

```python
from contextlib import ExitStack

import numpy as np

import concourse.bass as bass
import concourse.mybir as mybir

F32 = mybir.dt.float32
F32R = mybir.dt.float32r
I32 = mybir.dt.int32
ALU = mybir.AluOpType
ACT = mybir.ActivationFunctionType
AX = mybir.AxisListType

P = 128
IMAGES, TOKENS_PER_IMAGE = 32, 36
CHUNK_IMAGES = 8
CHUNKS = IMAGES // CHUNK_IMAGES
T = CHUNK_IMAGES * TOKENS_PER_IMAGE
PATCH_DIM, HIDDEN, INNER, STATES, DT_RANK, FFN_DIM = 768, 192, 384, 16, 96, 512
REST = HIDDEN - P
EXPERTS, TOP_K, EXPERT_DIM = 16, 4, 192
KP = PATCH_DIM // P
NJ = INNER // P
NF = FFN_DIM // P
D8 = P // STATES
GROUPS_PER_BLOCK = P // D8
PAIRS = EXPERTS // 2
UNITS = 3 * PAIRS
PAIR_COLS = 6 * P
STEPS_PER_BLOCK = GROUPS_PER_BLOCK // 2
SCAN_STEPS = NJ * STEPS_PER_BLOCK
RT = T // 3
LIMIT, ALPHA = 7.0, 1.702
PAD_LOGIT = -3.0e38
MIX_ROWS = 32 + EXPERTS

LOG1P = (0.999999971, -0.499995015, 0.333192713, -0.248443699, 0.191114311, -0.136747697,
         0.078361668, -0.0295885074, 0.0052534578)
POLY_STEPS = len(LOG1P) + 1
ROOT_GUESS = float(0x5F3759DF)
ROOT_STEPS = 13


class Signal:

    def __init__(self, semaphore, per_chunk, unit=1):
        self.sem, self.per_chunk, self.unit = semaphore, per_chunk, unit

    def at(self, chunk, k):
        return (chunk * self.per_chunk + k) * self.unit


def after_first(chunk):
    return not isinstance(chunk, int)


def schedule():
    pre = [("embed", 0), ("center", 0), ("variance", 0), ("scale", 0)]
    pre += [("inproj", j) for j in range(NJ)]
    pre += [("xproj", 0), ("delta", 0), ("broadcast", 0), ("log1p", 0), ("split", 0)]
    post = [("outproj", 0), ("variance2", 0), ("scale2", 0)] + [("ffn", k) for k in range(NF)]
    post += [("down", 0), ("center3", 0), ("variance3", 0), ("scale3", 0), ("topk", 0), ("weights", 0)]
    scan = []
    for i in range(SCAN_STEPS):
        j, r = divmod(i, STEPS_PER_BLOCK)
        if r == 2 and j + 1 < NJ:
            scan.append(("log1p", j + 1))
        if r == 4 and j + 1 < NJ:
            scan.append(("split", j + 1))
        scan += [("scan", i), ("advance", i)]
        if i >= 2:
            scan.append(("collect", i - 2))
    scan += [("collect", SCAN_STEPS - 2), ("collect", SCAN_STEPS - 1)]

    pieces = [[("start", 0)]]
    for u in range(UNITS):
        pieces.append([("gate", u)] + ([("scale", u - 1)] if u else []))
        pieces.append([("linear", u), ("mix", u)] + ([("down", u - 2)] if u % 2 and u > 2 else []))
    pieces.append([("scale", UNITS - 1)])
    pieces.append([("down", UNITS - 1), ("finish", 0)])
    out, half = [], 0
    for s in pre + scan + post:
        count = PIECES_BEFORE.get(s, 0)
        if s == ("scale3", 0):
            count = len(pieces)
        for _ in range(min(count, len(pieces))):
            out += [("B",) + p for p in pieces.pop(0)]
        if s in SPLIT_BEFORE:
            out.append(("prologue", "split_w1", half))
            half += 1
        out.append(("A",) + s)
    assert half == 2 * PAIRS
    return out


PIECES_BEFORE = {("center", 0): 2, ("variance", 0): 2, ("scale", 0): 3, ("inproj", 0): 2, ("inproj", 1): 1,
                 ("inproj", 2): 1, ("xproj", 0): 2, ("delta", 0): 2, ("broadcast", 0): 2, ("log1p", 0): 2,
                 ("split", 0): 6, ("scan", 0): 2, ("outproj", 0): 2, ("variance2", 0): 3, ("scale2", 0): 4,
                 ("ffn", 0): 2, ("ffn", 2): 1, ("down", 0): 2, ("center3", 0): 3, ("variance3", 0): 3}
SPLIT_BEFORE = ([("xproj", 0), ("delta", 0), ("broadcast", 0), ("log1p", 0)] + [("scan", i) for i in range(1, 24, 3)]
                + [("outproj", 0), ("scale2", 0), ("ffn", 0), ("down", 0)])


def vit_tower(nc, patches, embed_w, in_w, in_w_rest, xproj_w, dt_w, out_w, ffn_w, ffn_w_rest,
              ffn_down, router_w, router_w_rest, router_b, expert_w1, expert_w2, expert_b2,
              vectors, decay_log, unit_pick, group_pick, state_pick, channel_sum, ones_mean,
              identity, out_main, out_rest):
    ORDER = schedule()
    UNITS_BEFORE_SCAN = sum(s[1] == "linear" for s in ORDER[:ORDER.index(("A", "scan", 0))])
    assert UNITS_BEFORE_SCAN == sum(s[1] == "gate" for s in ORDER[:ORDER.index(("A", "scan", 0))])
    with ExitStack() as ctx:
        def sb(name, shape, dt=F32):
            return ctx.enter_context(nc.sbuf_tensor(name, shape, dt))

        def signal(name, per_chunk, unit=1):
            return Signal(ctx.enter_context(nc.semaphore(name)), per_chunk, unit)

        w_embed = sb("w_embed", [P, KP, 2 * P])
        w_in = sb("w_in", [P, 2, INNER])
        w_in_rest = sb("w_in_rest", [REST, 2, INNER])
        w_xproj = sb("w_xproj", [P, NJ, P])
        w_dt = sb("w_dt", [DT_RANK, INNER])
        w_out = sb("w_out", [P, NJ, 2 * P])
        w_ffn = sb("w_ffn", [P, 2, FFN_DIM])
        w_ffn_rest = sb("w_ffn_rest", [REST, 2, FFN_DIM])
        w_down = sb("w_down", [P, NF, 2 * P])
        w_router = sb("w_router", [P, EXPERTS])
        w_router_rest = sb("w_router_rest", [REST, EXPERTS])
        b_router = sb("b_router", [1, EXPERTS])
        w2 = sb("w2", [P, UNITS, HIDDEN])
        b2 = sb("b2", [EXPERTS, HIDDEN])
        vec = sb("vec", [P, vectors.shape[1]])
        decay = sb("decay", [P, NJ * GROUPS_PER_BLOCK])
        pick_unit = sb("pick_unit", [MIX_ROWS, UNITS, P], F32R)
        pick_group = sb("pick_group", [P, 2 * 4, P], F32R)
        pick_state = sb("pick_state", [2 * 32, 2, P], F32R)
        sum_channel = sb("sum_channel", [P, 4, 32])
        mean_ones = sb("mean_ones", [P, P])
        ident = sb("ident", [P, P])
        ones = sb("ones", [RT, P])
        after_wait = sb("after_wait", [RT, 1])
        at, first = {}, 0
        for name, n in (("embed_b", 2), ("norm1", 2), ("norm2", 2), ("norm3", 2), ("dt_b", NJ),
                        ("skip", NJ), ("b1_gate", UNITS), ("b1_linear", UNITS)):
            at[name] = first
            first += n

        def col(name, k):
            return vec[:, at[name] + k:at[name] + k + 1]

        x_patch = sb("x_patch", [P, KP, T])
        h0 = sb("h0", [P, 2, T])
        centered = sb("centered", [P, 2, T])
        squares = sb("squares", [P, 2, T])
        normed = squares
        root = sb("root", [RT, 4, 6])
        diag = sb("diag", [RT, 6, RT])
        y1 = sb("y1", [P, 2, T])
        gate_tanh = sb("gate_tanh", [P, 2, T])
        z = sb("z", [P, NJ, T])
        dt_in = sb("dt_in", [DT_RANK, T])
        bc = sb("bc", [32, T])
        bc_parts = sb("bc_parts", [2 * 32, T], F32R)
        b_all = sb("b_all", [P, T])
        c_all = sb("c_all", [P, T])
        sp_exp = sb("sp_exp", [P, NJ, T])
        dt = sb("dt", [P, NJ, T])
        u = sb("u", [P, NJ, T])
        y = sb("y", [P, NJ, T])
        ffn = sb("ffn", [P, NF, T])
        dt_rows = sb("dt_rows", [P, NJ, 2, T], F32R)
        u_rows = sb("u_rows", [P, NJ, 2, T], F32R)
        a_bar = sb("a_bar", [P, 2, 2 * T])
        b_x = sb("b_x", [P, 2, 2 * T])
        state = sb("state", [P, 2, 2 * T])
        read = sb("read", [P, 2, 2 * T])
        ffn_gate = sb("ffn_gate", [P, T])
        t_in = sb("t_in", [P, 2, T])
        t_high = sb("t_high", [P, 2, T], F32R)
        t_low = sb("t_low", [P, 2, T], F32R)
        base = sb("base", [P, 2, T])
        logits = sb("logits", [RT, 3, EXPERTS + 4])
        replaced = sb("replaced", [RT, 3, EXPERTS + 4])
        top8 = sb("top8", [RT, 3, 8])
        top4 = sb("top4", [RT, 3, 8])
        route = sb("route", [RT, 3, EXPERTS])
        chosen = sb("chosen", [RT, 3, EXPERTS])
        route_sum = sb("route_sum", [RT, 2, 3])
        mix_w = sb("mix_w", [EXPERTS, T])
        mix_parts = sb("mix_parts", [MIX_ROWS, T], F32R)

        HALF = PAIR_COLS // 2
        w1 = sb("w1", [P, 2, 3, PAIR_COLS], F32R)
        scratch = sb("scratch", [P, 9 * T])
        w1_raw = scratch[:, 0:3 * 2 * HALF].rearrange("p (b a n) -> p b a n", b=3, a=2)

        def piece(n):
            return scratch[:, n * T:(n + 1) * T]

        g_raw, l_raw, g_tanh, g_act, glu = piece(0), piece(1), piece(2), piece(3), piece(4)
        g_min, l_clip = (piece(5), piece(6)), (piece(7), piece(8))
        hid = sb("hid", [P, 4, T])
        result = sb("result", [P, 2, T])

        pa = ctx.enter_context(nc.psum_tensor("pa", [P, 3, 512], F32))
        pb = ctx.enter_context(nc.psum_tensor("pb", [P, 5, 512], F32))
        GATE, LINEAR, WEIGHT, SUM, SUM_REST = range(5)

        w1_store = nc.dram_tensor("w1_store", [PAIRS, P, 3, PAIR_COLS], F32).ap()

        load_embed = signal("load_embed", 0)
        load_ssm = signal("load_ssm", 0)
        load_late = signal("load_late", 0)
        constants = signal("constants", 0)
        in_halved = signal("in_halved", 0)
        bias_raised = signal("bias_raised", 0)
        picks_rounded = signal("picks_rounded", 0)
        decay_exp = signal("decay_exp", 0)
        decay_ready = signal("decay_ready", 0)
        w1_raw_in = [signal(f"w1_raw_in{k}", 0) for k in range(3)]
        w1_high_done = signal("w1_high_done", 0)
        w1_low_done = signal("w1_low_done", 0)
        w1_stored = [signal(f"w1_stored{k}", 0) for k in range(2)]

        patches_in = signal("patches_in", 1, 16)
        pe_embed = signal("pe_embed", 2)
        embedded = signal("embedded", 2)
        pe_mean = signal("pe_mean", 2)
        is_centered = signal("is_centered", 2)
        squared = signal("squared", 3)
        pe_var = signal("pe_var", 3)
        root_steps = signal("root_steps", 3 * ROOT_STEPS)
        pe_root = signal("pe_root", 3)
        y1_ready = signal("y1_ready", 3)
        norm_ready = signal("norm_ready", 4)
        pe_in = signal("pe_in", 2 * NJ)
        tanh_ready = signal("tanh_ready", NJ)
        z_ready = signal("z_ready", NJ)
        pe_xproj = signal("pe_xproj", 1)
        dt_in_ready = signal("dt_in_ready", 1)
        bc_copied = signal("bc_copied", 1)
        bc_high = signal("bc_high", 1)
        bc_low = signal("bc_low", 1)
        pe_bc = signal("pe_bc", 2)
        bc_ready = signal("bc_ready", 2)
        pe_dt = signal("pe_dt", NJ)
        v_abs = signal("v_abs", NJ)
        v_max = signal("v_max", NJ)
        exp_ready = signal("exp_ready", 1)
        poly = signal("poly", NJ * POLY_STEPS)
        u_ready = signal("u_ready", NJ)
        dt_high = signal("dt_high", NJ)
        dt_low = signal("dt_low", NJ)
        u_high = signal("u_high", NJ)
        u_low = signal("u_low", 2 * NJ)
        pe_dt_all = signal("pe_dt_all", 2 * SCAN_STEPS)
        pe_u_all = signal("pe_u_all", SCAN_STEPS)
        decayed = signal("decayed", 2 * SCAN_STEPS)
        bx_ready = signal("bx_ready", SCAN_STEPS)
        scanned = signal("scanned", SCAN_STEPS)
        read_out = signal("read_out", SCAN_STEPS)
        pe_y = signal("pe_y", SCAN_STEPS)
        y_ready = signal("y_ready", NJ)
        pe_out = signal("pe_out", 1)
        pe_ffn = signal("pe_ffn", 2 * NF)
        ffn_tanh = signal("ffn_tanh", NF)
        ffn_gated = signal("ffn_gated", NF)
        ffn_ready = signal("ffn_ready", NF)
        pe_down = signal("pe_down", 1)
        h1_ready = signal("h1_ready", 1)
        base_ready = signal("base_ready", 2)
        t_ready = signal("t_ready", 2)
        t_high_ready = signal("t_high_ready", 1)
        t_low_ready = signal("t_low_ready", 1)
        pe_logits = signal("pe_logits", 1)
        route_steps = signal("route_steps", 10)
        route_exp = signal("route_exp", 1)
        pe_mix = signal("pe_mix", 1)
        mix_copied = signal("mix_copied", 1)
        mix_high = signal("mix_high", 1)
        mix_low = signal("mix_low", 1)

        w1_in = [signal(f"w1_in{k}", PAIRS // 2, 16) for k in range(2)]
        pe_gate = signal("pe_gate", UNITS)
        pe_linear = signal("pe_linear", UNITS)
        pe_weight = signal("pe_weight", UNITS)
        gate_copied = signal("gate_copied", UNITS)
        linear_copied = signal("linear_copied", UNITS)
        gate_min = signal("gate_min", UNITS)
        linear_clip = signal("linear_clip", UNITS)
        g_tanh_ready = signal("g_tanh_ready", UNITS)
        gate_act = signal("gate_act", UNITS)
        glu_ready = signal("glu_ready", UNITS)
        hid_ready = signal("hid_ready", UNITS)
        pe_hid = signal("pe_hid", UNITS // 2)
        result_part = signal("result_part", 3)
        stored = signal("stored", 2, 16)

        block = ctx.enter_context(nc.Block())

        def run(engine, steps):
            for phase, step, i in ORDER:
                if phase == "A" and step in steps:
                    steps[step](0, i)
                elif phase == "prologue" and step in steps:
                    steps[step](i)
            with engine.Fori(1, CHUNKS) as c:
                for phase, step, i in ORDER:
                    name = step if phase == "A" else "experts_" + step
                    if phase != "prologue" and name in steps:
                        steps[name](c if phase == "A" else c - 1, i)
            for phase, step, i in ORDER:
                if phase == "B" and "experts_" + step in steps:
                    steps["experts_" + step](CHUNKS - 1, i)

        raw_state = result[0:64, 0, 0:2 * P].rearrange("p (k n) -> p k n", k=2)
        raw_group = hid[:, :, :].rearrange("p a t -> p (a t)")[:, 0:8 * P].rearrange("p (q n) -> p q n", q=8)
        raw_unit = [tile[0:MIX_ROWS, :, :].rearrange("p a t -> p (a t)")[:, 0:8 * P].rearrange("p (n m) -> p n m", n=8)
                    for tile in (b_x, state, read)]

        def scan_slot(i, k):
            j, r = divmod(i, STEPS_PER_BLOCK)
            q, pair = divmod(r, 2)
            return j, q, 2 * pair + k

        def over_images(ap):
            return ap.rearrange("p (n l) -> p n l", n=CHUNK_IMAGES)[:, :, 1:TOKENS_PER_IMAGE]

        def twice(ap):
            return ap.unsqueeze(1).to_broadcast([P, 2, T])

        EMBED_LOADS = ((w_embed[:, :, :], embed_w), (vec[:, :], vectors), (mean_ones[:, :], ones_mean),
                       (ident[:, :], identity))
        SSM_LOADS = ((w_in[:, :, :], in_w), (w_in_rest[:, :, :], in_w_rest),
                     (w_xproj[:, :, :], xproj_w), (raw_state, state_pick),
                     (w_dt[:, :], dt_w), (decay[:, :], decay_log), (raw_group, group_pick),
                     (sum_channel[:, :, :], channel_sum))
        LATE_LOADS = ((w_out[:, :, :], out_w), (w_ffn[:, :, :], ffn_w), (w_ffn_rest[:, :, :], ffn_w_rest),
                      (w_down[:, :, :], ffn_down), (w_router[:, :], router_w),
                      (w_router_rest[:, :], router_w_rest), (b_router[:, :], router_b),
                      (w2[:, :, :], expert_w2), (b2[:, :], expert_b2),
                      *((raw_unit[k], unit_pick[:, 8 * k:8 * (k + 1), :]) for k in range(3)))

        @block.sync
        def _(sp):
            def split_w1(n):
                if n >= 3:
                    sp.wait_ge(w1_low_done.sem, 2 * (n - 2))
                if n >= 4 and n % 2 == 0:
                    e = n // 2 - 2
                    sp.dma_start(w1_store[e], w1[:, e % 2, :, :].bitcast(F32)).then_inc(w1_stored[e % 2].sem, 16)
                e, half = divmod(n, 2)
                sp.dma_start(w1_raw[:, n % 3, :, :], expert_w1[e][:, :, half * HALF:(half + 1) * HALF])\
                    .then_inc(w1_raw_in[n % 3].sem, 16)
                if n == 2 * PAIRS - 1:
                    for e in (PAIRS - 2, PAIRS - 1):
                        sp.wait_ge(w1_low_done.sem, 2 * (2 * e + 2))
                        sp.dma_start(w1_store[e], w1[:, e % 2, :, :].bitcast(F32)).then_inc(w1_stored[e % 2].sem, 16)
                    for k in range(2):
                        sp.wait_ge(w1_stored[k].sem, 16 * PAIRS // 2)
                    for k in range(2):
                        sp.dma_start(w1[:, k, :, :].bitcast(F32), w1_store[k]).then_inc(w1_in[k].sem, 16)

            def embed(c, _):
                if after_first(c):
                    sp.wait_ge(pe_embed.sem, pe_embed.at(c - 1, 2))
                    sp.dma_start(x_patch[:, :, :], patches[c]).then_inc(patches_in.sem, 16)

            def experts_linear(c, un):
                e = un // 3
                if un % 3 == 2 and (e + 2 < PAIRS or after_first(c)):
                    sp.wait_ge(pe_linear.sem, pe_linear.at(c, un + 1))
                    sp.dma_start(w1[:, e % 2, :, :].bitcast(F32), w1_store[(e + 2) % PAIRS]).then_inc(w1_in[e % 2].sem, 16)

            def experts_finish(c, _):
                sp.wait_ge(result_part.sem, result_part.at(c, 1))
                sp.dma_start(out_main[c], result[:, 0, :]).then_inc(stored.sem, 16)
                sp.wait_ge(result_part.sem, result_part.at(c, 3))
                sp.dma_start(out_rest[c], result[0:REST, 1, :]).then_inc(stored.sem, 16)

            for dst, src in EMBED_LOADS[0:1]:
                sp.dma_start(dst, src).then_inc(load_embed.sem, 16)
            sp.dma_start(x_patch[:, :, :], patches[0]).then_inc(patches_in.sem, 16)
            for dst, src in EMBED_LOADS[1:]:
                sp.dma_start(dst, src).then_inc(load_embed.sem, 16)
            for dst, src in SSM_LOADS:
                sp.dma_start(dst, src).then_inc(load_ssm.sem, 16)
            for dst, src in LATE_LOADS:
                sp.dma_start(dst, src).then_inc(load_late.sem, 16)
            run(sp, {"split_w1": split_w1, "embed": embed,
                     "experts_linear": experts_linear, "experts_finish": experts_finish})
            sp.wait_ge(stored.sem, 2 * 16 * CHUNKS)

        @block.tensor
        def _(pe):
            def mm(out, lhsT, rhs, start, stop):
                return nc.tensor.matmul(out, lhsT, rhs, start=start, stop=stop)

            def embed(c, _):
                if not after_first(c):
                    pe.wait_ge(load_embed.sem, 16 * len(EMBED_LOADS))
                pe.wait_ge(patches_in.sem, patches_in.at(c, 1))
                if after_first(c):
                    pe.wait_ge(mix_copied.sem, mix_copied.at(c - 1, 1))
                    pe.wait_ge(root_steps.sem, root_steps.at(c - 1, 2 * ROOT_STEPS + 1))
                for m in range(2):
                    for k in range(KP):
                        last = mm(pa[:, m, 0:T], w_embed[:, k, m * P:(m + 1) * P], x_patch[:, k, :],
                                  k == 0, k == KP - 1)
                    last.then_inc(pe_embed.sem, 1)

            def feature_mean(bank, x, done):
                mm(pa[:, bank, 0:T], mean_ones[:, :], x[:, 0, :], True, False)
                mm(pa[:, bank, 0:T], mean_ones[0:REST, :], x[0:REST, 1, :], False, True).then_inc(done.sem, 1)

            def center(c, _):
                if after_first(c):
                    pe.wait_ge(route_steps.sem, route_steps.at(c - 1, 1))
                pe.wait_ge(embedded.sem, embedded.at(c, 2))
                feature_mean(2, h0, pe_mean)

            def token_means(bank):
                for i in range(3):
                    o = pa[0:RT, bank, i:i + 1]
                    mm(o, squares[:, 0, RT * i:RT * (i + 1)], mean_ones[:, 0:1], True, False)
                    last = mm(o, squares[0:REST, 1, RT * i:RT * (i + 1)], mean_ones[0:REST, 0:1], False, True)
                last.then_inc(pe_var.sem, 1)

            def spread_roots(c, n, banks):
                pe.wait_ge(root_steps.sem, root_steps.at(c, ROOT_STEPS * n))
                for k, bank in enumerate(banks):
                    last = mm(pa[:, bank, 0:T], ones[0:RT, :],
                              diag[:, 3 * k:3 * k + 3, :].rearrange("p i t -> p (i t)"), True, True)
                last.then_inc(pe_root.sem, 1)

            def variance(c, _):
                pe.wait_ge(squared.sem, squared.at(c, 1))
                token_means(2)

            def scale(c, _):
                spread_roots(c, 1, (0, 1))

            def two_tiles(bank, w, w_rest, which, m, done):
                mm(pa[:, bank, 0:T], w[:, which, m * P:(m + 1) * P], normed[:, 0, :], True, False)
                mm(pa[:, bank, 0:T], w_rest[:, which, m * P:(m + 1) * P], normed[0:REST, 1, :],
                   False, True).then_inc(done.sem, 1)

            def inproj(c, j):
                if j == 0:
                    if not after_first(c):
                        pe.wait_ge(load_ssm.sem, 16 * len(SSM_LOADS))
                        pe.wait_ge(in_halved.sem, 1)
                    pe.wait_ge(norm_ready.sem, norm_ready.at(c, 2))
                if j == 2:
                    pe.wait_ge(tanh_ready.sem, tanh_ready.at(c, 1))
                two_tiles((2 * j) % 3, w_in, w_in_rest, 0, j, pe_in)
                if j:
                    pe.wait_ge(z_ready.sem, z_ready.at(c, j))
                two_tiles((2 * j + 1) % 3, w_in, w_in_rest, 1, j, pe_in)

            def xproj(c, _):
                pe.wait_ge(z_ready.sem, z_ready.at(c, NJ))
                for j in range(NJ):
                    last = mm(pa[:, 0, 0:T], w_xproj[:, j, :], z[:, j, :], j == 0, j == NJ - 1)
                last.then_inc(pe_xproj.sem, 1)

            def delta(c, _):
                pe.wait_ge(dt_in_ready.sem, dt_in_ready.at(c, 1))
                for j in range(NJ):
                    if j == 2:
                        pe.wait_ge(bc_copied.sem, bc_copied.at(c, 1))
                    mm(pa[:, (j + 1) % 3, 0:T], w_dt[:, j * P:(j + 1) * P], dt_in[:, :],
                       True, True).then_inc(pe_dt.sem, 1)

            def broadcast(c, _):
                if not after_first(c):
                    pe.wait_ge(picks_rounded.sem, 1)
                pe.wait_ge(bc_high.sem, bc_high.at(c, 1))
                pe.wait_ge(bc_low.sem, bc_low.at(c, 1))
                for k in range(2):
                    pe.wait_ge(v_max.sem, v_max.at(c, k + 1))
                    mm(pa[:, 1 + k, 0:T], pick_state[:, k, :], bc_parts[:, :], True, True).then_inc(pe_bc.sem, 1)

            def expand(c, i):
                for k in range(2):
                    j, q, b = scan_slot(i, k)
                    if i == 0 and k == 0:
                        pe.wait_ge(v_max.sem, v_max.at(c, NJ))
                        pe.wait_ge(bc_ready.sem, bc_ready.at(c, 1))
                    if i:
                        pe.wait_ge(decayed.sem, decayed.at(c, 2 * i - 1 + k))
                    if i % STEPS_PER_BLOCK == 0 and k == 0:
                        pe.wait_ge(dt_high.sem, dt_high.at(c, j + 1))
                        pe.wait_ge(dt_low.sem, dt_low.at(c, j + 1))
                    mm(pa[:, k, 0:T], pick_group[:, 4 * (b % 2) + q, :], dt_rows[:, j, b // 2, :],
                       True, True).then_inc(pe_dt_all.sem, 1)
                if i:
                    pe.wait_ge(bx_ready.sem, bx_ready.at(c, i))
                elif after_first(c):
                    pe.wait_ge(gate_copied.sem, gate_copied.at(c - 1, UNITS_BEFORE_SCAN))
                    pe.wait_ge(linear_copied.sem, linear_copied.at(c - 1, UNITS_BEFORE_SCAN))
                if i % STEPS_PER_BLOCK == 0:
                    pe.wait_ge(u_high.sem, u_high.at(c, j + 1))
                    pe.wait_ge(u_low.sem, u_low.at(c, 2 * j + 2))
                for k in range(2):
                    j, q, b = scan_slot(i, k)
                    last = mm(pb[:, k, 0:T], pick_group[:, 4 * (b % 2) + q, :], u_rows[:, j, b // 2, :], True, True)
                last.then_inc(pe_u_all.sem, 1)

            def collect(c, i):
                if i == 0:
                    pe.wait_ge(bc_ready.sem, bc_ready.at(c, 2))
                elif i % STEPS_PER_BLOCK == 0:
                    pe.wait_ge(y_ready.sem, y_ready.at(c, i // STEPS_PER_BLOCK))
                pe.wait_ge(read_out.sem, read_out.at(c, i + 1))
                for k in range(2):
                    _, q, b = scan_slot(i, k)
                    last = mm(pa[32 * b:32 * b + 32, 2, 0:T], sum_channel[:, q, :],
                              read[:, i % 2, k * T:(k + 1) * T], q == 0, q == 3)
                last.then_inc(pe_y.sem, 1)

            def outproj(c, _):
                if not after_first(c):
                    pe.wait_ge(load_late.sem, 16 * len(LATE_LOADS))
                    pe.wait_ge(picks_rounded.sem, 2)
                    pe.wait_ge(bias_raised.sem, 1)
                pe.wait_ge(y_ready.sem, y_ready.at(c, NJ))
                for m in range(2):
                    for j in range(NJ):
                        last = mm(pa[:, m, 0:T], w_out[:, j, m * P:(m + 1) * P], y[:, j, :], j == 0, j == NJ - 1)
                last.then_inc(pe_out.sem, 1)

            def variance2(c, _):
                pe.wait_ge(squared.sem, squared.at(c, 2))
                token_means(2)

            def scale2(c, _):
                spread_roots(c, 2, (0,))

            def ffn_up(c, k):
                if k == 0:
                    pe.wait_ge(norm_ready.sem, norm_ready.at(c, 4))
                for which in range(2):
                    n = 2 * k + which
                    if n >= 3:
                        before = n - 3
                        if before % 2:
                            pe.wait_ge(ffn_ready.sem, ffn_ready.at(c, before // 2 + 1))
                        else:
                            pe.wait_ge(ffn_gated.sem, ffn_gated.at(c, before // 2 + 1))
                    two_tiles(n % 3, w_ffn, w_ffn_rest, which, k, pe_ffn)

            def down(c, _):
                pe.wait_ge(ffn_ready.sem, ffn_ready.at(c, NF))
                for m in range(2):
                    for k in range(NF):
                        last = mm(pa[:, 1 + m, 0:T], w_down[:, k, m * P:(m + 1) * P], ffn[:, k, :],
                                  k == 0, k == NF - 1)
                last.then_inc(pe_down.sem, 1)

            def center3(c, _):
                pe.wait_ge(h1_ready.sem, h1_ready.at(c, 1))
                feature_mean(0, h0, pe_mean)

            def variance3(c, _):
                pe.wait_ge(squared.sem, squared.at(c, 3))
                token_means(1)

            def scale3(c, _):
                spread_roots(c, 3, (0, 2))

            def topk(c, _):
                pe.wait_ge(t_ready.sem, t_ready.at(c, 2))
                for i in range(3):
                    o = pa[0:RT, 2, EXPERTS * i:EXPERTS * (i + 1)]
                    mm(o, t_in[:, 0, RT * i:RT * (i + 1)], w_router[:, :], True, False)
                    mm(o, t_in[0:REST, 1, RT * i:RT * (i + 1)], w_router_rest[:, :], False, False)
                    last = mm(o, ones[0:1, 0:RT], b_router[:, :], False, True)
                last.then_inc(pe_logits.sem, 1)

            def weights(c, _):
                pe.wait_ge(route_steps.sem, route_steps.at(c, 10))
                for i in range(3):
                    last = nc.tensor.transpose(pa[0:EXPERTS, 0, RT * i:RT * (i + 1)], route[:, i, :],
                                               ident[0:RT, 0:RT])
                last.then_inc(pe_mix.sem, 1)

            def experts_start(c, _):
                pe.wait_ge(mix_copied.sem, mix_copied.at(c, 1))
                pe.wait_ge(mix_high.sem, mix_high.at(c, 1))
                pe.wait_ge(mix_low.sem, mix_low.at(c, 1))
                pe.wait_ge(t_high_ready.sem, t_high_ready.at(c, 1))
                pe.wait_ge(t_low_ready.sem, t_low_ready.at(c, 1))
                mm(pb[:, SUM, 0:T], b2[:, 0:P], mix_w[:, :], True, False)
                mm(pb[0:REST, SUM_REST, 0:T], b2[:, P:HIDDEN], mix_w[:, :], True, False)

            def experts_up(bank, e, first):
                cols = slice(first, first + P)
                o = pb[:, bank, 0:T]
                w = w1[:, e % 2, :, cols]
                mm(o, w[:, 0, :], t_high[:, 0, :], True, False)
                mm(o, w[:, 1, :], t_high[:, 0, :], False, False)
                mm(o, w[:, 0, :], t_low[:, 0, :], False, False)
                mm(o, w[:, 2, :], t_high[:, 1, :], False, False)
                return mm(o, w[0:REST, 2, :], t_low[0:REST, 1, :], False, True)

            def experts_gate(c, un):
                e, k = divmod(un, 3)
                if k == 0:
                    pe.wait_ge(w1_in[e % 2].sem, w1_in[e % 2].at(c, e // 2 + 1))
                if un:
                    pe.wait_ge(gate_copied.sem, gate_copied.at(c, un))
                experts_up(GATE, e, 2 * k * P).then_inc(pe_gate.sem, 1)

            def experts_linear(c, un):
                e, k = divmod(un, 3)
                if un:
                    pe.wait_ge(linear_copied.sem, linear_copied.at(c, un))
                experts_up(LINEAR, e, (2 * k + 1) * P).then_inc(pe_linear.sem, 1)

            def experts_scale(c, un):
                if un:
                    pe.wait_ge(hid_ready.sem, hid_ready.at(c, un))
                mm(pb[:, WEIGHT, 0:T], pick_unit[:, un, :], mix_parts[:, :], True, True).then_inc(pe_weight.sem, 1)

            def experts_down(c, v):
                pe.wait_ge(hid_ready.sem, hid_ready.at(c, v + 1))
                for un in (v - 1, v):
                    mm(pb[:, SUM, 0:T], w2[:, un, 0:P], hid[:, un % 4, :], False, un == UNITS - 1)
                for k, un in enumerate((v - 1, v)):
                    last = mm(pb[k * REST:(k + 1) * REST, SUM_REST, 0:T], w2[:, un, P:HIDDEN],
                              hid[:, un % 4, :], un == 1, un >= UNITS - 2)
                last.then_inc(pe_hid.sem, 1)

            run(pe, {
                "embed": embed, "center": center, "variance": variance, "scale": scale, "inproj": inproj,
                "xproj": xproj, "delta": delta, "broadcast": broadcast,
                "scan": expand,
                "collect": collect, "outproj": outproj, "variance2": variance2, "scale2": scale2,
                "ffn": ffn_up, "down": down, "center3": center3, "variance3": variance3, "scale3": scale3, "topk": topk,
                "weights": weights, "experts_start": experts_start, "experts_gate": experts_gate,
                "experts_linear": experts_linear, "experts_scale": experts_scale,
                "experts_down": experts_down})

        @block.scalar
        def _(act):
            def activate(out, in_, func, **kw):
                return nc.scalar.activation(out, in_, func, **kw)

            def embed(c, _):
                if after_first(c):
                    act.wait_ge(base_ready.sem, base_ready.at(c - 1, 2))
                for m in range(2):
                    act.wait_ge(pe_embed.sem, pe_embed.at(c, m + 1))
                    activate(h0[:, m, :], pa[:, m, 0:T], ACT.Identity, bias=col("embed_b", m)).then_inc(embedded.sem, 1)

            def center(c, _):
                act.wait_ge(is_centered.sem, is_centered.at(c, 1))
                activate(squares[:, :, :], centered[:, :, :], ACT.Square).then_inc(squared.sem, 1)

            def inproj(c, j):
                act.wait_ge(pe_in.sem, pe_in.at(c, 2 * j + 2))
                if j >= 2:
                    act.wait_ge(z_ready.sem, z_ready.at(c, j - 1))
                activate(gate_tanh[:, j % 2, :], pa[:, (2 * j + 1) % 3, 0:T], ACT.Tanh, scale=0.5)\
                    .then_inc(tanh_ready.sem, 1)

            def xproj(c, _):
                act.wait_ge(pe_xproj.sem, pe_xproj.at(c, 1))
                activate(dt_in[:, :], pa[0:DT_RANK, 0, 0:T], ACT.Copy).then_inc(dt_in_ready.sem, 1)
                act.wait_ge(bc_copied.sem, bc_copied.at(c, 1))
                activate(bc_parts[0:32, :], bc[:, :], ACT.Copy).then_inc(bc_high.sem, 1)

            def delta(c, _):
                for j in range(NJ):
                    act.wait_ge(pe_dt.sem, pe_dt.at(c, j + 1))
                    activate(sp_exp[:, j, :], pa[:, (j + 1) % 3, 0:T], ACT.Abs, bias=col("dt_b", j))\
                        .then_inc(v_abs.sem, 1)
                act.wait_ge(v_abs.sem, v_abs.at(c, NJ))
                activate(sp_exp[:, :, :], sp_exp[:, :, :], ACT.Exp, scale=-1.0).then_inc(exp_ready.sem, 1)

            def broadcast(c, _):
                for k, tile in enumerate((b_all, c_all)):
                    act.wait_ge(pe_bc.sem, pe_bc.at(c, k + 1))
                    activate(tile[:, :], pa[:, 1 + k, 0:T], ACT.Copy).then_inc(bc_ready.sem, 1)

            def split(c, j):
                act.wait_ge(poly.sem, poly.at(c, POLY_STEPS * (j + 1)))
                activate(dt_rows[0:P // 2, j, 0, :], dt[0:P // 2, j, :], ACT.Copy)
                activate(dt_rows[P // 2:P, j, 1, :], dt[P // 2:P, j, :], ACT.Copy).then_inc(dt_high.sem, 1)
                act.wait_ge(u_ready.sem, u_ready.at(c, j + 1))
                activate(u_rows[0:P // 2, j, 0, :], u[0:P // 2, j, :], ACT.Copy)
                activate(u_rows[P // 2:P, j, 1, :], u[P // 2:P, j, :], ACT.Copy).then_inc(u_high.sem, 1)

            def decay_step(c, i):
                if not after_first(c) and i == 0:
                    act.wait_ge(constants.sem, 1)
                    act.wait_ge(decay_ready.sem, 1)
                if i >= 2:
                    act.wait_ge(scanned.sem, scanned.at(c, i - 1))
                for k in range(2):
                    j, q, b = scan_slot(i, k)
                    group = GROUPS_PER_BLOCK * j + 4 * b + q
                    act.wait_ge(pe_dt_all.sem, pe_dt_all.at(c, 2 * i + k + 1))
                    activate(over_images(a_bar[:, i % 2, k * T:(k + 1) * T]), over_images(pa[:, k, 0:T]), ACT.Exp,
                             scale=decay[:, group:group + 1]).then_inc(decayed.sem, 1)

            def split_w1(n):
                e, half = divmod(n, 2)
                cols = slice(half * HALF, (half + 1) * HALF)
                act.wait_ge(w1_raw_in[n % 3].sem, 16 * (n // 3 + 1))
                if e >= 2:
                    act.wait_ge(w1_stored[e % 2].sem, 16 * (e // 2))
                activate(w1[:, e % 2, 0, cols], w1_raw[:, n % 3, 0, :], ACT.Copy)
                activate(w1[:, e % 2, 2, cols], w1_raw[:, n % 3, 1, :], ACT.Copy).then_inc(w1_high_done.sem, 1)

            def variance2(c, _):
                act.wait_ge(y1_ready.sem, y1_ready.at(c, 2))
                activate(squares[:, :, :], y1[:, :, :], ACT.Square).then_inc(squared.sem, 1)

            def ffn_gate_tanh(c, k):
                act.wait_ge(pe_ffn.sem, pe_ffn.at(c, 2 * k + 1))
                if k >= 2:
                    act.wait_ge(ffn_gated.sem, ffn_gated.at(c, k - 1))
                activate(gate_tanh[:, k % 2, :], pa[:, (2 * k) % 3, 0:T], ACT.Tanh, scale=0.5).then_inc(ffn_tanh.sem, 1)

            def center3(c, _):
                act.wait_ge(is_centered.sem, is_centered.at(c, 2))
                activate(squares[:, :, :], centered[:, :, :], ACT.Square).then_inc(squared.sem, 1)

            def scale3(c, _):
                if after_first(c):
                    act.wait_ge(pe_linear.sem, pe_linear.at(c - 1, UNITS))
                act.wait_ge(t_ready.sem, t_ready.at(c, 2))
                activate(t_high[:, :, :], t_in[:, :, :], ACT.Copy).then_inc(t_high_ready.sem, 1)

            def topk(c, _):
                act.wait_ge(route_steps.sem, route_steps.at(c, 6))
                activate(route[:, :, :], route[:, :, :], ACT.Exp).then_inc(route_exp.sem, 1)

            def weights(c, _):
                act.wait_ge(pe_mix.sem, pe_mix.at(c, 1))
                activate(mix_w[:, :], pa[0:EXPERTS, 0, 0:T], ACT.Copy).then_inc(mix_copied.sem, 1)
                if after_first(c):
                    act.wait_ge(pe_weight.sem, pe_weight.at(c - 1, UNITS))
                act.wait_ge(mix_copied.sem, mix_copied.at(c, 1))
                activate(mix_parts[0:EXPERTS, :], mix_w[:, :], ACT.Copy).then_inc(mix_high.sem, 1)

            def experts_gate(c, un):
                act.wait_ge(pe_gate.sem, pe_gate.at(c, un + 1))
                if un:
                    act.wait_ge(gate_min.sem, gate_min.at(c, un))
                activate(g_raw, pb[:, GATE, 0:T], ACT.Identity, bias=col("b1_gate", un)).then_inc(gate_copied.sem, 1)

            def experts_linear(c, un):
                act.wait_ge(pe_linear.sem, pe_linear.at(c, un + 1))
                if un:
                    act.wait_ge(linear_clip.sem, linear_clip.at(c, un))
                activate(l_raw, pb[:, LINEAR, 0:T], ACT.Identity, bias=col("b1_linear", un))\
                    .then_inc(linear_copied.sem, 1)

            def experts_mix(c, un):
                act.wait_ge(gate_min.sem, gate_min.at(c, un + 1))
                if un:
                    act.wait_ge(gate_act.sem, gate_act.at(c, un))
                activate(g_tanh, g_min[un % 2], ACT.Tanh, scale=ALPHA / 2).then_inc(g_tanh_ready.sem, 1)

            act.wait_ge(load_ssm.sem, 16 * len(SSM_LOADS))
            activate(decay[:, :], decay[:, :], ACT.Exp).then_inc(decay_exp.sem, 1)
            act.wait_ge(load_embed.sem, 16 * len(EMBED_LOADS))
            run(act, {
                "embed": embed, "center": center, "inproj": inproj, "xproj": xproj, "delta": delta,
                "broadcast": broadcast, "split": split, "split_w1": split_w1,
                "scan": decay_step,
                "variance2": variance2, "ffn": ffn_gate_tanh, "center3": center3, "scale3": scale3,
                "topk": topk, "weights": weights, "experts_gate": experts_gate,
                "experts_linear": experts_linear, "experts_mix": experts_mix})

        @block.vector
        def _(dve):
            def center(c, _):
                dve.wait_ge(embedded.sem, embedded.at(c, 2))
                dve.wait_ge(pe_mean.sem, pe_mean.at(c, 1))
                dve.tensor_tensor(centered[:, :, :], h0[:, :, :], twice(pa[:, 2, 0:T]), ALU.subtract)\
                    .then_inc(is_centered.sem, 1)

            def roots(c, n, bank, ln_eps, rms_eps):
                step = ROOT_STEPS * (n - 1)
                x, r, s, bits = root[:, 0, :], root[:, 1, :], root[:, 2, :], root[:, 3, :].bitcast(I32)
                v = pa[0:RT, bank, 0:3]
                dve.wait_ge(pe_var.sem, pe_var.at(c, n))
                dve.tensor_scalar(x[:, 0:3], v, ln_eps, None, ALU.add)
                dve.tensor_scalar(x[:, 3:6], v, 1.0 + rms_eps, ln_eps * rms_eps, ALU.mult, ALU.add)\
                    .then_inc(root_steps.sem, 1)
                dve.wait_ge(root_steps.sem, root_steps.at(c, step + 1))
                dve.tensor_scalar(bits, x.bitcast(I32), 1, None, ALU.arith_shift_right).then_inc(root_steps.sem, 1)
                dve.wait_ge(root_steps.sem, root_steps.at(c, step + 2))
                dve.tensor_scalar(r.bitcast(I32), bits, -1.0, ROOT_GUESS, ALU.mult, ALU.add)\
                    .then_inc(root_steps.sem, 1)
                for k in range(3):
                    dve.wait_ge(root_steps.sem, root_steps.at(c, step + 3 * k + 3))
                    dve.scalar_tensor_tensor(s, r, -0.5, r, ALU.mult, ALU.mult).then_inc(root_steps.sem, 1)
                    dve.wait_ge(root_steps.sem, root_steps.at(c, step + 3 * k + 4))
                    dve.tensor_tensor(s, s, x, ALU.mult).then_inc(root_steps.sem, 1)
                    dve.wait_ge(root_steps.sem, root_steps.at(c, step + 3 * k + 5))
                    dve.scalar_tensor_tensor(r, s, 1.5, r, ALU.add, ALU.mult).then_inc(root_steps.sem, 1)
                dve.wait_ge(root_steps.sem, root_steps.at(c, step + 12))
                dve.tensor_tensor(diag[:, :, :], ident[0:RT, 0:RT].unsqueeze(1).to_broadcast([RT, 6, RT]),
                                  r.unsqueeze(2).to_broadcast([RT, 6, RT]), ALU.mult).then_inc(root_steps.sem, 1)

            def variance(c, _):
                roots(c, 1, 2, 1e-5, 1e-6)

            def scale(c, _):
                dve.wait_ge(pe_root.sem, pe_root.at(c, 1))
                dve.tensor_tensor(y1[:, :, :], centered[:, :, :], twice(pa[:, 0, 0:T]), ALU.mult)\
                    .then_inc(y1_ready.sem, 1)
                for m in range(2):
                    dve.scalar_tensor_tensor(normed[:, m, :], centered[:, m, :], col("norm1", m),
                                             pa[:, 1, 0:T], ALU.mult, ALU.mult).then_inc(norm_ready.sem, 1)

            def inproj(c, j):
                dve.wait_ge(tanh_ready.sem, tanh_ready.at(c, j + 1))
                dve.scalar_tensor_tensor(z[:, j, :], gate_tanh[:, j % 2, :], 1.0, pa[:, (2 * j) % 3, 0:T],
                                         ALU.add, ALU.mult).then_inc(z_ready.sem, 1)

            def xproj(c, _):
                dve.wait_ge(pe_xproj.sem, pe_xproj.at(c, 1))
                dve.tensor_copy(bc[:, :], pa[DT_RANK:P, 0, 0:T]).then_inc(bc_copied.sem, 1)
                dve.wait_ge(bc_high.sem, bc_high.at(c, 1))
                dve.wait_ge(bc_copied.sem, bc_copied.at(c, 1))
                dve.tensor_tensor(bc_parts[32:64, :], bc[:, :], bc_parts[0:32, :].bitcast(F32), ALU.subtract)\
                    .then_inc(bc_low.sem, 1)

            def delta(c, _):
                for j in range(NJ):
                    dve.wait_ge(v_abs.sem, v_abs.at(c, j + 1))
                    dve.tensor_scalar(u[:, j, :], pa[:, (j + 1) % 3, 0:T], col("dt_b", j), 0.0,
                                      ALU.add, ALU.max).then_inc(v_max.sem, 1)

            def log1p(c, j):
                done = POLY_STEPS * j
                if j == 0:
                    dve.wait_ge(exp_ready.sem, exp_ready.at(c, 1))
                    dve.wait_ge(v_max.sem, v_max.at(c, NJ))
                dve.tensor_scalar(dt[:, j, :], sp_exp[:, j, :], LOG1P[-1], None, ALU.mult).then_inc(poly.sem, 1)
                for n, coefficient in enumerate(LOG1P[-2::-1]):
                    dve.wait_ge(poly.sem, poly.at(c, done + n + 1))
                    dve.scalar_tensor_tensor(dt[:, j, :], dt[:, j, :], coefficient, sp_exp[:, j, :],
                                             ALU.add, ALU.mult).then_inc(poly.sem, 1)
                dve.wait_ge(poly.sem, poly.at(c, done + POLY_STEPS - 1))
                dve.tensor_tensor(dt[:, j, :], dt[:, j, :], u[:, j, :], ALU.add).then_inc(poly.sem, 1)

            def split(c, j):
                dve.wait_ge(dt_high.sem, dt_high.at(c, j + 1))
                dve.tensor_tensor(dt_rows[P // 2:P, j, 0, :], dt[0:P // 2, j, :],
                                  dt_rows[0:P // 2, j, 0, :].bitcast(F32), ALU.subtract)
                dve.tensor_tensor(dt_rows[0:P // 2, j, 1, :], dt[P // 2:P, j, :],
                                  dt_rows[P // 2:P, j, 1, :].bitcast(F32), ALU.subtract).then_inc(dt_low.sem, 1)

            def drive(c, i):
                if i == 0:
                    dve.wait_ge(bc_ready.sem, bc_ready.at(c, 1))
                dve.wait_ge(pe_u_all.sem, pe_u_all.at(c, i + 1))
                dve.tensor_tensor(b_x[:, i % 2, :].rearrange("p (k t) -> p k t", k=2), twice(b_all[:, :]),
                                  pb[:, 0:2, 0:T], ALU.mult).then_inc(bx_ready.sem, 1)

            def advance(c, i):
                dve.wait_ge(decayed.sem, decayed.at(c, 2 * i + 2))
                dve.wait_ge(bx_ready.sem, bx_ready.at(c, i + 1))
                if i >= 2:
                    dve.wait_ge(read_out.sem, read_out.at(c, i - 1))
                dve.tensor_tensor_scan(state[:, i % 2, :], a_bar[:, i % 2, :], b_x[:, i % 2, :], 0.0,
                                       ALU.mult, ALU.add).then_inc(scanned.sem, 1)

            def collect(c, i):
                j, r = divmod(i, STEPS_PER_BLOCK)
                if r == STEPS_PER_BLOCK - 1:
                    dve.wait_ge(pe_y.sem, pe_y.at(c, i + 1))
                    dve.scalar_tensor_tensor(y[:, j, :], z[:, j, :], col("skip", j), pa[:, 2, 0:T],
                                             ALU.mult, ALU.add).then_inc(y_ready.sem, 1)

            def outproj(c, _):
                dve.wait_ge(pe_out.sem, pe_out.at(c, 1))
                dve.tensor_tensor(y1[:, :, :], y1[:, :, :], pa[:, 0:2, 0:T], ALU.add).then_inc(y1_ready.sem, 1)

            def variance2(c, _):
                roots(c, 2, 2, 1e-6, 0.0)

            def scale2(c, _):
                dve.wait_ge(pe_root.sem, pe_root.at(c, 2))
                for m in range(2):
                    dve.scalar_tensor_tensor(normed[:, m, :], y1[:, m, :], col("norm2", m), pa[:, 0, 0:T],
                                             ALU.mult, ALU.mult).then_inc(norm_ready.sem, 1)

            def ffn_product(c, k):
                dve.wait_ge(ffn_tanh.sem, ffn_tanh.at(c, k + 1))
                if k:
                    dve.wait_ge(ffn_ready.sem, ffn_ready.at(c, k))
                dve.scalar_tensor_tensor(ffn_gate[:, :], gate_tanh[:, k % 2, :], 1.0, pa[:, (2 * k) % 3, 0:T],
                                         ALU.add, ALU.mult).then_inc(ffn_gated.sem, 1)
                dve.wait_ge(ffn_gated.sem, ffn_gated.at(c, k + 1))
                dve.wait_ge(pe_ffn.sem, pe_ffn.at(c, 2 * k + 2))
                dve.scalar_tensor_tensor(ffn[:, k, :], ffn_gate[:, :], 0.5, pa[:, (2 * k + 1) % 3, 0:T],
                                         ALU.mult, ALU.mult)\
                    .then_inc(ffn_ready.sem, 1)

            def down(c, _):
                dve.wait_ge(pe_down.sem, pe_down.at(c, 1))
                dve.tensor_tensor(y1[:, :, :], y1[:, :, :], pa[:, 1:3, 0:T], ALU.add).then_inc(y1_ready.sem, 1)
                dve.wait_ge(y1_ready.sem, y1_ready.at(c, 3))
                dve.tensor_tensor(h0[:, :, :], h0[:, :, :], y1[:, :, :], ALU.add).then_inc(h1_ready.sem, 1)

            def center3(c, _):
                dve.wait_ge(h1_ready.sem, h1_ready.at(c, 1))
                dve.wait_ge(pe_mean.sem, pe_mean.at(c, 2))
                dve.tensor_tensor(centered[:, :, :], h0[:, :, :], twice(pa[:, 0, 0:T]), ALU.subtract)\
                    .then_inc(is_centered.sem, 1)

            def variance3(c, _):
                roots(c, 3, 1, 1e-5, 1e-5)

            def scale3(c, _):
                dve.wait_ge(pe_root.sem, pe_root.at(c, 3))
                for m in range(2):
                    dve.scalar_tensor_tensor(t_in[:, m, :], centered[:, m, :], col("norm3", m),
                                             pa[:, 2, 0:T], ALU.mult, ALU.mult).then_inc(t_ready.sem, 1)
                dve.tensor_tensor(base[:, :, :], centered[:, :, :], twice(pa[:, 0, 0:T]), ALU.mult)\
                    .then_inc(base_ready.sem, 1)
                dve.wait_ge(t_high_ready.sem, t_high_ready.at(c, 1))
                dve.wait_ge(t_ready.sem, t_ready.at(c, 2))
                dve.tensor_tensor(t_low[:, :, :], t_in[:, :, :], t_high[:, :, :].bitcast(F32), ALU.subtract)\
                    .then_inc(t_low_ready.sem, 1)

            def topk(c, _):
                E = EXPERTS
                dve.wait_ge(pe_logits.sem, pe_logits.at(c, 1))
                dve.tensor_copy(logits[:, :, 0:E], pa[0:RT, 2, 0:3 * E].rearrange("p (i e) -> p i e", i=3))\
                    .then_inc(route_steps.sem, 1)
                dve.wait_ge(route_steps.sem, route_steps.at(c, 1))
                dve.memset(after_wait[:, :], 0.0)
                for i in range(3):
                    last = dve.max(top8[:, i, :], logits[:, i, 0:E])
                last.then_inc(route_steps.sem, 1)
                dve.wait_ge(route_steps.sem, route_steps.at(c, 2))
                dve.tensor_copy(top4[:, :, 0:TOP_K], top8[:, :, 0:TOP_K]).then_inc(route_steps.sem, 1)
                dve.wait_ge(route_steps.sem, route_steps.at(c, 3))
                dve.memset(after_wait[:, :], 0.0)
                for i in range(3):
                    last = dve.match_replace(replaced[:, i, :], top4[:, i, :], logits[:, i, :], -PAD_LOGIT)
                last.then_inc(route_steps.sem, 1)
                dve.wait_ge(route_steps.sem, route_steps.at(c, 4))
                dve.tensor_tensor(chosen[:, :, :], replaced[:, :, 0:E], logits[:, :, 0:E], ALU.not_equal)\
                    .then_inc(route_steps.sem, 1)
                dve.tensor_tensor(route[:, :, :], logits[:, :, 0:E],
                                  top8[:, :, 0:1].to_broadcast([RT, 3, E]), ALU.subtract)\
                    .then_inc(route_steps.sem, 1)
                dve.wait_ge(route_steps.sem, route_steps.at(c, 5))
                dve.wait_ge(route_exp.sem, route_exp.at(c, 1))
                dve.tensor_tensor(route[:, :, :], route[:, :, :], chosen[:, :, :], ALU.mult)\
                    .then_inc(route_steps.sem, 1)
                dve.wait_ge(route_steps.sem, route_steps.at(c, 7))
                dve.reduce_sum(route_sum[:, 0, :], route[:, :, :], AX.X).then_inc(route_steps.sem, 1)
                dve.wait_ge(route_steps.sem, route_steps.at(c, 8))
                dve.reciprocal(route_sum[:, 1, :], route_sum[:, 0, :]).then_inc(route_steps.sem, 1)
                dve.wait_ge(route_steps.sem, route_steps.at(c, 9))
                dve.tensor_tensor(route[:, :, :], route[:, :, :],
                                  route_sum[:, 1, :].unsqueeze(2).to_broadcast([RT, 3, E]), ALU.mult)\
                    .then_inc(route_steps.sem, 1)
                if after_first(c):
                    dve.wait_ge(stored.sem, stored.at(c - 1, 2))

            def weights(c, _):
                dve.wait_ge(mix_high.sem, mix_high.at(c, 1))
                dve.tensor_tensor(mix_parts[32:32 + EXPERTS, :], mix_w[:, :], mix_parts[0:EXPERTS, :].bitcast(F32),
                                  ALU.subtract).then_inc(mix_low.sem, 1)

            def experts_gate(c, un):
                dve.wait_ge(gate_copied.sem, gate_copied.at(c, un + 1))
                if un >= 2:
                    dve.wait_ge(gate_act.sem, gate_act.at(c, un - 1))
                dve.tensor_scalar(g_min[un % 2], g_raw, LIMIT, None, ALU.min).then_inc(gate_min.sem, 1)

            def experts_linear(c, un):
                dve.wait_ge(linear_copied.sem, linear_copied.at(c, un + 1))
                if un >= 2:
                    dve.wait_ge(glu_ready.sem, glu_ready.at(c, un - 1))
                dve.tensor_scalar(l_clip[un % 2], l_raw, 1.0 + LIMIT, 1.0 - LIMIT, ALU.min, ALU.max)\
                    .then_inc(linear_clip.sem, 1)

            def experts_mix(c, un):
                dve.wait_ge(g_tanh_ready.sem, g_tanh_ready.at(c, un + 1))
                if un:
                    dve.wait_ge(glu_ready.sem, glu_ready.at(c, un))
                dve.scalar_tensor_tensor(g_act, g_tanh, 1.0, g_min[un % 2], ALU.add, ALU.mult)\
                    .then_inc(gate_act.sem, 1)

            def experts_scale(c, un):
                dve.wait_ge(glu_ready.sem, glu_ready.at(c, un + 1))
                dve.wait_ge(pe_weight.sem, pe_weight.at(c, un + 1))
                if un >= 4:
                    dve.wait_ge(pe_hid.sem, pe_hid.at(c, (un - 4) // 2 + 1))
                dve.tensor_tensor(hid[:, un % 4, :], glu, pb[:, WEIGHT, 0:T], ALU.mult).then_inc(hid_ready.sem, 1)

            def experts_finish(c, _):
                dve.wait_ge(base_ready.sem, base_ready.at(c, 2))
                dve.wait_ge(pe_hid.sem, pe_hid.at(c, UNITS // 2))
                dve.tensor_tensor(result[:, 0, :], base[:, 0, :], pb[:, SUM, 0:T], ALU.add)\
                    .then_inc(result_part.sem, 1)
                dve.tensor_tensor(result[0:REST, 1, :], base[0:REST, 1, :], pb[0:REST, SUM_REST, 0:T], ALU.add)\
                    .then_inc(result_part.sem, 1)
                dve.wait_ge(result_part.sem, result_part.at(c, 2))
                dve.tensor_tensor(result[0:REST, 1, :], result[0:REST, 1, :], pb[REST:P, SUM_REST, 0:T], ALU.add)\
                    .then_inc(result_part.sem, 1)

            dve.wait_ge(load_embed.sem, 16 * len(EMBED_LOADS))
            dve.wait_ge(constants.sem, 1)
            run(dve, {
                "center": center, "variance": variance, "scale": scale, "inproj": inproj, "xproj": xproj,
                "delta": delta, "log1p": log1p, "split": split, "scan": drive, "weights": weights,
                "advance": advance, "collect": collect, "outproj": outproj, "variance2": variance2,
                "scale2": scale2, "ffn": ffn_product, "down": down, "center3": center3,
                "variance3": variance3, "scale3": scale3, "topk": topk, "experts_gate": experts_gate,
                "experts_linear": experts_linear, "experts_mix": experts_mix,
                "experts_scale": experts_scale, "experts_finish": experts_finish})

        @block.gpsimd
        def _(pool):
            def split_w1(n):
                e, half = divmod(n, 2)
                cols = slice(half * HALF, (half + 1) * HALF)
                pool.wait_ge(w1_high_done.sem, n + 1)
                pool.tensor_tensor(w1[:, e % 2, 1, cols], w1_raw[:, n % 3, 0, :],
                                   w1[:, e % 2, 0, cols].bitcast(F32), ALU.subtract).then_inc(w1_low_done.sem, 1)
                pool.wait_ge(w1_low_done.sem, 2 * n + 1)
                low = w1[REST:P, e % 2, 2, cols]
                pool.tensor_tensor(low, w1_raw[REST:P, n % 3, 1, :], low.bitcast(F32), ALU.subtract)\
                    .then_inc(w1_low_done.sem, 1)
                pool.wait_ge(w1_low_done.sem, 2 * n + 2)

            def split(c, j):
                pool.wait_ge(poly.sem, poly.at(c, POLY_STEPS * (j + 1)))
                pool.tensor_tensor(u[:, j, :], dt[:, j, :], z[:, j, :], ALU.mult).then_inc(u_ready.sem, 1)
                pool.wait_ge(u_ready.sem, u_ready.at(c, j + 1))
                pool.wait_ge(u_high.sem, u_high.at(c, j + 1))
                pool.tensor_tensor(u_rows[P // 2:P, j, 0, :], u[0:P // 2, j, :],
                                   u_rows[0:P // 2, j, 0, :].bitcast(F32), ALU.subtract).then_inc(u_low.sem, 1)
                pool.wait_ge(u_low.sem, u_low.at(c, 2 * j + 1))
                pool.tensor_tensor(u_rows[0:P // 2, j, 1, :], u[P // 2:P, j, :],
                                   u_rows[P // 2:P, j, 1, :].bitcast(F32), ALU.subtract).then_inc(u_low.sem, 1)
                pool.wait_ge(u_low.sem, u_low.at(c, 2 * j + 2))

            def advance(c, i):
                if i == 0:
                    pool.wait_ge(bc_ready.sem, bc_ready.at(c, 2))
                pool.wait_ge(scanned.sem, scanned.at(c, i + 1))
                if i >= 2:
                    pool.wait_ge(pe_y.sem, pe_y.at(c, i - 1))
                pool.tensor_tensor(read[:, i % 2, :].rearrange("p (k t) -> p k t", k=2),
                                   state[:, i % 2, :].rearrange("p (k t) -> p k t", k=2),
                                   twice(c_all[:, :]), ALU.mult).then_inc(read_out.sem, 1)

            def scale3(c, _):
                pool.wait_ge(base_ready.sem, base_ready.at(c, 1))
                pool.tensor_tensor(base[:, :, :], base[:, :, :], h0[:, :, :], ALU.add).then_inc(base_ready.sem, 1)

            def experts_mix(c, un):
                pool.wait_ge(gate_act.sem, gate_act.at(c, un + 1))
                pool.wait_ge(linear_clip.sem, linear_clip.at(c, un + 1))
                if un:
                    pool.wait_ge(hid_ready.sem, hid_ready.at(c, un))
                pool.tensor_tensor(glu, g_act, l_clip[un % 2], ALU.mult).then_inc(glu_ready.sem, 1)

            pool.memset(ones[:, :], 1.0)
            pool.memset(a_bar[:, :, :], 0.0)
            pool.memset(mix_parts[:, :].bitcast(F32), 0.0)
            pool.memset(logits[:, :, EXPERTS:EXPERTS + 4], PAD_LOGIT)
            pool.memset(top4[:, :, TOP_K:8], PAD_LOGIT).then_inc(constants.sem, 1)
            pool.wait_ge(constants.sem, 1)
            pool.wait_ge(load_ssm.sem, 16 * len(SSM_LOADS))
            pool.tensor_scalar(w_in[:, 0, :], w_in[:, 0, :], 0.5, None, ALU.mult)
            pool.tensor_scalar(w_in_rest[:, 0, :], w_in_rest[:, 0, :], 0.5, None, ALU.mult)\
                .then_inc(in_halved.sem, 1)
            pool.wait_ge(decay_exp.sem, 1)
            pool.tensor_scalar(decay[:, :], decay[:, :], -1.0, None, ALU.mult).then_inc(decay_ready.sem, 1)

            pool.tensor_scalar(pick_state[:, :, :], raw_state, 1.0, None, ALU.mult)
            pool.tensor_scalar(pick_group[:, :, :], raw_group, 1.0, None, ALU.mult)\
                .then_inc(picks_rounded.sem, 1)
            pool.wait_ge(load_late.sem, 16 * len(LATE_LOADS))
            for k in range(3):
                rounded = pool.tensor_scalar(pick_unit[:, 8 * k:8 * (k + 1), :], raw_unit[k], 1.0, None, ALU.mult)
            rounded.then_inc(picks_rounded.sem, 1)
            linear = vec[:, at["b1_linear"]:at["b1_linear"] + UNITS]
            pool.tensor_scalar(linear, linear, 1.0, None, ALU.add).then_inc(bias_raised.sem, 1)
            run(pool, {"split_w1": split_w1, "split": split, "advance": advance, "scale3": scale3,
                       "experts_mix": experts_mix})


def _twice(w):
    return np.concatenate([w, w[..., P:HIDDEN]], axis=-1)


def _tiles(w, n):
    return w.reshape(n, P, -1).transpose(1, 0, 2)


def _picks():
    unit = np.zeros((MIX_ROWS, UNITS, P), np.float32)
    group = np.zeros((P, 2 * 4, P), np.float32)
    state = np.zeros((2 * 32, 2, P), np.float32)
    total = np.zeros((P, 4, 32), np.float32)
    col = np.arange(P)
    for part in range(2):
        for un in range(UNITS):
            pair, k = divmod(un, 3)
            expert = 2 * pair + (k if k < 2 else col // REST)
            unit[32 * part + expert, un, col] = 0.5
        for q in range(8):
            group[64 * part + D8 * q + col // STATES, q, col] = 1
        for k in range(2):
            state[32 * part + STATES * k + col % STATES, k, col] = 1
    for q in range(4):
        total[col, q, D8 * q + col // STATES] = 1
    return unit, group, state, total


def _layout(i):
    x = i["x"].reshape(IMAGES, 3, 6, 16, 6, 16).transpose(0, 1, 2, 4, 3, 5).reshape(IMAGES * TOKENS_PER_IMAGE, PATCH_DIM)
    a = {"patches": x.T.reshape(KP, P, CHUNKS, T).transpose(2, 1, 0, 3)}
    a["embed_w"] = _tiles(_twice(i["L0_tok_W"].T), KP)
    w_in = np.stack([i["L0_attn_W_in"].T, i["L0_attn_W_gate"].T], axis=1)
    a["in_w"], a["in_w_rest"] = w_in[:P], w_in[P:]
    a["xproj_w"] = _tiles(i["L0_attn_W_xproj"].T, NJ)
    a["dt_w"] = i["L0_attn_W_dt"].T
    a["out_w"] = _tiles(_twice(i["L0_attn_W_out"].T), NJ)
    w_ffn = np.stack([i["L0_attn_W_gate_ffn"].T, i["L0_attn_W_up"].T], axis=1)
    a["ffn_w"], a["ffn_w_rest"] = w_ffn[:P], w_ffn[P:]
    a["ffn_down"] = _tiles(_twice(i["L0_attn_W_down"].T), NF)
    gate = i["L0_ffn_gate_w"].T
    a["router_w"], a["router_w_rest"] = gate[:P], gate[P:]
    a["router_b"] = i["L0_ffn_gate_b"][None]
    w1, b1, w2 = i["L0_ffn_w1"], i["L0_ffn_b1"][:, None], i["L0_ffn_w2"]
    I = EXPERT_DIM

    def units(w):
        w = w.reshape(PAIRS, 2, w.shape[1], 2, I).transpose(0, 2, 3, 1, 4)
        rest = w[..., P:].reshape(*w.shape[:3], 1, P)
        return np.concatenate([w[..., :P], rest], axis=3).transpose(0, 1, 3, 2, 4)

    w1 = units(w1).reshape(PAIRS, HIDDEN, PAIR_COLS)
    a["expert_w1"] = np.stack([w1[:, :P], np.concatenate([w1[:, P:], w1[:, P:]], axis=1)], axis=2)
    b1 = units(b1).reshape(UNITS, 2, P)
    w2 = w2.reshape(PAIRS, 2, I, HIDDEN)
    w2 = np.concatenate([w2[:, :, :P], w2[:, :, P:].reshape(PAIRS, 1, P, HIDDEN)], axis=1)
    a["expert_w2"] = w2.transpose(2, 0, 1, 3).reshape(P, UNITS, HIDDEN)
    a["expert_b2"] = i["L0_ffn_b2"]
    a["vectors"] = np.concatenate(
        [_twice(i[n]).reshape(2, P) for n in ("L0_tok_b", "L0_attn_w_norm1", "L0_attn_w_ffn_norm", "L0_ffn_scale")]
        + [i["L0_attn_b_dt"].reshape(NJ, P), i["L0_attn_D_skip"].reshape(NJ, P), b1[:, 0], b1[:, 1]]).T
    a["decay_log"] = i["L0_attn_A_log"].reshape(NJ * GROUPS_PER_BLOCK, P).T
    a["unit_pick"], a["group_pick"], a["state_pick"], a["channel_sum"] = _picks()
    a["ones_mean"] = np.full((P, P), 1 / HIDDEN, np.float32)
    a["identity"] = np.eye(P, dtype=np.float32)
    return a


def kernel(**inputs):
    import concourse.bacc as _bacc
    from concourse.bass_utils import run_bass_kernel_spmd as _run

    nc = _bacc.Bacc("TRN2", target_bir_lowering=False, num_devices=1)
    arrays, args = {}, {}
    for name, a in _layout({k: np.asarray(v) for k, v in inputs.items()}).items():
        a = np.ascontiguousarray(a)
        arrays[name] = a
        args[name] = nc.dram_tensor(name, a.shape, mybir.dt.from_np(a.dtype), kind="ExternalInput").ap()
    args["out_main"] = nc.dram_tensor("out_main", (CHUNKS, P, T), F32, kind="ExternalOutput").ap()
    args["out_rest"] = nc.dram_tensor("out_rest", (CHUNKS, REST, T), F32, kind="ExternalOutput").ap()
    vit_tower(nc, **args)
    r = _run(nc, [arrays], core_ids=[0]).results[0]
    features = np.concatenate([r["out_main"], r["out_rest"]], axis=1)
    return features.transpose(0, 2, 1).reshape(IMAGES, TOKENS_PER_IMAGE, HIDDEN)
```

```python
from contextlib import ExitStack

import numpy as np

import concourse.bass as bass
import concourse.mybir as mybir

F32 = mybir.dt.float32
F32R = mybir.dt.float32r
ALU = mybir.AluOpType
ACT = mybir.ActivationFunctionType
AX = mybir.AxisListType

P = 128
IMAGES, TOKENS_PER_IMAGE = 32, 36
CHUNK_IMAGES = 8
CHUNKS = IMAGES // CHUNK_IMAGES
T = CHUNK_IMAGES * TOKENS_PER_IMAGE
PATCH_DIM, HIDDEN, INNER, STATES, DT_RANK, FFN_DIM = 768, 192, 384, 16, 96, 512
REST = HIDDEN - P
EXPERTS, TOP_K, EXPERT_DIM = 16, 4, 192
KP = PATCH_DIM // P
NJ = INNER // P
NF = FFN_DIM // P
D8 = P // STATES
GROUPS_PER_BLOCK = P // D8
PAIRS = EXPERTS // 2
UNITS = 3 * PAIRS
PAIR_COLS = 6 * P
STEPS_PER_BLOCK = GROUPS_PER_BLOCK // 2
SCAN_STEPS = NJ * STEPS_PER_BLOCK
RT = T // 3
LIMIT, ALPHA = 7.0, 1.702
HID_TILES = 12
PAD_LOGIT = -3.0e38
MIX_ROWS = 32 + EXPERTS
DOWNS = 3 * (UNITS // 2)

LOG1P = ((-2.3294668197631836, 0.4346165060997009), (1.0091787576675415, 1.1116931438446045),
         (-1.430558443069458, 2.7158021926879883), (-0.08503787219524384, 3.2738332748413086))
LOG1P_SCALE = 0.005126102039759846
FACTORS = len(LOG1P)
POLY_STEPS = FACTORS + 1
ROOT_STEPS = 2


class Signal:

    def __init__(self, semaphore, per_chunk, unit=1):
        self.sem, self.per_chunk, self.unit = semaphore, per_chunk, unit

    def at(self, chunk, k):
        return (chunk * self.per_chunk + k) * self.unit


def after_first(chunk):
    return not isinstance(chunk, int)


def schedule():
    pre = [("embed", 0), ("center", 0), ("variance", 0), ("scale", 0)]
    pre += [("inproj", j) for j in range(NJ)]
    pre += [("xproj", 0), ("delta", 0), ("broadcast", 0)]
    pre += [("square", k) for k in range(FACTORS)] + [("log1p", 0), ("split", 0)]
    post = [("outproj", 0), ("variance2", 0), ("scale2", 0)] + [("ffn", k) for k in range(NF)]
    post += [("down", 0), ("center3", 0), ("variance3", 0), ("scale3", 0)]
    scan = []
    for i in range(SCAN_STEPS):
        j, r = divmod(i, STEPS_PER_BLOCK)
        if j + 1 < NJ:
            if r < FACTORS:
                scan.append(("square", FACTORS * (j + 1) + r))
            if r == 4:
                scan.append(("log1p", j + 1))
            if r == 6:
                scan.append(("split", j + 1))
        scan += [("scan", i), ("decay", i)]
        if i >= 1:
            scan.append(("advance", i - 1))
        if i >= 3:
            scan.append(("collect", i - 3))
    scan += [("collect", SCAN_STEPS - 3), ("advance", SCAN_STEPS - 1), ("collect", SCAN_STEPS - 2),
             ("collect", SCAN_STEPS - 1)]

    pieces = [[("topk", 0)], [("weights", 0)], [("start", 0)]]
    for u in range(UNITS):
        pieces.append([("gate", u)] + ([("scale", u - 1)] if u else []))
        pieces.append([("linear", u), ("mix", u)])
    pieces.append([("scale", UNITS - 1)])
    out, half, scaled, downs, after_scan = [], 0, -1, 0, False

    def down():
        if downs < DOWNS and 2 * (downs // 3) + 1 <= scaled:
            out.append(("B", "down", downs))
            return downs + 1
        return downs

    for s in pre + scan + post:
        last = s == ("scale3", 0)
        for _ in range(min(len(pieces), len(pieces) if last else PIECES_BEFORE.get(s, 0))):
            piece = pieces.pop(0)
            scaled = max([scaled] + [u for step, u in piece if step == "scale"])
            while scaled >= 2 * (downs // 3) + HID_TILES:
                downs = down()
            out += [("B",) + p for p in piece]
            if after_scan and piece[0][0] == "linear":
                downs = down()
                downs = down()
        for _ in range(DOWNS if last else DOWNS_BEFORE.get(s, 0)):
            downs = down()
        if last:
            out.append(("B", "finish", 0))
        if s in SPLIT_BEFORE:
            out.append(("prologue", "split_w1", half))
            half += 1
        if s == ("scan", 0):
            after_scan = True
        out.append(("A",) + s)
    assert half == 2 * PAIRS and downs == DOWNS
    return out


PIECES_BEFORE = {("embed", 0): 1, ("center", 0): 1, ("variance", 0): 5, ("scale", 0): 2, ("inproj", 0): 2,
                 ("inproj", 1): 1, ("inproj", 2): 1, ("xproj", 0): 2, ("delta", 0): 2, ("broadcast", 0): 3,
                 ("split", 0): 4, ("scan", 0): 1, ("outproj", 0): 5, ("variance2", 0): 3, ("scale2", 0): 2,
                 ("ffn", 0): 1, ("ffn", 2): 1, ("down", 0): 3, ("center3", 0): 1, ("variance3", 0): 3}
DOWNS_BEFORE = {("scan", 3): 1, ("scan", 4): 1, ("scan", 5): 1, ("scan", 6): 1, ("scan", 7): 1, ("scan", 8):
                2, ("scan", 9): 1, ("scan", 11): 1, ("scan", 12): 1, ("scan", 13): 3, ("scan", 16): 1,
                ("scan", 17): 1, ("scan", 18): 1, ("scan", 19): 1, ("scan", 20): 1}
SPLIT_BEFORE = [("inproj", 1), ("inproj", 2), ("xproj", 0), ("delta", 0), ("scan", 1), ("scan", 7), ("scan",
                13), ("scan", 19), ("outproj", 0), ("scale2", 0), ("ffn", 0), ("ffn", 1), ("down", 0),
                ("center3", 0), ("variance3", 0), ("scale3", 0)]


def vit_tower(nc, patches, embed_w, in_w, in_w_rest, xproj_w, dt_w, out_w, ffn_w, ffn_w_rest,
              ffn_down, router_w, router_w_rest, router_b, expert_w1, expert_w2, expert_b2,
              vectors, decay_log, unit_pick, group_pick, state_pick, channel_sum, ones_mean,
              identity, out_main, out_rest):
    ORDER = schedule()
    UNITS_BEFORE_SCAN = sum(s[1] == "linear" for s in ORDER[:ORDER.index(("A", "scan", 0))])
    assert UNITS_BEFORE_SCAN == sum(s[1] == "gate" for s in ORDER[:ORDER.index(("A", "scan", 0))])
    with ExitStack() as ctx:
        def sb(name, shape, dt=F32):
            return ctx.enter_context(nc.sbuf_tensor(name, shape, dt))

        def signal(name, per_chunk, unit=1):
            return Signal(ctx.enter_context(nc.semaphore(name)), per_chunk, unit)

        w_embed = sb("w_embed", [P, KP, 2 * P])
        w_in = sb("w_in", [P, 2, INNER])
        w_in_rest = sb("w_in_rest", [REST, 2, INNER])
        w_xproj = sb("w_xproj", [P, NJ, P])
        w_dt = sb("w_dt", [DT_RANK, INNER])
        w_out = sb("w_out", [P, NJ, 2 * P])
        w_ffn = sb("w_ffn", [P, 2, FFN_DIM])
        w_ffn_rest = sb("w_ffn_rest", [REST, 2, FFN_DIM])
        w_down = sb("w_down", [P, NF, 2 * P])
        w_router = sb("w_router", [P, EXPERTS])
        w_router_rest = sb("w_router_rest", [REST, EXPERTS])
        b_router = sb("b_router", [1, EXPERTS])
        w2 = sb("w2", [P, UNITS, HIDDEN])
        b2 = sb("b2", [EXPERTS, HIDDEN])
        vec = sb("vec", [P, vectors.shape[1]])
        decay = sb("decay", [P, NJ * GROUPS_PER_BLOCK])
        pick_unit = sb("pick_unit", [MIX_ROWS, UNITS, P], F32R)
        pick_group = sb("pick_group", [P, 2 * 4, P], F32R)
        pick_state = sb("pick_state", [2 * 32, 2, P], F32R)
        sum_channel = sb("sum_channel", [P, 4, 32])
        mean_ones = sb("mean_ones", [P, P])
        ident = sb("ident", [P, P])
        ones = sb("ones", [RT, P])
        after_wait = sb("after_wait", [RT, 1])
        at, first = {}, 0
        for name, n in (("embed_b", 2), ("norm1", 2), ("norm2", 2), ("norm3", 2), ("dt_b", NJ),
                        ("skip", NJ), ("b1_gate", UNITS), ("b1_linear", UNITS)):
            at[name] = first
            first += n

        def col(name, k):
            return vec[:, at[name] + k:at[name] + k + 1]

        x_patch = sb("x_patch", [P, KP, T])
        h0 = sb("h0", [P, 2, T])
        centered = sb("centered", [P, 2, T])
        squares = sb("squares", [P, 2, T])
        normed = squares
        root = sb("root", [RT, 2, 6])
        minus_half = sb("minus_half", [RT, 6])
        diag = sb("diag", [RT, 6, RT])
        y1 = sb("y1", [P, 2, T])
        gate_tanh = sb("gate_tanh", [P, 2, T])
        z = sb("z", [P, NJ, T])
        dt_in = sb("dt_in", [DT_RANK, T])
        bc = sb("bc", [32, T])
        bc_parts = sb("bc_parts", [2 * 32, T], F32R)
        b_all = sb("b_all", [P, T])
        c_all = sb("c_all", [P, T])
        sp_exp = sb("sp_exp", [P, NJ, T])
        ffn = sb("ffn", [P, NF, T])
        factors = ffn
        shifts = sb("shifts", [P, FACTORS])
        dt = sb("dt", [P, NJ, T])
        u = sb("u", [P, NJ, T])
        y = sb("y", [P, NJ, T])
        dt_rows = sb("dt_rows", [P, NJ, 2, T], F32R)
        u_rows = sb("u_rows", [P, NJ, 2, T], F32R)
        a_bar = sb("a_bar", [P, 2, 2 * T])
        b_x = sb("b_x", [P, 3, 2 * T])
        state = sb("state", [P, 2, 2 * T])
        read = sb("read", [P, 2, 2 * T])
        ffn_gate = sb("ffn_gate", [P, T])
        t_in = sb("t_in", [P, 2, T])
        t_high = sb("t_high", [P, 2, T], F32R)
        t_low = sb("t_low", [P, 2, T], F32R)
        base = sb("base", [P, 2, T])
        logits = sb("logits", [RT, 3, EXPERTS + 4])
        replaced = sb("replaced", [RT, 3, EXPERTS + 4])
        top8 = sb("top8", [RT, 3, 8])
        top4 = sb("top4", [RT, 3, 8])
        route = sb("route", [RT, 3, EXPERTS])
        chosen = sb("chosen", [RT, 3, EXPERTS])
        route_sum = sb("route_sum", [RT, 2, 3])
        mix_w = sb("mix_w", [EXPERTS, T])
        mix_parts = sb("mix_parts", [MIX_ROWS, T], F32R)

        HALF = PAIR_COLS // 2
        w1 = sb("w1", [P, 2, 3, PAIR_COLS], F32R)
        scratch = sb("scratch", [P, 9 * T])
        w1_raw = scratch[:, 0:3 * 2 * HALF].rearrange("p (b a n) -> p b a n", b=3, a=2)

        def piece(n):
            return scratch[:, n * T:(n + 1) * T]

        g_raw, l_raw, g_tanh, g_act, glu = piece(0), piece(1), piece(2), piece(3), piece(4)
        g_min, l_clip = (piece(5), piece(6)), (piece(7), piece(8))
        hid = sb("hid", [P, HID_TILES, T])
        result = sb("result", [P, 2, T])

        pa = ctx.enter_context(nc.psum_tensor("pa", [P, 3, 512], F32))
        pb = ctx.enter_context(nc.psum_tensor("pb", [P, 5, 512], F32))
        GATE, LINEAR, WEIGHT, SUM, SUM_REST = range(5)

        w1_store = nc.dram_tensor("w1_store", [PAIRS, P, 3, PAIR_COLS], F32).ap()

        first_tiles = [signal(f"first_tiles{n}", 0) for n in range(KP // 2)]
        load_embed = signal("load_embed", 0)
        load_ssm = signal("load_ssm", 0)
        load_late = signal("load_late", 0)
        constants = signal("constants", 0)
        in_halved = signal("in_halved", 0)
        bias_raised = signal("bias_raised", 0)
        picks_rounded = signal("picks_rounded", 0)
        decay_exp = signal("decay_exp", 0)
        decay_ready = signal("decay_ready", 0)
        w1_raw_in = [signal(f"w1_raw_in{k}", 0) for k in range(3)]
        w1_high_done = signal("w1_high_done", 0)
        w1_low_done = signal("w1_low_done", 0)
        w1_stored = [signal(f"w1_stored{k}", 0) for k in range(2)]

        patches_in = signal("patches_in", 1, 16)
        pe_embed = signal("pe_embed", 2)
        embedded = signal("embedded", 2)
        pe_mean = signal("pe_mean", 2)
        is_centered = signal("is_centered", 2)
        squared = signal("squared", 3)
        pe_var = signal("pe_var", 3)
        root_steps = signal("root_steps", 3 * ROOT_STEPS)
        root_taken = signal("root_taken", 3)
        pe_root = signal("pe_root", 3)
        y1_ready = signal("y1_ready", 3)
        norm_ready = signal("norm_ready", 4)
        pe_in = signal("pe_in", 2 * NJ)
        tanh_ready = signal("tanh_ready", NJ)
        z_ready = signal("z_ready", NJ)
        pe_xproj = signal("pe_xproj", 1)
        dt_in_ready = signal("dt_in_ready", 1)
        bc_copied = signal("bc_copied", 1)
        bc_high = signal("bc_high", 1)
        bc_low = signal("bc_low", 1)
        pe_bc = signal("pe_bc", 2)
        bc_ready = signal("bc_ready", 2)
        pe_dt = signal("pe_dt", NJ)
        v_abs = signal("v_abs", NJ)
        v_max = signal("v_max", NJ)
        exp_ready = signal("exp_ready", 1)
        factor_ready = signal("factor_ready", NJ * FACTORS)
        poly = signal("poly", NJ * POLY_STEPS)
        u_ready = signal("u_ready", NJ)
        dt_high = signal("dt_high", NJ)
        dt_low = signal("dt_low", NJ)
        u_high = signal("u_high", NJ)
        u_low = signal("u_low", 2 * NJ)
        pe_dt_all = signal("pe_dt_all", 2 * SCAN_STEPS)
        pe_u_all = signal("pe_u_all", SCAN_STEPS)
        decayed = signal("decayed", 2 * SCAN_STEPS)
        bx_ready = signal("bx_ready", SCAN_STEPS)
        scanned = signal("scanned", SCAN_STEPS)
        read_out = signal("read_out", SCAN_STEPS)
        pe_y = signal("pe_y", SCAN_STEPS)
        y_ready = signal("y_ready", NJ)
        pe_out = signal("pe_out", 1)
        pe_ffn = signal("pe_ffn", 2 * NF)
        ffn_tanh = signal("ffn_tanh", NF)
        ffn_gated = signal("ffn_gated", NF)
        ffn_ready = signal("ffn_ready", NF)
        pe_down = signal("pe_down", 1)
        h1_ready = signal("h1_ready", 1)
        base_ready = signal("base_ready", 2)
        t_ready = signal("t_ready", 2)
        t_high_ready = signal("t_high_ready", 1)
        t_low_ready = signal("t_low_ready", 1)
        pe_logits = signal("pe_logits", 1)
        route_steps = signal("route_steps", 10)
        route_exp = signal("route_exp", 1)
        pe_mix = signal("pe_mix", 1)
        mix_copied = signal("mix_copied", 1)
        mix_high = signal("mix_high", 1)
        mix_low = signal("mix_low", 1)

        w1_in = [signal(f"w1_in{k}", PAIRS // 2, 16) for k in range(2)]
        pe_gate = signal("pe_gate", UNITS)
        pe_linear = signal("pe_linear", UNITS)
        pe_weight = signal("pe_weight", UNITS)
        gate_copied = signal("gate_copied", UNITS)
        linear_copied = signal("linear_copied", UNITS)
        gate_min = signal("gate_min", UNITS)
        linear_clip = signal("linear_clip", UNITS)
        g_tanh_ready = signal("g_tanh_ready", UNITS)
        gate_act = signal("gate_act", UNITS)
        glu_ready = signal("glu_ready", UNITS)
        hid_ready = signal("hid_ready", UNITS)
        pe_hid = signal("pe_hid", UNITS // 2)
        result_part = signal("result_part", 3)
        stored = signal("stored", 2, 16)

        block = ctx.enter_context(nc.Block())

        def run(engine, steps):
            for phase, step, i in ORDER:
                if phase == "A" and step in steps:
                    steps[step](0, i)
                elif phase == "prologue" and step in steps:
                    steps[step](i)
            with engine.Fori(1, CHUNKS) as c:
                for phase, step, i in ORDER:
                    name = step if phase == "A" else "experts_" + step
                    if phase != "prologue" and name in steps:
                        steps[name](c if phase == "A" else c - 1, i)
            for phase, step, i in ORDER:
                if phase == "B" and "experts_" + step in steps:
                    steps["experts_" + step](CHUNKS - 1, i)

        raw_state = result[0:64, 0, 0:2 * P].rearrange("p (k n) -> p k n", k=2)
        raw_group = hid[:, :, :].rearrange("p a t -> p (a t)")[:, 0:8 * P].rearrange("p (q n) -> p q n", q=8)
        raw_unit = [tile[0:MIX_ROWS, :, :].rearrange("p a t -> p (a t)")[:, 0:8 * P].rearrange("p (n m) -> p n m", n=8)
                    for tile in (b_x, state, read)]

        def scan_slot(i, k):
            j, r = divmod(i, STEPS_PER_BLOCK)
            q, pair = divmod(r, 2)
            return j, q, 2 * pair + k

        def over_images(ap):
            return ap.rearrange("p (n l) -> p n l", n=CHUNK_IMAGES)[:, :, 1:TOKENS_PER_IMAGE]

        def twice(ap):
            return ap.unsqueeze(1).to_broadcast([P, 2, T])

        EMBED_LOADS = ((vec[:, :], vectors), (mean_ones[:, :], ones_mean),
                       (ident[:, :], identity))
        SSM_LOADS = ((w_in[:, :, :], in_w), (w_in_rest[:, :, :], in_w_rest),
                     (w_xproj[:, :, :], xproj_w), (raw_state, state_pick),
                     (w_dt[:, :], dt_w), (decay[:, :], decay_log), (raw_group, group_pick),
                     (sum_channel[:, :, :], channel_sum))
        LATE_LOADS = ((w_out[:, :, :], out_w), (w_ffn[:, :, :], ffn_w), (w_ffn_rest[:, :, :], ffn_w_rest),
                      (w_down[:, :, :], ffn_down), (w_router[:, :], router_w),
                      (w_router_rest[:, :], router_w_rest), (b_router[:, :], router_b),
                      (w2[:, :, :], expert_w2), (b2[:, :], expert_b2),
                      *((raw_unit[k], unit_pick[:, 8 * k:8 * (k + 1), :]) for k in range(3)))

        @block.sync
        def _(sp):
            def load_raw(n):
                e, half = divmod(n, 2)
                sp.dma_start(w1_raw[:, n % 3, :, :], expert_w1[e][:, :, half * HALF:(half + 1) * HALF])\
                    .then_inc(w1_raw_in[n % 3].sem, 16)

            def split_w1(n):
                if n >= 3:
                    sp.wait_ge(w1_low_done.sem, 2 * (n - 2))
                if n >= 4 and n % 2 == 0:
                    e = n // 2 - 2
                    sp.dma_start(w1_store[e], w1[:, e % 2, :, :].bitcast(F32)).then_inc(w1_stored[e % 2].sem, 16)
                if n >= 3:
                    load_raw(n)
                if n == 2 * PAIRS - 1:
                    for e in (PAIRS - 2, PAIRS - 1):
                        sp.wait_ge(w1_low_done.sem, 2 * (2 * e + 2))
                        sp.dma_start(w1_store[e], w1[:, e % 2, :, :].bitcast(F32)).then_inc(w1_stored[e % 2].sem, 16)
                    for k in range(2):
                        sp.wait_ge(w1_stored[k].sem, 16 * PAIRS // 2)
                    for k in range(2):
                        sp.dma_start(w1[:, k, :, :].bitcast(F32), w1_store[k]).then_inc(w1_in[k].sem, 16)

            def center(c, _):
                sp.wait_ge(pe_embed.sem, pe_embed.at(c, 2))
                sp.dma_start(x_patch[:, :, :], patches[c]).then_inc(patches_in.sem, 16)

            def experts_linear(c, un):
                e = un // 3
                if un % 3 == 2 and (e + 2 < PAIRS or after_first(c)):
                    sp.wait_ge(pe_linear.sem, pe_linear.at(c, un + 1))
                    sp.dma_start(w1[:, e % 2, :, :].bitcast(F32), w1_store[(e + 2) % PAIRS]).then_inc(w1_in[e % 2].sem, 16)

            def experts_finish(c, _):
                sp.wait_ge(result_part.sem, result_part.at(c, 1))
                sp.dma_start(out_main[c], result[:, 0, :]).then_inc(stored.sem, 16)
                sp.wait_ge(result_part.sem, result_part.at(c, 3))
                sp.dma_start(out_rest[c], result[0:REST, 1, :]).then_inc(stored.sem, 16)

            for n in range(KP // 2):
                k = slice(2 * n, 2 * n + 2)
                sp.dma_start(w_embed[:, k, :], embed_w[:, k, :]).then_inc(first_tiles[n].sem, 16)
                sp.dma_start(x_patch[:, k, :], patches[CHUNKS - 1][:, k, :]).then_inc(first_tiles[n].sem, 16)
            for dst, src in EMBED_LOADS:
                sp.dma_start(dst, src).then_inc(load_embed.sem, 16)
            for dst, src in SSM_LOADS:
                sp.dma_start(dst, src).then_inc(load_ssm.sem, 16)
            for n in range(3):
                load_raw(n)
            for dst, src in LATE_LOADS:
                sp.dma_start(dst, src).then_inc(load_late.sem, 16)
            run(sp, {"split_w1": split_w1, "center": center,
                     "experts_linear": experts_linear, "experts_finish": experts_finish})
            sp.wait_ge(patches_in.sem, 16 * CHUNKS)
            sp.wait_ge(stored.sem, 2 * 16 * CHUNKS)

        @block.tensor
        def _(pe):
            def mm(out, lhsT, rhs, start, stop):
                return nc.tensor.matmul(out, lhsT, rhs, start=start, stop=stop)

            def embed(c, _):
                if after_first(c):
                    pe.wait_ge(patches_in.sem, patches_in.at(c - 1, 1))
                    pe.wait_ge(base_ready.sem, base_ready.at(c - 1, 1))
                for k in range(KP):
                    if not after_first(c) and k % 2 == 0:
                        pe.wait_ge(first_tiles[k // 2].sem, 2 * 16)
                    for m in range(2):
                        last = mm(pa[:, m, 0:T], w_embed[:, k, m * P:(m + 1) * P], x_patch[:, k, :],
                                  k == 0, k == KP - 1)
                        if k == KP - 1:
                            last.then_inc(pe_embed.sem, 1)

            def feature_mean(bank, x, done):
                mm(pa[:, bank, 0:T], mean_ones[:, :], x[:, 0, :], True, False)
                mm(pa[:, bank, 0:T], mean_ones[0:REST, :], x[0:REST, 1, :], False, True).then_inc(done.sem, 1)

            def center(c, _):
                if not after_first(c):
                    pe.wait_ge(load_embed.sem, 16 * len(EMBED_LOADS))
                pe.wait_ge(embedded.sem, embedded.at(c, 2))
                feature_mean(2, h0, pe_mean)

            def token_means(bank):
                for i in range(3):
                    o = pa[0:RT, bank, i:i + 1]
                    mm(o, squares[:, 0, RT * i:RT * (i + 1)], mean_ones[:, 0:1], True, False)
                    last = mm(o, squares[0:REST, 1, RT * i:RT * (i + 1)], mean_ones[0:REST, 0:1], False, True)
                last.then_inc(pe_var.sem, 1)

            def spread_roots(c, n, banks):
                pe.wait_ge(root_steps.sem, root_steps.at(c, ROOT_STEPS * n))
                for k, bank in enumerate(banks):
                    last = mm(pa[:, bank, 0:T], ones[0:RT, :],
                              diag[:, 3 * k:3 * k + 3, :].rearrange("p i t -> p (i t)"), True, True)
                last.then_inc(pe_root.sem, 1)

            def variance(c, _):
                pe.wait_ge(squared.sem, squared.at(c, 1))
                token_means(2)

            def scale(c, _):
                spread_roots(c, 1, (0, 1))

            def two_tiles(bank, w, w_rest, which, m, done):
                mm(pa[:, bank, 0:T], w[:, which, m * P:(m + 1) * P], normed[:, 0, :], True, False)
                mm(pa[:, bank, 0:T], w_rest[:, which, m * P:(m + 1) * P], normed[0:REST, 1, :],
                   False, True).then_inc(done.sem, 1)

            def inproj(c, j):
                if j == 0:
                    if not after_first(c):
                        pe.wait_ge(load_ssm.sem, 16 * len(SSM_LOADS))
                        pe.wait_ge(in_halved.sem, 1)
                    pe.wait_ge(norm_ready.sem, norm_ready.at(c, 2))
                if j == 2:
                    pe.wait_ge(tanh_ready.sem, tanh_ready.at(c, 1))
                two_tiles((2 * j) % 3, w_in, w_in_rest, 0, j, pe_in)
                if j:
                    pe.wait_ge(z_ready.sem, z_ready.at(c, j))
                two_tiles((2 * j + 1) % 3, w_in, w_in_rest, 1, j, pe_in)

            def xproj(c, _):
                pe.wait_ge(z_ready.sem, z_ready.at(c, NJ))
                for j in range(NJ):
                    last = mm(pa[:, 0, 0:T], w_xproj[:, j, :], z[:, j, :], j == 0, j == NJ - 1)
                last.then_inc(pe_xproj.sem, 1)

            def delta(c, _):
                pe.wait_ge(dt_in_ready.sem, dt_in_ready.at(c, 1))
                for j in range(NJ):
                    if j == 2:
                        pe.wait_ge(bc_copied.sem, bc_copied.at(c, 1))
                    mm(pa[:, (j + 1) % 3, 0:T], w_dt[:, j * P:(j + 1) * P], dt_in[:, :],
                       True, True).then_inc(pe_dt.sem, 1)

            def broadcast(c, _):
                if not after_first(c):
                    pe.wait_ge(picks_rounded.sem, 1)
                pe.wait_ge(bc_high.sem, bc_high.at(c, 1))
                pe.wait_ge(bc_low.sem, bc_low.at(c, 1))
                for k in range(2):
                    pe.wait_ge(v_max.sem, v_max.at(c, k + 1))
                    mm(pa[:, 1 + k, 0:T], pick_state[:, k, :], bc_parts[:, :], True, True).then_inc(pe_bc.sem, 1)

            def expand_u(c, i):
                j = i // STEPS_PER_BLOCK
                if i:
                    pe.wait_ge(bx_ready.sem, bx_ready.at(c, i))
                elif after_first(c):
                    pe.wait_ge(gate_copied.sem, gate_copied.at(c - 1, UNITS_BEFORE_SCAN))
                    pe.wait_ge(linear_copied.sem, linear_copied.at(c - 1, UNITS_BEFORE_SCAN))
                if i % STEPS_PER_BLOCK == 0:
                    pe.wait_ge(u_high.sem, u_high.at(c, j + 1))
                    pe.wait_ge(u_low.sem, u_low.at(c, 2 * j + 2))
                for k in range(2):
                    _, q, b = scan_slot(i, k)
                    last = mm(pb[:, k, 0:T], pick_group[:, 4 * (b % 2) + q, :], u_rows[:, j, b // 2, :], True, True)
                last.then_inc(pe_u_all.sem, 1)

            def expand_dt(c, i):
                j = i // STEPS_PER_BLOCK
                if i % STEPS_PER_BLOCK == 0:
                    pe.wait_ge(dt_high.sem, dt_high.at(c, j + 1))
                    pe.wait_ge(dt_low.sem, dt_low.at(c, j + 1))
                for k in range(2):
                    _, q, b = scan_slot(i, k)
                    if i:
                        pe.wait_ge(decayed.sem, decayed.at(c, 2 * i - 1 + k))
                    elif k == 0:
                        pe.wait_ge(v_max.sem, v_max.at(c, NJ))
                        pe.wait_ge(bc_ready.sem, bc_ready.at(c, 1))
                    mm(pa[:, k, 0:T], pick_group[:, 4 * (b % 2) + q, :], dt_rows[:, j, b // 2, :],
                       True, True).then_inc(pe_dt_all.sem, 1)

            def collect(c, i):
                if i == 0:
                    pe.wait_ge(bc_ready.sem, bc_ready.at(c, 2))
                elif i % STEPS_PER_BLOCK == 0:
                    pe.wait_ge(y_ready.sem, y_ready.at(c, i // STEPS_PER_BLOCK))
                pe.wait_ge(read_out.sem, read_out.at(c, i + 1))
                for k in range(2):
                    _, q, b = scan_slot(i, k)
                    last = mm(pa[32 * b:32 * b + 32, 2, 0:T], sum_channel[:, q, :],
                              read[:, i % 2, k * T:(k + 1) * T], q == 0, q == 3)
                last.then_inc(pe_y.sem, 1)

            def outproj(c, _):
                if not after_first(c):
                    pe.wait_ge(load_late.sem, 16 * len(LATE_LOADS))
                pe.wait_ge(y_ready.sem, y_ready.at(c, NJ))
                for m in range(2):
                    for j in range(NJ):
                        last = mm(pa[:, m, 0:T], w_out[:, j, m * P:(m + 1) * P], y[:, j, :], j == 0, j == NJ - 1)
                last.then_inc(pe_out.sem, 1)

            def variance2(c, _):
                pe.wait_ge(squared.sem, squared.at(c, 2))
                token_means(2)

            def scale2(c, _):
                spread_roots(c, 2, (0,))

            def ffn_up(c, k):
                if k == 0:
                    pe.wait_ge(norm_ready.sem, norm_ready.at(c, 4))
                for which in range(2):
                    n = 2 * k + which
                    if n >= 3:
                        before = n - 3
                        if before % 2:
                            pe.wait_ge(ffn_ready.sem, ffn_ready.at(c, before // 2 + 1))
                        else:
                            pe.wait_ge(ffn_gated.sem, ffn_gated.at(c, before // 2 + 1))
                    two_tiles(n % 3, w_ffn, w_ffn_rest, which, k, pe_ffn)

            def down(c, _):
                pe.wait_ge(ffn_ready.sem, ffn_ready.at(c, NF))
                for m in range(2):
                    for k in range(NF):
                        last = mm(pa[:, 1 + m, 0:T], w_down[:, k, m * P:(m + 1) * P], ffn[:, k, :],
                                  k == 0, k == NF - 1)
                last.then_inc(pe_down.sem, 1)

            def center3(c, _):
                pe.wait_ge(h1_ready.sem, h1_ready.at(c, 1))
                feature_mean(0, h0, pe_mean)

            def variance3(c, _):
                pe.wait_ge(squared.sem, squared.at(c, 3))
                token_means(1)

            def scale3(c, _):
                if not after_first(c):
                    pe.wait_ge(picks_rounded.sem, 2)
                    pe.wait_ge(bias_raised.sem, 1)
                spread_roots(c, 3, (0, 2))

            def experts_topk(c, _):
                pe.wait_ge(t_ready.sem, t_ready.at(c, 2))
                for i in range(3):
                    o = pb[0:RT, GATE, EXPERTS * i:EXPERTS * (i + 1)]
                    mm(o, t_in[:, 0, RT * i:RT * (i + 1)], w_router[:, :], True, False)
                    mm(o, t_in[0:REST, 1, RT * i:RT * (i + 1)], w_router_rest[:, :], False, False)
                    last = mm(o, ones[0:1, 0:RT], b_router[:, :], False, True)
                last.then_inc(pe_logits.sem, 1)

            def experts_weights(c, _):
                pe.wait_ge(route_steps.sem, route_steps.at(c, 10))
                for i in range(3):
                    last = nc.tensor.transpose(pb[0:EXPERTS, LINEAR, RT * i:RT * (i + 1)], route[:, i, :],
                                               ident[0:RT, 0:RT])
                last.then_inc(pe_mix.sem, 1)

            def experts_start(c, _):
                pe.wait_ge(mix_copied.sem, mix_copied.at(c, 1))
                pe.wait_ge(mix_high.sem, mix_high.at(c, 1))
                pe.wait_ge(mix_low.sem, mix_low.at(c, 1))
                pe.wait_ge(t_high_ready.sem, t_high_ready.at(c, 1))
                pe.wait_ge(t_low_ready.sem, t_low_ready.at(c, 1))
                mm(pb[:, SUM, 0:T], b2[:, 0:P], mix_w[:, :], True, False)
                mm(pb[0:REST, SUM_REST, 0:T], b2[:, P:HIDDEN], mix_w[:, :], True, False)

            def experts_up(bank, e, first):
                cols = slice(first, first + P)
                o = pb[:, bank, 0:T]
                w = w1[:, e % 2, :, cols]
                mm(o, w[:, 0, :], t_high[:, 0, :], True, False)
                mm(o, w[:, 1, :], t_high[:, 0, :], False, False)
                mm(o, w[:, 0, :], t_low[:, 0, :], False, False)
                mm(o, w[:, 2, :], t_high[:, 1, :], False, False)
                return mm(o, w[0:REST, 2, :], t_low[0:REST, 1, :], False, True)

            def experts_gate(c, un):
                e, k = divmod(un, 3)
                if k == 0:
                    pe.wait_ge(w1_in[e % 2].sem, w1_in[e % 2].at(c, e // 2 + 1))
                if un:
                    pe.wait_ge(gate_copied.sem, gate_copied.at(c, un))
                experts_up(GATE, e, 2 * k * P).then_inc(pe_gate.sem, 1)

            def experts_linear(c, un):
                e, k = divmod(un, 3)
                if un:
                    pe.wait_ge(linear_copied.sem, linear_copied.at(c, un))
                experts_up(LINEAR, e, (2 * k + 1) * P).then_inc(pe_linear.sem, 1)

            def experts_scale(c, un):
                if un:
                    pe.wait_ge(hid_ready.sem, hid_ready.at(c, un))
                mm(pb[:, WEIGHT, 0:T], pick_unit[:, un, :], mix_parts[:, :], True, True).then_inc(pe_weight.sem, 1)

            def experts_down(c, n):
                pair, part = divmod(n, 3)
                first = 2 * pair
                if part == 0:
                    pe.wait_ge(hid_ready.sem, hid_ready.at(c, first + 2))
                if part < 2:
                    un = first + part
                    mm(pb[:, SUM, 0:T], w2[:, un, 0:P], hid[:, un % HID_TILES, :], False, un == UNITS - 1)
                else:
                    for k in range(2):
                        last = mm(pb[k * REST:(k + 1) * REST, SUM_REST, 0:T], w2[:, first + k, P:HIDDEN],
                                  hid[:, (first + k) % HID_TILES, :], (pair, k) == (0, 1), pair == UNITS // 2 - 1)
                    last.then_inc(pe_hid.sem, 1)

            run(pe, {
                "embed": embed, "center": center, "variance": variance, "scale": scale, "inproj": inproj,
                "xproj": xproj, "delta": delta, "broadcast": broadcast,
                "scan": expand_u, "decay": expand_dt,
                "collect": collect, "outproj": outproj, "variance2": variance2, "scale2": scale2,
                "ffn": ffn_up, "down": down, "center3": center3, "variance3": variance3, "scale3": scale3,
                "experts_topk": experts_topk, "experts_weights": experts_weights, "experts_start": experts_start, "experts_gate": experts_gate,
                "experts_linear": experts_linear, "experts_scale": experts_scale,
                "experts_down": experts_down})

        @block.scalar
        def _(act):
            def activate(out, in_, func, **kw):
                return nc.scalar.activation(out, in_, func, **kw)

            def embed(c, _):
                if after_first(c):
                    act.wait_ge(base_ready.sem, base_ready.at(c - 1, 2))
                for m in range(2):
                    act.wait_ge(pe_embed.sem, pe_embed.at(c, m + 1))
                    activate(h0[:, m, :], pa[:, m, 0:T], ACT.Identity, bias=col("embed_b", m)).then_inc(embedded.sem, 1)

            def center(c, _):
                act.wait_ge(is_centered.sem, is_centered.at(c, 1))
                activate(squares[:, :, :], centered[:, :, :], ACT.Square).then_inc(squared.sem, 1)

            def inproj(c, j):
                act.wait_ge(pe_in.sem, pe_in.at(c, 2 * j + 2))
                if j >= 2:
                    act.wait_ge(z_ready.sem, z_ready.at(c, j - 1))
                activate(gate_tanh[:, j % 2, :], pa[:, (2 * j + 1) % 3, 0:T], ACT.Tanh, scale=0.5)\
                    .then_inc(tanh_ready.sem, 1)

            def xproj(c, _):
                act.wait_ge(pe_xproj.sem, pe_xproj.at(c, 1))
                activate(dt_in[:, :], pa[0:DT_RANK, 0, 0:T], ACT.Copy).then_inc(dt_in_ready.sem, 1)
                act.wait_ge(bc_copied.sem, bc_copied.at(c, 1))
                activate(bc_parts[0:32, :], bc[:, :], ACT.Copy).then_inc(bc_high.sem, 1)

            def delta(c, _):
                for j in range(NJ):
                    act.wait_ge(pe_dt.sem, pe_dt.at(c, j + 1))
                    activate(sp_exp[:, j, :], pa[:, (j + 1) % 3, 0:T], ACT.Abs, bias=col("dt_b", j))\
                        .then_inc(v_abs.sem, 1)
                act.wait_ge(v_abs.sem, v_abs.at(c, NJ))
                activate(sp_exp[:, :, :], sp_exp[:, :, :], ACT.Exp, scale=-1.0).then_inc(exp_ready.sem, 1)

            def broadcast(c, _):
                for k, tile in enumerate((b_all, c_all)):
                    act.wait_ge(pe_bc.sem, pe_bc.at(c, k + 1))
                    activate(tile[:, :], pa[:, 1 + k, 0:T], ACT.Copy).then_inc(bc_ready.sem, 1)

            def split(c, j):
                act.wait_ge(poly.sem, poly.at(c, POLY_STEPS * (j + 1)))
                activate(dt_rows[0:P // 2, j, 0, :], dt[0:P // 2, j, :], ACT.Copy)
                activate(dt_rows[P // 2:P, j, 1, :], dt[P // 2:P, j, :], ACT.Copy).then_inc(dt_high.sem, 1)
                act.wait_ge(u_ready.sem, u_ready.at(c, j + 1))
                activate(u_rows[0:P // 2, j, 0, :], u[0:P // 2, j, :], ACT.Copy)
                activate(u_rows[P // 2:P, j, 1, :], u[P // 2:P, j, :], ACT.Copy).then_inc(u_high.sem, 1)

            def square(c, n):
                j, k = divmod(n, FACTORS)
                if n == 0 and not after_first(c):
                    act.wait_ge(constants.sem, 1)
                if n == 0:
                    act.wait_ge(exp_ready.sem, exp_ready.at(c, 1))
                if j:
                    act.wait_ge(poly.sem, poly.at(c, POLY_STEPS * j))
                activate(factors[:, k, :], sp_exp[:, j, :], ACT.Square, bias=shifts[:, k:k + 1])\
                    .then_inc(factor_ready.sem, 1)

            def log1p(c, j):
                if not after_first(c) and j == 0:
                    act.wait_ge(load_late.sem, 16 * len(LATE_LOADS))
                    for k in range(3):
                        rounded = activate(pick_unit[:, 8 * k:8 * (k + 1), :], raw_unit[k], ACT.Copy)
                    rounded.then_inc(picks_rounded.sem, 1)

            def decay_step(c, i):
                if not after_first(c) and i == 0:
                    act.wait_ge(constants.sem, 1)
                    act.wait_ge(decay_ready.sem, 1)
                if i >= 2:
                    act.wait_ge(scanned.sem, scanned.at(c, i - 1))
                for k in range(2):
                    j, q, b = scan_slot(i, k)
                    group = GROUPS_PER_BLOCK * j + 4 * b + q
                    act.wait_ge(pe_dt_all.sem, pe_dt_all.at(c, 2 * i + k + 1))
                    activate(over_images(a_bar[:, i % 2, k * T:(k + 1) * T]), over_images(pa[:, k, 0:T]), ACT.Exp,
                             scale=decay[:, group:group + 1]).then_inc(decayed.sem, 1)

            def split_w1(n):
                e, half = divmod(n, 2)
                cols = slice(half * HALF, (half + 1) * HALF)
                act.wait_ge(w1_raw_in[n % 3].sem, 16 * (n // 3 + 1))
                if e >= 2:
                    act.wait_ge(w1_stored[e % 2].sem, 16 * (e // 2))
                activate(w1[:, e % 2, 0, cols], w1_raw[:, n % 3, 0, :], ACT.Copy)
                activate(w1[:, e % 2, 2, cols], w1_raw[:, n % 3, 1, :], ACT.Copy).then_inc(w1_high_done.sem, 1)

            def variance2(c, _):
                act.wait_ge(y1_ready.sem, y1_ready.at(c, 2))
                activate(squares[:, :, :], y1[:, :, :], ACT.Square).then_inc(squared.sem, 1)

            def ffn_gate_tanh(c, k):
                act.wait_ge(pe_ffn.sem, pe_ffn.at(c, 2 * k + 1))
                if k >= 2:
                    act.wait_ge(ffn_gated.sem, ffn_gated.at(c, k - 1))
                activate(gate_tanh[:, k % 2, :], pa[:, (2 * k) % 3, 0:T], ACT.Tanh, scale=0.5).then_inc(ffn_tanh.sem, 1)

            def center3(c, _):
                act.wait_ge(is_centered.sem, is_centered.at(c, 2))
                activate(squares[:, :, :], centered[:, :, :], ACT.Square).then_inc(squared.sem, 1)

            def scale3(c, _):
                if after_first(c):
                    act.wait_ge(pe_linear.sem, pe_linear.at(c - 1, UNITS))
                act.wait_ge(t_ready.sem, t_ready.at(c, 2))
                activate(t_high[:, :, :], t_in[:, :, :], ACT.Copy).then_inc(t_high_ready.sem, 1)
                if after_first(c):
                    act.wait_ge(stored.sem, stored.at(c - 1, 2))

            def experts_topk(c, _):
                act.wait_ge(route_steps.sem, route_steps.at(c, 6))
                activate(route[:, :, :], route[:, :, :], ACT.Exp).then_inc(route_exp.sem, 1)

            def experts_weights(c, _):
                act.wait_ge(pe_mix.sem, pe_mix.at(c, 1))
                activate(mix_w[:, :], pb[0:EXPERTS, LINEAR, 0:T], ACT.Copy).then_inc(mix_copied.sem, 1)
                act.wait_ge(mix_copied.sem, mix_copied.at(c, 1))
                activate(mix_parts[0:EXPERTS, :], mix_w[:, :], ACT.Copy).then_inc(mix_high.sem, 1)

            def experts_gate(c, un):
                act.wait_ge(pe_gate.sem, pe_gate.at(c, un + 1))
                if un:
                    act.wait_ge(gate_min.sem, gate_min.at(c, un))
                activate(g_raw, pb[:, GATE, 0:T], ACT.Identity, bias=col("b1_gate", un)).then_inc(gate_copied.sem, 1)

            def experts_linear(c, un):
                act.wait_ge(pe_linear.sem, pe_linear.at(c, un + 1))
                if un:
                    act.wait_ge(linear_clip.sem, linear_clip.at(c, un))
                activate(l_raw, pb[:, LINEAR, 0:T], ACT.Identity, bias=col("b1_linear", un))\
                    .then_inc(linear_copied.sem, 1)

            def experts_mix(c, un):
                act.wait_ge(gate_min.sem, gate_min.at(c, un + 1))
                if un:
                    act.wait_ge(gate_act.sem, gate_act.at(c, un))
                activate(g_tanh, g_min[un % 2], ACT.Tanh, scale=ALPHA / 2).then_inc(g_tanh_ready.sem, 1)

            act.wait_ge(load_ssm.sem, 16 * len(SSM_LOADS))
            activate(decay[:, :], decay[:, :], ACT.Exp).then_inc(decay_exp.sem, 1)
            act.wait_ge(load_embed.sem, 16 * len(EMBED_LOADS))
            run(act, {
                "embed": embed, "center": center, "inproj": inproj, "xproj": xproj, "delta": delta,
                "broadcast": broadcast, "square": square, "log1p": log1p,
                "split": split, "split_w1": split_w1,
                "decay": decay_step,
                "variance2": variance2, "ffn": ffn_gate_tanh, "center3": center3, "scale3": scale3,
                "experts_topk": experts_topk,
                "experts_weights": experts_weights, "experts_gate": experts_gate,
                "experts_linear": experts_linear, "experts_mix": experts_mix})

        @block.vector
        def _(dve):
            def center(c, _):
                dve.wait_ge(embedded.sem, embedded.at(c, 2))
                dve.wait_ge(pe_mean.sem, pe_mean.at(c, 1))
                dve.tensor_tensor(centered[:, :, :], h0[:, :, :], twice(pa[:, 2, 0:T]), ALU.subtract)\
                    .then_inc(is_centered.sem, 1)

            def roots(c, n, bank, ln_eps, rms_eps):
                v = pa[0:RT, bank, 0:3]
                dve.wait_ge(pe_var.sem, pe_var.at(c, n))
                dve.tensor_scalar(root[:, 0, 0:3], v, ln_eps, None, ALU.add)
                dve.tensor_scalar(root[:, 0, 3:6], v, 1.0 + rms_eps, ln_eps * rms_eps, ALU.mult, ALU.add)\
                    .then_inc(root_steps.sem, 1)
                dve.wait_ge(root_taken.sem, root_taken.at(c, n))
                used = 3 if n == 2 else 6
                dve.tensor_tensor(diag[:, 0:used, :], ident[0:RT, 0:RT].unsqueeze(1).to_broadcast([RT, used, RT]),
                                  root[:, 1, 0:used].unsqueeze(2).to_broadcast([RT, used, RT]), ALU.mult)\
                    .then_inc(root_steps.sem, 1)

            def variance(c, _):
                roots(c, 1, 2, 1e-5, 1e-6)

            def scale(c, _):
                dve.wait_ge(pe_root.sem, pe_root.at(c, 1))
                dve.tensor_tensor(y1[:, :, :], centered[:, :, :], twice(pa[:, 0, 0:T]), ALU.mult)\
                    .then_inc(y1_ready.sem, 1)
                for m in range(2):
                    dve.scalar_tensor_tensor(normed[:, m, :], centered[:, m, :], col("norm1", m),
                                             pa[:, 1, 0:T], ALU.mult, ALU.mult).then_inc(norm_ready.sem, 1)

            def inproj(c, j):
                dve.wait_ge(tanh_ready.sem, tanh_ready.at(c, j + 1))
                dve.scalar_tensor_tensor(z[:, j, :], gate_tanh[:, j % 2, :], 1.0, pa[:, (2 * j) % 3, 0:T],
                                         ALU.add, ALU.mult).then_inc(z_ready.sem, 1)

            def xproj(c, _):
                dve.wait_ge(pe_xproj.sem, pe_xproj.at(c, 1))
                dve.tensor_copy(bc[:, :], pa[DT_RANK:P, 0, 0:T]).then_inc(bc_copied.sem, 1)
                dve.wait_ge(bc_high.sem, bc_high.at(c, 1))
                dve.wait_ge(bc_copied.sem, bc_copied.at(c, 1))
                dve.tensor_tensor(bc_parts[32:64, :], bc[:, :], bc_parts[0:32, :].bitcast(F32), ALU.subtract)\
                    .then_inc(bc_low.sem, 1)

            def delta(c, _):
                for j in range(NJ):
                    dve.wait_ge(v_abs.sem, v_abs.at(c, j + 1))
                    dve.tensor_scalar(u[:, j, :], pa[:, (j + 1) % 3, 0:T], col("dt_b", j), 0.0,
                                      ALU.add, ALU.max).then_inc(v_max.sem, 1)

            def log1p(c, j):
                if j == 0:
                    dve.wait_ge(exp_ready.sem, exp_ready.at(c, 1))
                for k, (_, rest) in enumerate(LOG1P):
                    dve.wait_ge(factor_ready.sem, factor_ready.at(c, FACTORS * j + k + 1))
                    if k:
                        dve.wait_ge(poly.sem, poly.at(c, POLY_STEPS * j + k))
                    dve.scalar_tensor_tensor(dt[:, j, :], factors[:, k, :], rest, dt[:, j, :] if k else sp_exp[:, j, :],
                                             ALU.add, ALU.mult).then_inc(poly.sem, 1)
                dve.wait_ge(v_max.sem, v_max.at(c, NJ))
                dve.wait_ge(poly.sem, poly.at(c, POLY_STEPS * j + FACTORS))
                dve.scalar_tensor_tensor(dt[:, j, :], dt[:, j, :], LOG1P_SCALE, u[:, j, :],
                                         ALU.mult, ALU.add).then_inc(poly.sem, 1)

            def split(c, j):
                dve.wait_ge(dt_high.sem, dt_high.at(c, j + 1))
                dve.tensor_tensor(dt_rows[P // 2:P, j, 0, :], dt[0:P // 2, j, :],
                                  dt_rows[0:P // 2, j, 0, :].bitcast(F32), ALU.subtract)
                dve.tensor_tensor(dt_rows[0:P // 2, j, 1, :], dt[P // 2:P, j, :],
                                  dt_rows[P // 2:P, j, 1, :].bitcast(F32), ALU.subtract).then_inc(dt_low.sem, 1)

            def drive(c, i):
                if i == 0:
                    dve.wait_ge(bc_ready.sem, bc_ready.at(c, 1))
                if i >= 3:
                    dve.wait_ge(scanned.sem, scanned.at(c, i - 2))
                dve.wait_ge(pe_u_all.sem, pe_u_all.at(c, i + 1))
                dve.tensor_tensor(b_x[:, i % 3, :].rearrange("p (k t) -> p k t", k=2), twice(b_all[:, :]),
                                  pb[:, 0:2, 0:T], ALU.mult).then_inc(bx_ready.sem, 1)

            def advance(c, i):
                dve.wait_ge(decayed.sem, decayed.at(c, 2 * i + 2))
                dve.wait_ge(bx_ready.sem, bx_ready.at(c, i + 1))
                if i >= 2:
                    dve.wait_ge(read_out.sem, read_out.at(c, i - 1))
                dve.tensor_tensor_scan(state[:, i % 2, :], a_bar[:, i % 2, :], b_x[:, i % 3, :], 0.0,
                                       ALU.mult, ALU.add).then_inc(scanned.sem, 1)

            def collect(c, i):
                j, r = divmod(i, STEPS_PER_BLOCK)
                if r == STEPS_PER_BLOCK - 1:
                    dve.wait_ge(pe_y.sem, pe_y.at(c, i + 1))
                    dve.scalar_tensor_tensor(y[:, j, :], z[:, j, :], col("skip", j), pa[:, 2, 0:T],
                                             ALU.mult, ALU.add).then_inc(y_ready.sem, 1)

            def outproj(c, _):
                dve.wait_ge(pe_out.sem, pe_out.at(c, 1))
                dve.tensor_tensor(y1[:, :, :], y1[:, :, :], pa[:, 0:2, 0:T], ALU.add).then_inc(y1_ready.sem, 1)

            def variance2(c, _):
                roots(c, 2, 2, 1e-6, 0.0)

            def scale2(c, _):
                dve.wait_ge(pe_root.sem, pe_root.at(c, 2))
                for m in range(2):
                    dve.scalar_tensor_tensor(normed[:, m, :], y1[:, m, :], col("norm2", m), pa[:, 0, 0:T],
                                             ALU.mult, ALU.mult).then_inc(norm_ready.sem, 1)

            def ffn_product(c, k):
                dve.wait_ge(ffn_tanh.sem, ffn_tanh.at(c, k + 1))
                if k:
                    dve.wait_ge(ffn_ready.sem, ffn_ready.at(c, k))
                dve.scalar_tensor_tensor(ffn_gate[:, :], gate_tanh[:, k % 2, :], 1.0, pa[:, (2 * k) % 3, 0:T],
                                         ALU.add, ALU.mult).then_inc(ffn_gated.sem, 1)
                dve.wait_ge(ffn_gated.sem, ffn_gated.at(c, k + 1))
                dve.wait_ge(pe_ffn.sem, pe_ffn.at(c, 2 * k + 2))
                dve.scalar_tensor_tensor(ffn[:, k, :], ffn_gate[:, :], 0.5, pa[:, (2 * k + 1) % 3, 0:T],
                                         ALU.mult, ALU.mult)\
                    .then_inc(ffn_ready.sem, 1)

            def down(c, _):
                dve.wait_ge(pe_down.sem, pe_down.at(c, 1))
                dve.tensor_tensor(y1[:, :, :], y1[:, :, :], pa[:, 1:3, 0:T], ALU.add).then_inc(y1_ready.sem, 1)
                dve.wait_ge(y1_ready.sem, y1_ready.at(c, 3))
                dve.tensor_tensor(h0[:, :, :], h0[:, :, :], y1[:, :, :], ALU.add).then_inc(h1_ready.sem, 1)

            def center3(c, _):
                dve.wait_ge(h1_ready.sem, h1_ready.at(c, 1))
                dve.wait_ge(pe_mean.sem, pe_mean.at(c, 2))
                dve.tensor_tensor(centered[:, :, :], h0[:, :, :], twice(pa[:, 0, 0:T]), ALU.subtract)\
                    .then_inc(is_centered.sem, 1)

            def variance3(c, _):
                roots(c, 3, 1, 1e-5, 1e-5)

            def scale3(c, _):
                dve.wait_ge(pe_root.sem, pe_root.at(c, 3))
                for m in range(2):
                    dve.scalar_tensor_tensor(t_in[:, m, :], centered[:, m, :], col("norm3", m),
                                             pa[:, 2, 0:T], ALU.mult, ALU.mult).then_inc(t_ready.sem, 1)
                dve.tensor_tensor(base[:, :, :], centered[:, :, :], twice(pa[:, 0, 0:T]), ALU.mult)\
                    .then_inc(base_ready.sem, 1)
                dve.wait_ge(t_high_ready.sem, t_high_ready.at(c, 1))
                dve.wait_ge(t_ready.sem, t_ready.at(c, 2))
                dve.tensor_tensor(t_low[:, :, :], t_in[:, :, :], t_high[:, :, :].bitcast(F32), ALU.subtract)\
                    .then_inc(t_low_ready.sem, 1)

            def experts_topk(c, _):
                E = EXPERTS
                dve.wait_ge(pe_logits.sem, pe_logits.at(c, 1))
                dve.tensor_copy(logits[:, :, 0:E], pb[0:RT, GATE, 0:3 * E].rearrange("p (i e) -> p i e", i=3))\
                    .then_inc(route_steps.sem, 1)
                dve.wait_ge(route_steps.sem, route_steps.at(c, 1))
                dve.memset(after_wait[:, :], 0.0)
                for i in range(3):
                    last = dve.max(top8[:, i, :], logits[:, i, 0:E])
                last.then_inc(route_steps.sem, 1)
                dve.wait_ge(route_steps.sem, route_steps.at(c, 2))
                dve.tensor_copy(top4[:, :, 0:TOP_K], top8[:, :, 0:TOP_K]).then_inc(route_steps.sem, 1)
                dve.wait_ge(route_steps.sem, route_steps.at(c, 3))
                dve.memset(after_wait[:, :], 0.0)
                for i in range(3):
                    last = dve.match_replace(replaced[:, i, :], top4[:, i, :], logits[:, i, :], -PAD_LOGIT)
                last.then_inc(route_steps.sem, 1)
                dve.wait_ge(route_steps.sem, route_steps.at(c, 4))
                dve.tensor_tensor(chosen[:, :, :], replaced[:, :, 0:E], logits[:, :, 0:E], ALU.not_equal)\
                    .then_inc(route_steps.sem, 1)
                dve.tensor_tensor(route[:, :, :], logits[:, :, 0:E],
                                  top8[:, :, 0:1].to_broadcast([RT, 3, E]), ALU.subtract)\
                    .then_inc(route_steps.sem, 1)
                dve.wait_ge(route_steps.sem, route_steps.at(c, 5))
                dve.wait_ge(route_exp.sem, route_exp.at(c, 1))
                dve.tensor_tensor(route[:, :, :], route[:, :, :], chosen[:, :, :], ALU.mult)\
                    .then_inc(route_steps.sem, 1)
                dve.wait_ge(route_steps.sem, route_steps.at(c, 7))
                dve.reduce_sum(route_sum[:, 0, :], route[:, :, :], AX.X).then_inc(route_steps.sem, 1)
                dve.wait_ge(route_steps.sem, route_steps.at(c, 8))
                dve.reciprocal(route_sum[:, 1, :], route_sum[:, 0, :]).then_inc(route_steps.sem, 1)
                dve.wait_ge(route_steps.sem, route_steps.at(c, 9))
                dve.tensor_tensor(route[:, :, :], route[:, :, :],
                                  route_sum[:, 1, :].unsqueeze(2).to_broadcast([RT, 3, E]), ALU.mult)\
                    .then_inc(route_steps.sem, 1)

            def experts_weights(c, _):
                dve.wait_ge(mix_high.sem, mix_high.at(c, 1))
                dve.tensor_tensor(mix_parts[32:32 + EXPERTS, :], mix_w[:, :], mix_parts[0:EXPERTS, :].bitcast(F32),
                                  ALU.subtract).then_inc(mix_low.sem, 1)

            def experts_gate(c, un):
                dve.wait_ge(gate_copied.sem, gate_copied.at(c, un + 1))
                if un >= 2:
                    dve.wait_ge(gate_act.sem, gate_act.at(c, un - 1))
                dve.tensor_scalar(g_min[un % 2], g_raw, LIMIT, None, ALU.min).then_inc(gate_min.sem, 1)

            def experts_linear(c, un):
                dve.wait_ge(linear_copied.sem, linear_copied.at(c, un + 1))
                if un >= 2:
                    dve.wait_ge(glu_ready.sem, glu_ready.at(c, un - 1))
                dve.tensor_scalar(l_clip[un % 2], l_raw, 1.0 + LIMIT, 1.0 - LIMIT, ALU.min, ALU.max)\
                    .then_inc(linear_clip.sem, 1)

            def experts_mix(c, un):
                dve.wait_ge(g_tanh_ready.sem, g_tanh_ready.at(c, un + 1))
                if un:
                    dve.wait_ge(glu_ready.sem, glu_ready.at(c, un))
                dve.scalar_tensor_tensor(g_act, g_tanh, 1.0, g_min[un % 2], ALU.add, ALU.mult)\
                    .then_inc(gate_act.sem, 1)

            def experts_scale(c, un):
                dve.wait_ge(glu_ready.sem, glu_ready.at(c, un + 1))
                dve.wait_ge(pe_weight.sem, pe_weight.at(c, un + 1))
                if un >= HID_TILES:
                    dve.wait_ge(pe_hid.sem, pe_hid.at(c, (un - HID_TILES) // 2 + 1))
                dve.tensor_tensor(hid[:, un % HID_TILES, :], glu, pb[:, WEIGHT, 0:T], ALU.mult).then_inc(hid_ready.sem, 1)

            def experts_finish(c, _):
                dve.wait_ge(base_ready.sem, base_ready.at(c, 2))
                dve.wait_ge(pe_hid.sem, pe_hid.at(c, UNITS // 2))
                dve.tensor_tensor(result[:, 0, :], base[:, 0, :], pb[:, SUM, 0:T], ALU.add)\
                    .then_inc(result_part.sem, 1)
                dve.tensor_tensor(result[0:REST, 1, :], base[0:REST, 1, :], pb[0:REST, SUM_REST, 0:T], ALU.add)\
                    .then_inc(result_part.sem, 1)
                dve.wait_ge(result_part.sem, result_part.at(c, 2))
                dve.tensor_tensor(result[0:REST, 1, :], result[0:REST, 1, :], pb[REST:P, SUM_REST, 0:T], ALU.add)\
                    .then_inc(result_part.sem, 1)

            dve.wait_ge(load_embed.sem, 16 * len(EMBED_LOADS))
            dve.wait_ge(constants.sem, 1)
            run(dve, {
                "center": center, "variance": variance, "scale": scale, "inproj": inproj, "xproj": xproj,
                "delta": delta, "log1p": log1p, "split": split, "scan": drive,
                "advance": advance, "collect": collect, "outproj": outproj, "variance2": variance2,
                "scale2": scale2, "ffn": ffn_product, "down": down, "center3": center3,
                "variance3": variance3, "scale3": scale3, "experts_topk": experts_topk,
                "experts_weights": experts_weights, "experts_gate": experts_gate,
                "experts_linear": experts_linear, "experts_mix": experts_mix,
                "experts_scale": experts_scale, "experts_finish": experts_finish})

        @block.gpsimd
        def _(pool):
            def take_roots(c, n):
                pool.wait_ge(root_steps.sem, root_steps.at(c, ROOT_STEPS * (n - 1) + 1))
                pool.tensor_tensor(root[:, 1, :], root[:, 0, :], minus_half[:, :], ALU.pow).then_inc(root_taken.sem, 1)

            def scale(c, _):
                if not after_first(c):
                    pool.wait_ge(decay_exp.sem, 1)
                    pool.tensor_scalar(decay[:, :], decay[:, :], -1.0, None, ALU.mult).then_inc(decay_ready.sem, 1)
                    pool.tensor_scalar(pick_state[:, :, :], raw_state, 1.0, None, ALU.mult)
                    pool.tensor_scalar(pick_group[:, :, :], raw_group, 1.0, None, ALU.mult)\
                        .then_inc(picks_rounded.sem, 1)

            def split_w1(n):
                e, half = divmod(n, 2)
                cols = slice(half * HALF, (half + 1) * HALF)
                pool.wait_ge(w1_high_done.sem, n + 1)
                pool.tensor_tensor(w1[:, e % 2, 1, cols], w1_raw[:, n % 3, 0, :],
                                   w1[:, e % 2, 0, cols].bitcast(F32), ALU.subtract).then_inc(w1_low_done.sem, 1)
                pool.wait_ge(w1_low_done.sem, 2 * n + 1)
                low = w1[REST:P, e % 2, 2, cols]
                pool.tensor_tensor(low, w1_raw[REST:P, n % 3, 1, :], low.bitcast(F32), ALU.subtract)\
                    .then_inc(w1_low_done.sem, 1)
                pool.wait_ge(w1_low_done.sem, 2 * n + 2)

            def split(c, j):
                pool.wait_ge(poly.sem, poly.at(c, POLY_STEPS * (j + 1)))
                pool.tensor_tensor(u[:, j, :], dt[:, j, :], z[:, j, :], ALU.mult).then_inc(u_ready.sem, 1)
                pool.wait_ge(u_ready.sem, u_ready.at(c, j + 1))
                pool.wait_ge(u_high.sem, u_high.at(c, j + 1))
                pool.tensor_tensor(u_rows[P // 2:P, j, 0, :], u[0:P // 2, j, :],
                                   u_rows[0:P // 2, j, 0, :].bitcast(F32), ALU.subtract).then_inc(u_low.sem, 1)
                pool.wait_ge(u_low.sem, u_low.at(c, 2 * j + 1))
                pool.tensor_tensor(u_rows[0:P // 2, j, 1, :], u[P // 2:P, j, :],
                                   u_rows[P // 2:P, j, 1, :].bitcast(F32), ALU.subtract).then_inc(u_low.sem, 1)
                pool.wait_ge(u_low.sem, u_low.at(c, 2 * j + 2))

            def outproj(c, _):
                if not after_first(c):
                    pool.wait_ge(load_late.sem, 16 * len(LATE_LOADS))
                    linear = vec[:, at["b1_linear"]:at["b1_linear"] + UNITS]
                    pool.tensor_scalar(linear, linear, 1.0, None, ALU.add).then_inc(bias_raised.sem, 1)

            def advance(c, i):
                if i == 0:
                    pool.wait_ge(bc_ready.sem, bc_ready.at(c, 2))
                pool.wait_ge(scanned.sem, scanned.at(c, i + 1))
                if i >= 2:
                    pool.wait_ge(pe_y.sem, pe_y.at(c, i - 1))
                pool.tensor_tensor(read[:, i % 2, :].rearrange("p (k t) -> p k t", k=2),
                                   state[:, i % 2, :].rearrange("p (k t) -> p k t", k=2),
                                   twice(c_all[:, :]), ALU.mult).then_inc(read_out.sem, 1)

            def scale3(c, _):
                pool.wait_ge(base_ready.sem, base_ready.at(c, 1))
                pool.tensor_tensor(base[:, :, :], base[:, :, :], h0[:, :, :], ALU.add).then_inc(base_ready.sem, 1)

            def experts_mix(c, un):
                pool.wait_ge(gate_act.sem, gate_act.at(c, un + 1))
                pool.wait_ge(linear_clip.sem, linear_clip.at(c, un + 1))
                if un:
                    pool.wait_ge(hid_ready.sem, hid_ready.at(c, un))
                pool.tensor_tensor(glu, g_act, l_clip[un % 2], ALU.mult).then_inc(glu_ready.sem, 1)

            pool.memset(ones[:, :], 1.0)
            pool.memset(minus_half[:, :], -0.5)
            for k, (shift, _) in enumerate(LOG1P):
                pool.memset(shifts[:, k:k + 1], shift)
            pool.memset(a_bar[:, :, :], 0.0)
            pool.memset(mix_parts[:, :].bitcast(F32), 0.0)
            pool.memset(logits[:, :, EXPERTS:EXPERTS + 4], PAD_LOGIT)
            pool.memset(top4[:, :, TOP_K:8], PAD_LOGIT).then_inc(constants.sem, 1)
            pool.wait_ge(constants.sem, 1)
            pool.wait_ge(load_ssm.sem, 16 * len(SSM_LOADS))
            pool.tensor_scalar(w_in[:, 0, :], w_in[:, 0, :], 0.5, None, ALU.mult)
            pool.tensor_scalar(w_in_rest[:, 0, :], w_in_rest[:, 0, :], 0.5, None, ALU.mult)\
                .then_inc(in_halved.sem, 1)
            run(pool, {
                "scale": scale, "variance": lambda c, _: take_roots(c, 1), "variance2": lambda c, _: take_roots(c, 2),
                "variance3": lambda c, _: take_roots(c, 3), "split_w1": split_w1, "split": split,
                "advance": advance, "outproj": outproj, "scale3": scale3, "experts_mix": experts_mix})


def _twice(w):
    return np.concatenate([w, w[..., P:HIDDEN]], axis=-1)


def _tiles(w, n):
    return w.reshape(n, P, -1).transpose(1, 0, 2)


def _picks():
    unit = np.zeros((MIX_ROWS, UNITS, P), np.float32)
    group = np.zeros((P, 2 * 4, P), np.float32)
    state = np.zeros((2 * 32, 2, P), np.float32)
    total = np.zeros((P, 4, 32), np.float32)
    col = np.arange(P)
    for part in range(2):
        for un in range(UNITS):
            pair, k = divmod(un, 3)
            expert = 2 * pair + (k if k < 2 else col // REST)
            unit[32 * part + expert, un, col] = 0.5
        for q in range(8):
            group[64 * part + D8 * q + col // STATES, q, col] = 1
        for k in range(2):
            state[32 * part + STATES * k + col % STATES, k, col] = 1
    for q in range(4):
        total[col, q, D8 * q + col // STATES] = 1
    return unit, group, state, total


def _layout(i):
    x = i["x"].reshape(IMAGES, 3, 6, 16, 6, 16).transpose(0, 1, 2, 4, 3, 5).reshape(IMAGES * TOKENS_PER_IMAGE, PATCH_DIM)
    x = x.T.reshape(KP, P, CHUNKS, T).transpose(2, 1, 0, 3)
    a = {"patches": np.roll(x, -1, axis=0)}
    a["embed_w"] = _tiles(_twice(i["L0_tok_W"].T), KP)
    w_in = np.stack([i["L0_attn_W_in"].T, i["L0_attn_W_gate"].T], axis=1)
    a["in_w"], a["in_w_rest"] = w_in[:P], w_in[P:]
    a["xproj_w"] = _tiles(i["L0_attn_W_xproj"].T, NJ)
    a["dt_w"] = i["L0_attn_W_dt"].T
    a["out_w"] = _tiles(_twice(i["L0_attn_W_out"].T), NJ)
    w_ffn = np.stack([i["L0_attn_W_gate_ffn"].T, i["L0_attn_W_up"].T], axis=1)
    a["ffn_w"], a["ffn_w_rest"] = w_ffn[:P], w_ffn[P:]
    a["ffn_down"] = _tiles(_twice(i["L0_attn_W_down"].T), NF)
    gate = i["L0_ffn_gate_w"].T
    a["router_w"], a["router_w_rest"] = gate[:P], gate[P:]
    a["router_b"] = i["L0_ffn_gate_b"][None]
    w1, b1, w2 = i["L0_ffn_w1"], i["L0_ffn_b1"][:, None], i["L0_ffn_w2"]
    I = EXPERT_DIM

    def units(w):
        w = w.reshape(PAIRS, 2, w.shape[1], 2, I).transpose(0, 2, 3, 1, 4)
        rest = w[..., P:].reshape(*w.shape[:3], 1, P)
        return np.concatenate([w[..., :P], rest], axis=3).transpose(0, 1, 3, 2, 4)

    w1 = units(w1).reshape(PAIRS, HIDDEN, PAIR_COLS)
    a["expert_w1"] = np.stack([w1[:, :P], np.concatenate([w1[:, P:], w1[:, P:]], axis=1)], axis=2)
    b1 = units(b1).reshape(UNITS, 2, P)
    w2 = w2.reshape(PAIRS, 2, I, HIDDEN)
    w2 = np.concatenate([w2[:, :, :P], w2[:, :, P:].reshape(PAIRS, 1, P, HIDDEN)], axis=1)
    a["expert_w2"] = w2.transpose(2, 0, 1, 3).reshape(P, UNITS, HIDDEN)
    a["expert_b2"] = i["L0_ffn_b2"]
    a["vectors"] = np.concatenate(
        [_twice(i[n]).reshape(2, P) for n in ("L0_tok_b", "L0_attn_w_norm1", "L0_attn_w_ffn_norm", "L0_ffn_scale")]
        + [i["L0_attn_b_dt"].reshape(NJ, P), i["L0_attn_D_skip"].reshape(NJ, P), b1[:, 0], b1[:, 1]]).T
    a["decay_log"] = i["L0_attn_A_log"].reshape(NJ * GROUPS_PER_BLOCK, P).T
    a["unit_pick"], a["group_pick"], a["state_pick"], a["channel_sum"] = _picks()
    a["ones_mean"] = np.full((P, P), 1 / HIDDEN, np.float32)
    a["identity"] = np.eye(P, dtype=np.float32)
    return a


def kernel(**inputs):
    import concourse.bacc as _bacc
    from concourse.bass_utils import run_bass_kernel_spmd as _run

    nc = _bacc.Bacc("TRN2", target_bir_lowering=False, num_devices=1)
    arrays, args = {}, {}
    for name, a in _layout({k: np.asarray(v) for k, v in inputs.items()}).items():
        a = np.ascontiguousarray(a)
        arrays[name] = a
        args[name] = nc.dram_tensor(name, a.shape, mybir.dt.from_np(a.dtype), kind="ExternalInput").ap()
    args["out_main"] = nc.dram_tensor("out_main", (CHUNKS, P, T), F32, kind="ExternalOutput").ap()
    args["out_rest"] = nc.dram_tensor("out_rest", (CHUNKS, REST, T), F32, kind="ExternalOutput").ap()
    vit_tower(nc, **args)
    r = _run(nc, [arrays], core_ids=[0]).results[0]
    features = np.concatenate([r["out_main"], r["out_rest"]], axis=1)
    return features.transpose(0, 2, 1).reshape(IMAGES, TOKENS_PER_IMAGE, HIDDEN)
```
